# Optimizing a Trainium2 kernel written in Bass

```python
import numpy as np
import jax
import jax.numpy as jnp

def _softmax(x, axis=-1):
    return jax.nn.softmax(x, axis=axis)

def _gelu(x):
    return jax.nn.gelu(x, approximate=True)

def _silu(x):
    return jax.nn.silu(x)

def _sigmoid(x):
    return jax.nn.sigmoid(x)

def _layernorm(x, axis=-1, eps=1e-05):
    m = jnp.mean(x, axis=axis, keepdims=True)
    v = jnp.var(x, axis=axis, keepdims=True)
    return (x - m) / jnp.sqrt(v + eps)

def _scatter_add(tgt, idx, src, axis=0):
    return tgt.at[idx].add(src)

def _segment_sum(src, seg, n):
    return jax.ops.segment_sum(src, seg, n)
kernel_name = 'mk_xattn_ffn_d1_seqx_r8_ef2634'

def setup_inputs(seed: int=0):
    np.random.seed(seed)
    _w = jnp.asarray

    def _rec_inputs():
        import jax
        import jax.numpy as jnp
        _rk = jax.random.key(seed)
        x = -0.0005207 + 1.001 * jax.random.normal(jax.random.fold_in(_rk, 1), (16, 64, 128), jnp.float32)
        _lenS = 64 - jax.random.randint(jax.random.fold_in(_rk, 7), (16,), 0, max(1, 64 // 4) + 1, jnp.int32)
        _lenS2 = 64 - jax.random.randint(jax.random.fold_in(_rk, 8), (16,), 0, max(1, 64 // 4) + 1, jnp.int32)
        _ctx_1024P = jax.random.normal(jax.random.fold_in(_rk, 11), (16, 16, 128), jnp.float32)
        _ctx_1024c = jax.random.dirichlet(jax.random.fold_in(_rk, 511), 0.3 * jnp.ones((16,), jnp.float32), (16, 64))
        _ctx_1024t = jnp.einsum('bsk,bkd->bsd', _ctx_1024c, _ctx_1024P)
        _ctx_1024t = _ctx_1024t * jax.lax.rsqrt(jnp.mean(jnp.square(_ctx_1024t)) + 1e-12) * 0.953939
        ctx_1024 = -1.52775e-05 + 0.999936 * (_ctx_1024t + 0.3 * jax.random.normal(jax.random.fold_in(_rk, 611), (16, 64, 128), jnp.float32))
        _validS = jnp.arange(64)[None, :] < _lenS[:, None]
        _validS2 = jnp.arange(64)[None, :] < _lenS2[:, None]
        _causal = jnp.tril(jnp.ones((64, 64), dtype=bool))
        mask_BxS2_ik0 = jnp.where(jnp.broadcast_to(_validS2[:, :], (16, 64)), 0, 1).astype(jnp.int32)
        return (x, ctx_1024, mask_BxS2_ik0)
    x, ctx_1024, mask_BxS2_ik0 = _rec_inputs()

    def _L0_xattn_setup():
        import jax, jax.numpy as jnp
        import numpy as np
        DIM = 128
        HEADS = 16
        HEAD_DIM = DIM // HEADS
        SCALE = HEAD_DIM ** (-0.5)
        MASK_FILL = -1000000000.0

        def layer_norm(x, gamma, beta, eps=1e-05):
            mu = jnp.mean(x, axis=-1, keepdims=True)
            var = jnp.var(x, axis=-1, keepdims=True)
            return (x - mu) * jax.lax.rsqrt(var + eps) * gamma + beta
        key = jax.random.key(seed)
        ks = jax.random.split(key, 10)
        B, N1, N2, C = (8, 32, 512, DIM)
        s = C ** (-0.5)
        return {'x': jax.random.normal(ks[0], (B, N1, C), jnp.float32), 'kv': jax.random.normal(ks[1], (B, N2, C), jnp.float32), 'padding_mask': jax.random.randint(ks[2], (B, N2), 0, 2, jnp.int32), 'w_q': jax.random.normal(ks[3], (C, C), jnp.float32) * s, 'w_kv': jax.random.normal(ks[4], (C, 2 * C), jnp.float32) * s, 'w_proj': jax.random.normal(ks[5], (C, C), jnp.float32) * s, 'b_proj': jnp.zeros((C,), jnp.float32), 'g_x': jnp.ones((C,), jnp.float32), 'b_x': jnp.zeros((C,), jnp.float32), 'g_kv': jnp.ones((C,), jnp.float32), 'b_kv': jnp.zeros((C,), jnp.float32)}
    _L0_xattn_all = _L0_xattn_setup()
    _L0_xattn_in = {k: v for k, v in _L0_xattn_all.items() if k in ('w_q', 'w_kv', 'w_proj', 'b_proj', 'g_x', 'b_x', 'g_kv', 'b_kv')}
    del _L0_xattn_all

    def _L0_ffn_setup():
        import jax, jax.numpy as jnp
        import numpy as np
        D, H, P, E, K, F = (128, 16, 64, 8, 2, 512)
        B, S = (2, 256)
        NROT = 32
        BASE = 10000.0
        EPS = 1e-05

        def _ln(x, g, b):
            m = jnp.mean(x, -1, keepdims=True)
            v = jnp.mean(jnp.square(x - m), -1, keepdims=True)
            return (x - m) * jax.lax.rsqrt(v + EPS) * g + b

        def _rope(x):
            xr, xp = (x[..., :NROT], x[..., NROT:])
            half = NROT // 2
            inv = BASE ** (-jnp.arange(half, dtype=jnp.float32) / half)
            ang = jnp.arange(x.shape[2], dtype=jnp.float32)[:, None] * inv[None, :]
            cos, sin = (jnp.cos(ang), jnp.sin(ang))
            x1, x2 = (xr[..., :half], xr[..., half:])
            xr = jnp.concatenate([x1 * cos - x2 * sin, x1 * sin + x2 * cos], -1)
            return jnp.concatenate([xr, xp], -1)

        def _gate(x, Wsel):
            s = jax.nn.sigmoid(jnp.einsum('bsd,hed->bhse', x, Wsel))
            _, idx = jax.lax.top_k(s, K)
            mask = jax.nn.one_hot(idx, E, dtype=s.dtype).sum(-2)
            return s * mask

        def _moe_attn(x, Wq, Wk, Wv, Wo, Wsel_v, Wsel_o):
            q = _rope(jnp.einsum('bsd,hdp->bhsp', x, Wq))
            k = _rope(jnp.einsum('bsd,hdp->bhsp', x, Wk))
            gv = _gate(x, Wsel_v)
            v = jnp.einsum('bsd,bhse,hedp->bhsp', x, gv, Wv)
            att = jax.nn.softmax(jnp.einsum('bhsp,bhtp->bhst', q, k) / np.sqrt(P), axis=-1)
            o = jnp.einsum('bhst,bhtp->bhsp', att, v)
            go = _gate(x, Wsel_o)
            return jnp.einsum('bhsp,bhse,hepd->bsd', o, go, Wo)
        key = jax.random.key(seed)
        ks = jax.random.split(key, 10)
        f = lambda k, sh: jax.random.normal(k, sh, jnp.float32) * 0.02
        return dict(src=jax.random.normal(ks[0], (B, S, D), jnp.float32), Wq=f(ks[1], (H, D, P)), Wk=f(ks[2], (H, D, P)), Wv=f(ks[3], (H, E, D, P)), Wo=f(ks[4], (H, E, P, D)), Wsel_v=f(ks[5], (H, E, D)), Wsel_o=f(ks[6], (H, E, D)), ln1_g=jnp.ones(D, jnp.float32), ln1_b=jnp.zeros(D, jnp.float32), ln2_g=jnp.ones(D, jnp.float32), ln2_b=jnp.zeros(D, jnp.float32), W1=f(ks[7], (D, F)), b1=jnp.zeros(F, jnp.float32), W2=f(ks[8], (F, D)), b2=jnp.zeros(D, jnp.float32))
    _L0_ffn_all = _L0_ffn_setup()
    _L0_ffn_in = {k: v for k, v in _L0_ffn_all.items() if k in ('Wq', 'Wk', 'Wv', 'Wo', 'Wsel_v', 'Wsel_o', 'ln1_g', 'ln1_b', 'ln2_g', 'ln2_b', 'W1', 'b1', 'W2', 'b2')}
    del _L0_ffn_all
    return {'x': x, 'ctx_1024': ctx_1024, 'mask_BxS2_ik0': mask_BxS2_ik0, 'L0_xattn_w_q': _L0_xattn_in['w_q'], 'L0_xattn_w_kv': _L0_xattn_in['w_kv'], 'L0_xattn_w_proj': _L0_xattn_in['w_proj'], 'L0_xattn_b_proj': _L0_xattn_in['b_proj'], 'L0_xattn_g_x': _L0_xattn_in['g_x'], 'L0_xattn_b_x': _L0_xattn_in['b_x'], 'L0_xattn_g_kv': _L0_xattn_in['g_kv'], 'L0_xattn_b_kv': _L0_xattn_in['b_kv'], 'L0_ffn_Wq': _L0_ffn_in['Wq'], 'L0_ffn_Wk': _L0_ffn_in['Wk'], 'L0_ffn_Wv': _L0_ffn_in['Wv'], 'L0_ffn_Wo': _L0_ffn_in['Wo'], 'L0_ffn_Wsel_v': _L0_ffn_in['Wsel_v'], 'L0_ffn_Wsel_o': _L0_ffn_in['Wsel_o'], 'L0_ffn_ln1_g': _L0_ffn_in['ln1_g'], 'L0_ffn_ln1_b': _L0_ffn_in['ln1_b'], 'L0_ffn_ln2_g': _L0_ffn_in['ln2_g'], 'L0_ffn_ln2_b': _L0_ffn_in['ln2_b'], 'L0_ffn_W1': _L0_ffn_in['W1'], 'L0_ffn_b1': _L0_ffn_in['b1'], 'L0_ffn_W2': _L0_ffn_in['W2'], 'L0_ffn_b2': _L0_ffn_in['b2']}

def reference(x, ctx_1024, mask_BxS2_ik0, L0_xattn_w_q, L0_xattn_w_kv, L0_xattn_w_proj, L0_xattn_b_proj, L0_xattn_g_x, L0_xattn_b_x, L0_xattn_g_kv, L0_xattn_b_kv, L0_ffn_Wq, L0_ffn_Wk, L0_ffn_Wv, L0_ffn_Wo, L0_ffn_Wsel_v, L0_ffn_Wsel_o, L0_ffn_ln1_g, L0_ffn_ln1_b, L0_ffn_ln2_g, L0_ffn_ln2_b, L0_ffn_W1, L0_ffn_b1, L0_ffn_W2, L0_ffn_b2):
    import jax
    import jax.numpy as jnp

    def _L0_xattn_ref(x, kv, padding_mask, w_q, w_kv, w_proj, b_proj, g_x, b_x, g_kv, b_kv):
        import jax, jax.numpy as jnp
        import numpy as np
        DIM = 128
        HEADS = 16
        HEAD_DIM = DIM // HEADS
        SCALE = HEAD_DIM ** (-0.5)
        MASK_FILL = -1000000000.0

        def layer_norm(x, gamma, beta, eps=1e-05):
            mu = jnp.mean(x, axis=-1, keepdims=True)
            var = jnp.var(x, axis=-1, keepdims=True)
            return (x - mu) * jax.lax.rsqrt(var + eps) * gamma + beta
        B, N1, C = x.shape
        N2 = kv.shape[1]
        xn = layer_norm(x, g_x, b_x)
        kvn = layer_norm(kv, g_kv, b_kv)
        q = (xn @ w_q).reshape(B, N1, HEADS, HEAD_DIM).transpose(0, 2, 1, 3)
        kv_proj = (kvn @ w_kv).reshape(B, N2, 2, HEADS, HEAD_DIM).transpose(2, 0, 3, 1, 4)
        k, v = (kv_proj[0], kv_proj[1])
        attn = jnp.einsum('bhqd,bhkd->bhqk', q, k) * SCALE
        mask = padding_mask[:, None, None, :]
        attn = jnp.where(mask == 0, MASK_FILL, attn)
        attn = jax.nn.softmax(attn, axis=-1)
        out = jnp.einsum('bhqk,bhkd->bhqd', attn, v)
        out = out.transpose(0, 2, 1, 3).reshape(B, N1, C)
        return out @ w_proj + b_proj

    def _L0_ffn_ref(src, Wq, Wk, Wv, Wo, Wsel_v, Wsel_o, ln1_g, ln1_b, ln2_g, ln2_b, W1, b1, W2, b2):
        import jax, jax.numpy as jnp
        import numpy as np
        D, H, P, E, K, F = (128, 16, 64, 8, 2, 512)
        B, S = (2, 256)
        NROT = 32
        BASE = 10000.0
        EPS = 1e-05

        def _ln(x, g, b):
            m = jnp.mean(x, -1, keepdims=True)
            v = jnp.mean(jnp.square(x - m), -1, keepdims=True)
            return (x - m) * jax.lax.rsqrt(v + EPS) * g + b

        def _rope(x):
            xr, xp = (x[..., :NROT], x[..., NROT:])
            half = NROT // 2
            inv = BASE ** (-jnp.arange(half, dtype=jnp.float32) / half)
            ang = jnp.arange(x.shape[2], dtype=jnp.float32)[:, None] * inv[None, :]
            cos, sin = (jnp.cos(ang), jnp.sin(ang))
            x1, x2 = (xr[..., :half], xr[..., half:])
            xr = jnp.concatenate([x1 * cos - x2 * sin, x1 * sin + x2 * cos], -1)
            return jnp.concatenate([xr, xp], -1)

        def _gate(x, Wsel):
            s = jax.nn.sigmoid(jnp.einsum('bsd,hed->bhse', x, Wsel))
            _, idx = jax.lax.top_k(s, K)
            mask = jax.nn.one_hot(idx, E, dtype=s.dtype).sum(-2)
            return s * mask

        def _moe_attn(x, Wq, Wk, Wv, Wo, Wsel_v, Wsel_o):
            q = _rope(jnp.einsum('bsd,hdp->bhsp', x, Wq))
            k = _rope(jnp.einsum('bsd,hdp->bhsp', x, Wk))
            gv = _gate(x, Wsel_v)
            v = jnp.einsum('bsd,bhse,hedp->bhsp', x, gv, Wv)
            att = jax.nn.softmax(jnp.einsum('bhsp,bhtp->bhst', q, k) / np.sqrt(P), axis=-1)
            o = jnp.einsum('bhst,bhtp->bhsp', att, v)
            go = _gate(x, Wsel_o)
            return jnp.einsum('bhsp,bhse,hepd->bsd', o, go, Wo)
        src2 = _moe_attn(src, Wq, Wk, Wv, Wo, Wsel_v, Wsel_o)
        src = src + src2
        src = _ln(src, ln1_g, ln1_b)
        src2 = jax.nn.relu(src @ W1 + b1) @ W2 + b2
        src = src + src2
        return _ln(src, ln2_g, ln2_b)
    x = x + _L0_xattn_ref(_layernorm(x, axis=-1), ctx_1024, mask_BxS2_ik0, L0_xattn_w_q, L0_xattn_w_kv, L0_xattn_w_proj, L0_xattn_b_proj, L0_xattn_g_x, L0_xattn_b_x, L0_xattn_g_kv, L0_xattn_b_kv)
    x = x + _L0_ffn_ref(_layernorm(x, axis=-1), L0_ffn_Wq, L0_ffn_Wk, L0_ffn_Wv, L0_ffn_Wo, L0_ffn_Wsel_v, L0_ffn_Wsel_o, L0_ffn_ln1_g, L0_ffn_ln1_b, L0_ffn_ln2_g, L0_ffn_ln2_b, L0_ffn_W1, L0_ffn_b1, L0_ffn_W2, L0_ffn_b2)
    return x

_drawn_inputs = setup_inputs


def setup_inputs(seed=0):
    import zlib

    import numpy as np

    out = dict(_drawn_inputs(seed))
    spreads = {'L0_xattn_b_proj': (0.0, 0.1),
     'L0_xattn_g_x': (1.0, 0.2),
     'L0_xattn_b_x': (0.0, 0.295),
     'L0_xattn_g_kv': (1.0, 0.2),
     'L0_xattn_b_kv': (0.0, 0.1),
     'L0_ffn_ln1_g': (1.0, 0.2),
     'L0_ffn_ln1_b': (0.0, 0.1),
     'L0_ffn_ln2_g': (1.0, 0.2),
     'L0_ffn_ln2_b': (0.0, 0.1),
     'L0_ffn_b1': (0.0, 0.629),
     'L0_ffn_b2': (0.0, 0.1)}
    factors = {'L0_ffn_Wq': 8.0,
     'L0_ffn_Wk': 8.0,
     'L0_ffn_Wv': 3.541,
     'L0_ffn_Wo': 3.506,
     'L0_ffn_Wsel_v': 5.36,
     'L0_ffn_Wsel_o': 4.065}
    for name, (base, spread) in spreads.items():
        noise = np.random.default_rng([zlib.crc32(name.encode()), seed]).standard_normal(out[name].shape)
        drawn = base * np.exp(spread * noise) if base else spread * noise
        out[name] = jnp.asarray(drawn.astype(out[name].dtype))
    for name, factor in factors.items():
        out[name] = (out[name] * factor).astype(out[name].dtype)
    return out
```

```python
from contextlib import ExitStack

import numpy as np

import concourse.bass as bass
from concourse import mybir

F32 = mybir.dt.float32
BF16 = mybir.dt.bfloat16
I32 = mybir.dt.int32
ALU = mybir.AluOpType
ACT = mybir.ActivationFunctionType
AX_X = mybir.AxisListType.X

P = 128
BATCH, SEQ, DIM = 16, 64, 128
TILES = BATCH * SEQ // P
XH, XD = 16, 8
H, HD, E = 16, 64, 8
HP = H // 2
NROT, HALF_ROT = 32, 16
FF = 512
HALVES, HTOK = 2, 512
HT = HTOK // P
QUADS = H // 4
SPLITS = 3
EPS = 1e-5
FILL = 1e9
BIG = 1e30

C_ID, C_BM, C_COS, C_SIN, C_RANK, C_END = 0, 128, 144, 176, 208, 216


def constants():
    c = np.zeros((P, C_END), np.float32)
    c[:, C_ID:C_ID + P] = np.eye(P)
    c[:, C_BM:C_BM + XH] = np.arange(P)[:, None] // XD == np.arange(XH)[None]
    inv = 10000.0 ** (-np.arange(HALF_ROT, dtype=np.float32) / HALF_ROT)
    angle = (np.arange(P) % SEQ).astype(np.float32)[:, None] * inv[None].astype(np.float32)
    cos, sin = np.cos(angle), np.sin(angle)
    c[:, C_COS:C_COS + NROT] = np.concatenate([cos, cos], 1)
    c[:, C_SIN:C_SIN + NROT] = np.concatenate([sin, -sin], 1)
    c[:, C_RANK:C_RANK + E] = E - np.arange(E)
    row = np.arange(P)
    sel = np.zeros((P, 2, E, P), np.float32)
    for pair in range(2):
        for e in range(E):
            for half in range(2):
                rows = (row // 32 == 2 * pair + half) & (row % 32 < 8 * SPLITS) & (row % 8 == e)
                sel[rows, pair, e, half * HD:(half + 1) * HD] = 1
    return c, sel.reshape(P, 2 * E * P)


class Count:

    def __init__(self, sem, per, first=0):
        self.sem, self.per, self.first = sem, per, first

    def at(self, i, k=None):
        return i * self.per + (self.per if k is None else k) + self.first


def build(nc, x, ctx_in, mask, w_q, w_kv, w_proj, b_proj, g_x, b_x, g_kv, b_kv, Wq, Wk, Wv, Wo,
          Wsel_v, Wsel_o, ln1_g, ln1_b, ln2_g, ln2_b, W1, b1, W2, b2, const, const_sel, const_idb, out):
    st = ExitStack()
    with st:
        def sb(name, shape, dt=F32):
            return st.enter_context(nc.sbuf_tensor(name, shape, dt))

        def sem(name, per=1, first=0):
            return Count(st.enter_context(nc.semaphore(name)), per, first)

        cst = sb("cst", [P, C_END])
        ident = cst[:, C_ID:C_ID + P]
        head_block = cst[:, C_BM:C_BM + XH]
        cos_t, sin_t = cst[:, C_COS:C_COS + NROT], cst[:, C_SIN:C_SIN + NROT]
        rank_t = cst[:, C_RANK:C_RANK + E]
        sel = sb("sel", [P, 2 * E, P], BF16)
        identb = sb("identb", [P, P], BF16)
        wq_sb = sb("wq_sb", [P, DIM])
        wkv_sb = sb("wkv_sb", [P, 2 * DIM])
        wproj_sb = sb("wproj_sb", [P, DIM])
        big_w = sb("big_w", [P, H, E * HD])
        Wq_sb = sb("Wq_sb", [P, H, HD])
        Wk_sb = sb("Wk_sb", [P, H, HD])
        wsel_sb = sb("wsel_sb", [P, 2 * H * E])
        W1_sb = sb("W1_sb", [P, FF])
        W2_sb = sb("W2_sb", [P, FF // P, DIM])
        cols = sb("cols", [P, 16])
        COL = {n: cols[:, k:k + 1] for k, n in enumerate(
            ["g_x", "b_x", "g_kv", "b_kv", "ln1_g", "ln1_b", "b2"])}
        b1_sb = cols[:, 8:12]
        rows = sb("rows", [P, 3, DIM])
        powers = sb("powers", [P, 4])
        eps_t = sb("eps_t", [P, 4])

        x_all = sb("x_all", [P, TILES, DIM])
        c_all = sb("c_all", [P, TILES, DIM])
        x2_all = sb("x2_all", [P, TILES, DIM])
        src_all = sb("src_all", [P, TILES, DIM])
        keep_k = sb("keep_k", [P, TILES, P])
        fill_f = sb("fill_f", [P, TILES, SEQ])
        oT_all = sb("oT_all", [P, HP, TILES * P])
        mask_k = oT_all[:, 0, :].bitcast(I32).rearrange("p (t s) -> p t s", t=TILES)
        mask_f = oT_all[:, 1, 0:TILES * SEQ].bitcast(I32).rearrange("p (t s) -> p t s", t=TILES)
        wsel_raw = oT_all[:, 2, 0:2 * DIM].rearrange("p (a d) -> p a d", a=2)
        goT_all = sb("goT_all", [P, QUADS, TILES * P], BF16)

        x_bn = sb("x_bn", [P, 2, 6])
        x_mv = sb("x_mv", [P, 2, 2])
        x_ve = sb("x_ve", [P, 8])
        x_hat = sb("x_hat", [P, 2, DIM])
        x_nT = sb("x_nT", [P, 2, P])
        x_qT = sb("x_qT", [P, P])
        x_kT = sb("x_kT", [P, P])
        x_v = sb("x_v", [P, XH, XD + 1])
        kbd = sb("kbd", [P, 2, XH, SEQ])
        x_p = sb("x_p", [P, XH, SEQ])
        x_mx = sb("x_mx", [P, XH])
        x_att = sb("x_att", [P, XH, P])
        x_rc = sb("x_rc", [P, XH])
        x_o = sb("x_o", [P, XH, XD])
        x_oT = sb("x_oT", [P, P])
        f_bn = sb("f_bn", [P, 6])
        f_mv = sb("f_mv", [P, 2])
        f_ve = sb("f_ve", [P, 2])
        x2_s = sb("x2_s", [P, DIM])
        src_s = sb("src_s", [P, DIM])

        srcT = sb("srcT", [P, P])
        lg = sb("lg", [P, 2 * H, E])
        top = sb("top", [P, 2, 2 * H])
        top_e = sb("top_e", [P, 2, 2 * H])
        top_s = sb("top_s", [P, 2, 2 * H])
        eq = sb("eq", [P, 2 * H, E])
        oh1 = sb("oh1", [P, 2 * H, E])
        oh2 = sb("oh2", [P, 2 * H, E])
        l2 = sb("l2", [P, 2 * H, E])
        kk = sb("kk", [P, 2 * H])
        gate = sb("gate", [P, 2, H, E])
        go3 = sb("go3", [P, QUADS, 4, 4, E], BF16)
        go_r = sb("go_r", [P, H, E])
        qk = sb("qk", [P, 2 * H, HD])
        rot_c = sb("rot_c", [P, 2 * H, NROT])
        rot_s = sb("rot_s", [P, 2 * H, NROT])
        q_bd = sb("q_bd", [P, H, P])
        kT = sb("kT", [P, H, SEQ])
        p_f = sb("p_f", [P, H, SEQ])
        f_mx = sb("f_mx", [P, H])
        att = sb("att", [P, H, P])
        v = sb("v", [P, H, HD + 1])
        gy = sb("gy", [P, 4, E, HD])
        f_rc = sb("f_rc", [P, H])
        o_sb = sb("o_sb", [P, H, HD])

        ps = st.enter_context(nc.psum_tensor("ps", [P, 8, 512], F32))
        Y = [ps[:, 0, :], ps[:, 1, :]]
        A = ps[:, 2:4, :].rearrange("p a b -> p (a b)")
        T = ps[:, 4:6, :].rearrange("p a b -> p (a b)")
        X = ps[:, 6:8, :].rearrange("p a b -> p (a b)")
        X0, X1 = ps[:, 6, :], ps[:, 7, :]

        loads = {n: sem("ld_" + n) for n in
                 ["const", "sel", "x", "ctx", "mask", "vec", "xw", "qk", "wsel", "ff"]}
        ld_wv = [sem(f"ld_wv{k}") for k in range(4)]
        ld_wo = [sem(f"ld_wo{k}") for k in range(4)]
        set_dve, set_pool, set_t = sem("set_dve"), sem("set_pool"), sem("set_t")
        xs_bn, xs_mv, xs_r, xs_hat = sem("xs_bn", 2), sem("xs_mv", 2), sem("xs_r", 7), sem("xs_hat", 2)
        xs_tp, xs_n, xs_proj, xs_q = sem("xs_tp"), sem("xs_n", 2), sem("xs_proj"), sem("xs_q", 2)
        xs_k, xs_kbd, xs_s, xs_f = sem("xs_k"), sem("xs_kbd"), sem("xs_s"), sem("xs_f")
        xs_mx, xs_sub, xs_e, xs_pt = sem("xs_mx"), sem("xs_sub"), sem("xs_e"), sem("xs_pt")
        xs_att, xs_pv, xs_rc, xs_o = sem("xs_att", 4), sem("xs_pv"), sem("xs_rc"), sem("xs_o")
        xs_ot, xs_otc, xs_pj, xs_x2 = sem("xs_ot"), sem("xs_otc"), sem("xs_pj"), sem("xs_x2")
        fs_bn, fs_mv, fs_r, fs_src = sem("fs_bn"), sem("fs_mv"), sem("fs_r", 2), sem("fs_src", 2)
        f_tp, f_srcT, f_g, f_q, f_k = sem("f_tp"), sem("f_srcT"), sem("f_g"), sem("f_q"), sem("f_k")
        f_lg, f_top, f_exp, f_sig = sem("f_lg"), sem("f_top", 11), sem("f_exp"), sem("f_sig", 2)
        f_gate, f_go, f_gt, f_got = sem("f_gate", 3), sem("f_go", 4), sem("f_gt"), sem("f_got", 1, 1)
        f_qkev, f_rot, f_ra = sem("f_qkev", 2), sem("f_rot", 2), sem("f_ra", 2)
        f_qt, f_kt, f_qb, f_kb = sem("f_qt"), sem("f_kt"), sem("f_qb", 4), sem("f_kb", 4)
        f_s, f_m, f_sub, f_e = sem("f_s"), sem("f_m"), sem("f_sub"), sem("f_e")
        f_pt, f_att, f_pv, f_rcs = sem("f_pt"), sem("f_att", 4), sem("f_pv"), sem("f_rcs", 2)
        f_on, f_ot, f_otev = sem("f_on", 2), sem("f_ot"), sem("f_otev", 1, 1)
        f_y, f_vg, f_es = sem("f_y", H), sem("f_vg", H, 1), sem("f_es", 3 * H // 2)
        STEPS = HP * E
        p_res, p_bc, p_gm, p_fin = sem("p_res"), sem("p_bc", STEPS), sem("p_gm", STEPS), sem("p_fin", STEPS)
        t_acc, t_rt, t_bn, t_mv, t_r = sem("t_acc"), sem("t_rt"), sem("t_bn", HT), sem("t_mv", HT), sem("t_r", 2)
        t_z, t_zt, t_y1, t_h, t_relu = sem("t_z", HT + 1), sem("t_zt"), sem("t_y1"), sem("t_h", 4), sem("t_relu", 4)
        t_o, t_z2, t_z2t = sem("t_o"), sem("t_z2"), sem("t_z2t")
        u_bn, u_mv, u_r, u_z = sem("u_bn", HT), sem("u_mv", HT), sem("u_r", 2), sem("u_z", HT + 1)
        u_g, u_b, u_out, u_st = sem("u_g"), sem("u_b"), sem("u_out"), sem("u_st", 16)
        block = st.enter_context(nc.Block())

        x_tok = x.rearrange("(t b) s d -> (b s) t d", b=2)
        ctx_tok = ctx_in.rearrange("(t b) s d -> (b s) t d", b=2)
        out_tok = out.rearrange("(t b) s d -> (b s) t d", b=2)
        wv_cols = Wv.rearrange("h e d p -> d h e p")
        wo_view = big_w[:, :, :].rearrange("p (a b) n -> p a (b n)", b=2).rearrange("p a (e n) -> p a e n", e=E)
        wv_view = big_w[:, :, :].rearrange("p h (e n) -> p h e n", e=E)

        g_ring = [gy[:, k, :, :].rearrange("p e n -> p (e n)") for k in range(4)]
        acc = ps[:, 0, :]
        BC = [ps[:, 1, :], ps[:, 2, :], ps[:, 3, :]]
        TA = ps[:, 4, :]
        TH = [ps[:, 5, :], ps[:, 6, :]]
        TO = ps[:, 7, :]
        r1T = kbd[:, 0, :, :].rearrange("p h s -> p (h s)")[:, 0:HTOK]
        y1T = kbd[:, 0, :, :].rearrange("p h s -> p (h s)")[:, HTOK:2 * HTOK]
        hT = q_bd[:, :, :].rearrange("p h s -> p (h s)").rearrange("p (k t) -> p k t", k=4)
        z2T = kbd[:, 1, :, :].rearrange("p h s -> p (h s)")[:, 0:HTOK]
        z_t = x_p[:, 0:8, :].rearrange("p h s -> p (h s)").rearrange("p (t d) -> p t d", t=HT)
        z2_t = x_p[:, 8:16, :].rearrange("p h s -> p (h s)").rearrange("p (t d) -> p t d", t=HT)
        tail_bn = sb("tail_bn", [P, 2, HT, 6])
        tail_mv = sb("tail_mv", [P, 2, HT, 2])
        tail_ve = sb("tail_ve", [P, 2, 2, HT])

        @block.sync
        def _(sp):
            sp.dma_start(x_all[:], x_tok).then_inc(loads["x"].sem, 16)
            sp.dma_start(c_all[:], ctx_tok).then_inc(loads["ctx"].sem, 16)
            sp.dma_start(cst[:], const).then_inc(loads["const"].sem, 16)
            m_row = mask.rearrange("(o t b) s -> o t (b s)", o=1, b=2)
            sp.dma_start(mask_k, m_row.broadcast_to([P, TILES, P])).then_inc(loads["mask"].sem, 16)
            for b in range(2):
                mb = mask.rearrange("(o t b) s -> b o t s", o=1, b=2)[b]
                sp.dma_start(mask_f[64 * b:64 * b + 64], mb.broadcast_to([64, TILES, SEQ])).then_inc(
                    loads["mask"].sem, 16)
            for name, a in [("g_x", g_x), ("b_x", b_x), ("g_kv", g_kv), ("b_kv", b_kv),
                            ("ln1_g", ln1_g), ("ln1_b", ln1_b), ("b2", b2)]:
                sp.dma_start(COL[name], a.rearrange("(p o) -> p o", o=1)).then_inc(loads["vec"].sem, 16)
            for k in range(4):
                sp.dma_start(b1_sb[:, k:k + 1], b1[P * k:P * k + P].rearrange("(p o) -> p o", o=1)).then_inc(
                    loads["vec"].sem, 16)
            for k, a in enumerate([b_proj, ln2_g, ln2_b]):
                sp.dma_start(rows[:, k, :], a.rearrange("(o d) -> o d", o=1).broadcast_to([P, DIM])).then_inc(
                    loads["vec"].sem, 16)
            for dst, a in [(wq_sb, w_q), (wkv_sb, w_kv), (wproj_sb, w_proj)]:
                sp.dma_start(dst[:], a).then_inc(loads["xw"].sem, 16)
            sp.dma_start(wsel_raw[:, 0, :], Wsel_v.rearrange("h e d -> (h e) d")).then_inc(loads["wsel"].sem, 16)
            sp.dma_start(wsel_raw[:, 1, :], Wsel_o.rearrange("h e d -> (h e) d")).then_inc(loads["wsel"].sem, 16)
            sp.dma_start(Wq_sb[:], Wq.rearrange("h d p -> d h p")).then_inc(loads["qk"].sem, 16)
            sp.dma_start(Wk_sb[:], Wk.rearrange("h d p -> d h p")).then_inc(loads["qk"].sem, 16)
            for k in range(4):
                for h in range(4 * k, 4 * k + 4):
                    sp.dma_start(wv_view[:, h], wv_cols[:, h]).then_inc(ld_wv[k].sem, 16)
            sp.dma_start(sel[:], const_sel.rearrange("p (a m) -> p a m", m=P)).then_inc(loads["sel"].sem, 16)
            sp.dma_start(identb[:], const_idb).then_inc(loads["sel"].sem, 16)
            sp.dma_start(W1_sb[:], W1).then_inc(loads["ff"].sem, 16)
            sp.dma_start(W2_sb[:], W2.rearrange("(k p) n -> p k n", p=P)).then_inc(loads["ff"].sem, 16)
            for k in range(4):
                sp.wait_ge(f_y.sem, f_y.at(TILES - 1, 4 * k + 4))
                for hp in (2 * k, 2 * k + 1):
                    for b in range(2):
                        sp.dma_start(wo_view[64 * b:64 * b + 64, hp],
                                     Wo[2 * hp + b].rearrange("e p n -> p e n")).then_inc(ld_wo[k].sem, 16)
            with sp.Fori(0, HALVES) as hf:
                sp.wait_ge(u_out.sem, u_out.at(hf))
                sp.dma_start(out_tok[:, bass.ds(hf * HT, HT), :], x_all[:, bass.ds(hf * HT, HT), :]).then_inc(u_st.sem, 16)
            sp.wait_ge(u_st.sem, u_st.at(HALVES - 1))

        @block.tensor
        def _(pe):
            def x_transpose(j):
                pe.wait_ge(xs_hat.sem, xs_hat.at(j))
                pe.transpose(X0[:, 0:P], x_hat[:, 0, :], ident)
                pe.transpose(X0[:, P:2 * P], x_hat[:, 1, :], ident).then_inc(xs_tp.sem, 1)

            def x_project(j):
                pe.wait_ge(xs_n.sem, xs_n.at(j))
                pe.matmul(X1[:, 0:P], wq_sb[:], x_nT[:, 0, :], start=True, stop=True)
                pe.matmul(X1[:, P:2 * P], x_nT[:, 1, :], wkv_sb[:, DIM:], start=True, stop=True)
                pe.matmul(X0[:, 2 * P:3 * P], wkv_sb[:, 0:DIM], x_nT[:, 1, :],
                          start=True, stop=True).then_inc(xs_proj.sem, 1)

            def x_scores(j):
                pe.wait_ge(xs_q.sem, xs_q.at(j))
                pe.wait_ge(xs_kbd.sem, xs_kbd.at(j))
                for c in range(2):
                    for b in range(2):
                        mm = pe.matmul(X[64 * b:64 * b + 64, 512 * c:512 * c + 512], x_qT[:, 64 * b:64 * b + 64],
                                       kbd[:, b, 8 * c:8 * c + 8, :].rearrange("p h s -> p (h s)"),
                                       start=True, stop=True)
                mm.then_inc(xs_s.sem, 1)

            def x_ptrans(j):
                pe.wait_ge(xs_e.sem, xs_e.at(j))
                for k in range(8):
                    mm = pe.transpose(X[:, P * k:P * k + P], x_p[:, 2 * k:2 * k + 2, :].rearrange(
                        "p h s -> p (h s)"), ident)
                mm.then_inc(xs_pt.sem, 1)

            def x_values(j):
                pe.wait_ge(xs_att.sem, xs_att.at(j))
                for h in range(XH):
                    mm = pe.matmul(X0[:, (XD + 1) * h:(XD + 1) * (h + 1)], x_att[:, h, :], x_v[:, h, :],
                                   start=True, stop=True)
                mm.then_inc(xs_pv.sem, 1)

            def x_otrans(j):
                pe.wait_ge(xs_o.sem, xs_o.at(j))
                pe.transpose(X1[:, 0:P], x_o[:, :, :].rearrange("p h d -> p (h d)"), ident).then_inc(xs_ot.sem, 1)

            def x_out(j):
                pe.wait_ge(xs_otc.sem, xs_otc.at(j))
                pe.matmul(X1[:, P:2 * P], x_oT[:], wproj_sb[:], start=True, stop=True).then_inc(xs_pj.sem, 1)

            def f_start(i, peeled):
                pe.wait_ge(fs_src.sem, fs_src.at(i))
                pe.wait_ge(f_got.sem, f_got.at(i, 0))
                pe.transpose(Y[0][:, 0:P], src_s[:], ident).then_inc(f_tp.sem, 1)
                pe.wait_ge(f_srcT.sem, f_srcT.at(i))
                pe.wait_ge(f_vg.sem, f_vg.at(i, 0))
                pe.matmul(Y[1][:, 0:2 * P], srcT[:], wsel_sb[:], start=True, stop=True).then_inc(f_g.sem, 1)
                pe.wait_ge(f_otev.sem, f_otev.at(i, 0))
                for w, dst, done in ((Wq_sb, T, f_q), (Wk_sb, A, f_k)):
                    for c in range(2):
                        mm = pe.matmul(dst[:, 512 * c:512 * c + 512], srcT[:],
                                       w[:, 8 * c:8 * c + 8, :].rearrange("p h s -> p (h s)"),
                                       start=True, stop=True)
                    mm.then_inc(done.sem, 1)

            def f_value(i, h):
                if h == 1:
                    pe.wait_ge(f_lg.sem, f_lg.at(i))
                if h >= 2:
                    pe.wait_ge(f_vg.sem, f_vg.at(i, h - 1))
                pe.matmul(Y[h % 2], srcT[:], big_w[:, h, :], start=True, stop=True).then_inc(f_y.sem, 1)

            def f_qktrans(i):
                pe.wait_ge(f_ra.sem, f_ra.at(i))
                for half, dst, done in ((0, T, f_qt), (1, A, f_kt)):
                    for k in range(8):
                        mm = pe.transpose(dst[:, P * k:P * k + P],
                                          qk[:, H * half + 2 * k:H * half + 2 * k + 2, :].rearrange(
                                              "p h s -> p (h s)"), ident)
                    mm.then_inc(done.sem, 1)

            def f_scores(i):
                pe.wait_ge(f_qb.sem, f_qb.at(i))
                pe.wait_ge(f_kb.sem, f_kb.at(i))
                for h in range(H):
                    mm = pe.matmul(A[:, SEQ * h:SEQ * h + SEQ], q_bd[:, h, :], kT[:, h, :], start=True, stop=True)
                mm.then_inc(f_s.sem, 1)

            def f_ptrans(i):
                pe.wait_ge(f_e.sem, f_e.at(i))
                for k in range(8):
                    mm = pe.transpose(T[:, P * k:P * k + P], p_f[:, 2 * k:2 * k + 2, :].rearrange(
                        "p h s -> p (h s)"), ident)
                mm.then_inc(f_pt.sem, 1)

            def f_gtrans(i):
                pe.wait_ge(f_go.sem, f_go.at(i))
                pe.wait_ge(f_vg.sem, f_vg.at(i, 15))
                y0 = Y[0].bitcast(BF16)
                for q in range(QUADS):
                    mm = pe.transpose(y0[:, P * q:P * q + P],
                                      go3[:, q].rearrange("p h s e -> p (h s e)"), identb[:])
                mm.then_inc(f_gt.sem, 1)

            def f_values(i):
                pe.wait_ge(f_att.sem, f_att.at(i))
                pe.wait_ge(f_es.sem, f_es.at(i))
                for h in range(H):
                    mm = pe.matmul(ps[:, 2 + h // 7, (HD + 1) * (h % 7):(HD + 1) * (h % 7 + 1)],
                                   att[:, h, :], v[:, h, :], start=True, stop=True)
                mm.then_inc(f_pv.sem, 1)

            def f_otrans(i):
                pe.wait_ge(f_on.sem, f_on.at(i))
                for k in range(HP):
                    mm = pe.transpose(T[:, P * k:P * k + P],
                                      o_sb[:, 2 * k:2 * k + 2, :].rearrange("p h s -> p (h s)"), ident)
                mm.then_inc(f_ot.sem, 1)

            def tile(i, j, peeled=False):
                f_start(i, peeled)
                after = {3: [f_qktrans], 7: [f_scores], 11: [f_ptrans], 15: [f_gtrans]}
                xs = {0: [x_transpose], 1: [x_project], 5: [x_scores], 9: [x_ptrans], 12: [x_values],
                      14: [x_otrans], 15: [x_out]}
                for h in range(H):
                    f_value(i, h)
                    if h in after:
                        for f in after[h]:
                            f(i)
                    if j is not None:
                        for f in xs.get(h, ()):
                            f(j)
                f_values(i)
                f_otrans(i)

            pe.wait_ge(loads["const"].sem, 16)
            pe.wait_ge(loads["wsel"].sem, 32)
            pe.transpose(Y[0][:, 0:P], wsel_raw[:, 0, :], ident)
            pe.transpose(Y[0][:, P:2 * P], wsel_raw[:, 1, :], ident).then_inc(set_t.sem, 1)
            pe.wait_ge(loads["xw"].sem, 48)
            for f in (x_transpose, x_project, x_scores, x_ptrans, x_values, x_otrans, x_out):
                f(0)
            pe.wait_ge(f_got.sem, 1)
            pe.wait_ge(loads["qk"].sem, 32)
            for k in range(4):
                pe.wait_ge(ld_wv[k].sem, 64)
            pe.wait_ge(loads["sel"].sem, 32)
            with pe.Fori(0, TILES - 1) as i:
                tile(i, i + 1)
            tile(TILES - 1, None, True)

            pe.wait_ge(loads["ff"].sem, 32)
            with pe.Fori(0, HALVES) as hf:
                pe.wait_ge(f_otev.sem, f_otev.at(TILES - 1))
                pe.wait_ge(f_got.sem, f_got.at(TILES - 1))
                pe.wait_ge(p_res.sem, p_res.at(hf))
                for t in range(HT):
                    pe.matmul(acc[:, P * t:P * t + P], z2_t[:, t, :], ident, start=(t == 0), stop=False,
                              skip_group_check=True)

                def spread(s):
                    if s >= 3:
                        pe.wait_ge(p_gm.sem, p_gm.at(hf, s - 2))
                    pe.matmul(BC[s % 3], sel[:, s % 16, :], goT_all[:, s // 16, bass.ds(hf * HTOK, HTOK)],
                              start=True, stop=True).then_inc(p_bc.sem, 1)

                spread(0)
                spread(1)
                for s in range(STEPS):
                    if s + 2 < STEPS:
                        spread(s + 2)
                    if s % 16 == 0:
                        pe.wait_ge(ld_wo[s // 16].sem, 64)
                    pe.wait_ge(p_gm.sem, p_gm.at(hf, s + 1))
                    mm = pe.matmul(acc, wo_view[:, s // E, s % E, :], g_ring[s % 4], start=False,
                                   stop=(s == STEPS - 1), skip_group_check=True)
                    mm.then_inc(p_fin.sem, 1)

                pe.wait_ge(t_acc.sem, t_acc.at(hf))
                for t in range(HT):
                    mm = pe.transpose(TA[:, P * t:P * t + P], r1T[:, P * t:P * t + P], ident)
                mm.then_inc(t_rt.sem, 1)
                pe.wait_ge(t_z.sem, t_z.at(hf))
                for t in range(HT):
                    mm = pe.transpose(TA[:, P * t:P * t + P], z_t[:, t, :], ident)
                mm.then_inc(t_zt.sem, 1)
                pe.wait_ge(t_y1.sem, t_y1.at(hf))
                for k in range(4):
                    if k >= 2:
                        pe.wait_ge(t_relu.sem, t_relu.at(hf, k - 1))
                    pe.matmul(TH[k % 2], W1_sb[:, P * k:P * k + P], y1T, start=True, stop=True).then_inc(t_h.sem, 1)
                for k in range(4):
                    pe.wait_ge(t_relu.sem, t_relu.at(hf, k + 1))
                    mm = pe.matmul(TO, W2_sb[:, k, :], hT[:, k, :], start=(k == 0), stop=(k == 3))
                mm.then_inc(t_o.sem, 1)
                pe.wait_ge(t_z2.sem, t_z2.at(hf))
                for t in range(HT):
                    mm = pe.transpose(TA[:, P * t:P * t + P], z2T[:, P * t:P * t + P], ident)
                mm.then_inc(t_z2t.sem, 1)

        @block.scalar
        def _(act):
            def move_blocks(src, dst, done):
                for par in range(2):
                    for b in range(2):
                        s = src[64 * par:64 * par + 64, :].rearrange("p (k c) -> p k c", k=8)
                        act.activation(dst(b, par), s[:, :, 64 * b:64 * b + 64], ACT.Copy).then_inc(done.sem, 1)

            def diag(t):
                return lambda b, par: t[64 * b:64 * b + 64, :, :].rearrange(
                    "p (k a) s -> p k a s", a=2)[:, :, par, 64 * b:64 * b + 64]

            def plain(t):
                return lambda b, par: t[64 * b:64 * b + 64, :, :].rearrange("p (k a) s -> p k a s", a=2)[:, :, par, :]

            def x_norm(j):
                act.wait_ge(xs_tp.sem, xs_tp.at(j))
                act.activation(x_nT[:, 0, :], X0[:, 0:P], ACT.Identity, bias=COL["b_x"],
                               scale=COL["g_x"]).then_inc(xs_n.sem, 1)
                act.activation(x_nT[:, 1, :], X0[:, P:2 * P], ACT.Identity, bias=COL["b_kv"],
                               scale=COL["g_kv"]).then_inc(xs_n.sem, 1)

            def x_qv(j):
                act.wait_ge(xs_proj.sem, xs_proj.at(j))
                act.activation(x_qT[:], X1[:, 0:P], ACT.Copy, scale=float(XD) ** -0.5).then_inc(xs_q.sem, 1)
                act.activation(x_v[:, :, 0:XD], X1[:, P:2 * P].rearrange("p (h d) -> p h d", d=XD),
                               ACT.Copy).then_inc(xs_q.sem, 1)

            def x_exp(j):
                act.wait_ge(xs_sub.sem, xs_sub.at(j))
                act.activation(x_p[:], x_p[:], ACT.Exp).then_inc(xs_e.sem, 1)

            def x_att_copy(j):
                act.wait_ge(xs_pt.sem, xs_pt.at(j))
                move_blocks(X, diag(x_att), xs_att)

            def x_ot_copy(j):
                act.wait_ge(xs_ot.sem, xs_ot.at(j))
                act.activation(x_oT[:], X1[:, 0:P], ACT.Copy).then_inc(xs_otc.sem, 1)

            def f_start(i):
                act.wait_ge(f_tp.sem, f_tp.at(i))
                act.activation(srcT[:], Y[0][:, 0:P], ACT.Copy).then_inc(f_srcT.sem, 1)
                act.wait_ge(f_g.sem, f_g.at(i))
                act.activation(lg[:, :, :].rearrange("p h e -> p (h e)"), Y[1][:, 0:2 * P],
                               ACT.Copy).then_inc(f_lg.sem, 1)
                for half, src, ready in ((0, T, f_q), (1, A, f_k)):
                    act.wait_ge(ready.sem, ready.at(i))
                    act.activation(qk[:, H * half:H * half + H, :].rearrange("p h s -> p (h s)"), src,
                                   ACT.Copy).then_inc(f_qkev.sem, 1)

            def f_sigmoid(i):
                act.wait_ge(f_top.sem, f_top.at(i, 7))
                act.activation(top_e[:], top[:], ACT.Exp, scale=-1.0).then_inc(f_exp.sem, 1)

            def f_qk_copy(i):
                act.wait_ge(f_qt.sem, f_qt.at(i))
                move_blocks(T, diag(q_bd), f_qb)
                act.wait_ge(f_kt.sem, f_kt.at(i))
                move_blocks(A, plain(kT), f_kb)

            def f_exps(i):
                act.wait_ge(f_sub.sem, f_sub.at(i))
                act.activation(p_f[:], p_f[:], ACT.Exp, scale=float(HD) ** -0.5).then_inc(f_e.sem, 1)

            def f_att_copy(i):
                act.wait_ge(f_pt.sem, f_pt.at(i))
                move_blocks(T, diag(att), f_att)

            def f_gt_copy(i):
                act.wait_ge(f_gt.sem, f_gt.at(i))
                act.activation(goT_all[:, :, bass.ds(i * P, P)],
                               Y[0].bitcast(BF16)[:, 0:QUADS * P].rearrange("p (q t) -> p q t", q=QUADS),
                               ACT.Copy).then_inc(f_got.sem, 1)

            def f_ot_copy(i):
                act.wait_ge(f_ot.sem, f_ot.at(i))
                act.activation(oT_all[:, :, bass.ds(i * P, P)], T.rearrange("p (h t) -> p h t", h=HP),
                               ACT.Copy).then_inc(f_otev.sem, 1)

            def tile(i, j):
                f_start(i)
                f_sigmoid(i)
                if j is not None:
                    x_norm(j)
                if j is not None:
                    x_qv(j)
                f_qk_copy(i)
                if j is not None:
                    x_exp(j)
                f_exps(i)
                if j is not None:
                    x_att_copy(j)
                f_att_copy(i)
                if j is not None:
                    x_ot_copy(j)
                f_gt_copy(i)
                f_ot_copy(i)

            act.wait_ge(set_t.sem, 1)
            act.activation(wsel_sb[:], Y[0][:, 0:2 * P], ACT.Copy).then_inc(f_got.sem, 1)
            act.sem_inc(f_otev.sem, 1)
            act.wait_ge(loads["vec"].sem, 16 * 14)
            act.wait_ge(set_pool.sem, 1)
            for f in (x_norm, x_qv, x_exp, x_att_copy, x_ot_copy):
                f(0)
            with act.Fori(0, TILES - 1) as i:
                tile(i, i + 1)
            tile(TILES - 1, None)

            with act.Fori(0, HALVES) as hf:
                act.wait_ge(p_fin.sem, p_fin.at(hf))
                act.activation(r1T, acc, ACT.Copy).then_inc(t_acc.sem, 1)
                act.wait_ge(t_zt.sem, t_zt.at(hf))
                act.activation(y1T, TA, ACT.Identity, bias=COL["ln1_b"], scale=COL["ln1_g"]).then_inc(t_y1.sem, 1)
                for k in range(4):
                    act.wait_ge(t_h.sem, t_h.at(hf, k + 1))
                    act.activation(hT[:, k, :], TH[k % 2], ACT.Relu, bias=b1_sb[:, k:k + 1]).then_inc(t_relu.sem, 1)

        @block.vector
        def _(dve):
            def x_stats(j):
                dve.bn_stats(x_bn[:, 0, :], x_all[:, j, :]).then_inc(xs_bn.sem, 1)
                dve.bn_stats(x_bn[:, 1, :], c_all[:, j, :]).then_inc(xs_bn.sem, 1)

            def x_aggregate(j):
                for k in range(2):
                    dve.bn_aggr(x_mv[:, k, :], x_bn[:, k, :]).then_inc(xs_mv.sem, 1)

            def x_center(j):
                dve.wait_ge(xs_r.sem, xs_r.at(j))
                dve.tensor_scalar(x_hat[:, 0, :], x_all[:, j, :], x_mv[:, 0, 0:1], x_ve[:, 6:7],
                                  ALU.subtract, ALU.mult).then_inc(xs_hat.sem, 1)
                dve.tensor_scalar(x_hat[:, 1, :], c_all[:, j, :], x_mv[:, 1, 0:1], x_ve[:, 3:4],
                                  ALU.subtract, ALU.mult).then_inc(xs_hat.sem, 1)

            def x_keys(j):
                dve.wait_ge(xs_proj.sem, xs_proj.at(j))
                dve.tensor_tensor(x_kT[:], X0[:, 2 * P:3 * P], keep_k[:, j, :], ALU.mult).then_inc(xs_k.sem, 1)
                dve.wait_ge(xs_k.sem, xs_k.at(j))
                dve.tensor_tensor(kbd[:],
                                  x_kT[:].rearrange("p (b o s) -> p b o s", b=2, o=1).broadcast_to([P, 2, XH, SEQ]),
                                  head_block.rearrange("p (o h q) -> p o h q", o=1, q=1).broadcast_to([P, 2, XH, SEQ]),
                                  ALU.mult).then_inc(xs_kbd.sem, 1)

            def x_soft(j):
                dve.wait_ge(xs_s.sem, xs_s.at(j))
                dve.tensor_tensor(x_p[:], X.rearrange("p (h s) -> p h s", h=XH),
                                  fill_f[:, j, :].unsqueeze(1).broadcast_to([P, XH, SEQ]), ALU.add).then_inc(xs_f.sem, 1)
                dve.wait_ge(xs_f.sem, xs_f.at(j))
                dve.tensor_reduce(x_mx[:], x_p[:], AX_X, ALU.max).then_inc(xs_mx.sem, 1)
                dve.wait_ge(xs_mx.sem, xs_mx.at(j))
                dve.tensor_tensor(x_p[:], x_p[:], x_mx[:].unsqueeze(2).broadcast_to([P, XH, SEQ]),
                                  ALU.subtract).then_inc(xs_sub.sem, 1)

            def x_divide(j):
                dve.wait_ge(xs_pv.sem, xs_pv.at(j))
                o = X0[:, 0:XH * (XD + 1)].rearrange("p (h d) -> p h d", h=XH)
                dve.reciprocal(x_rc[:], o[:, :, XD]).then_inc(xs_rc.sem, 1)
                dve.wait_ge(xs_rc.sem, xs_rc.at(j))
                dve.tensor_tensor(x_o[:], o[:, :, 0:XD], x_rc[:].unsqueeze(2).broadcast_to([P, XH, XD]),
                                  ALU.mult).then_inc(xs_o.sem, 1)

            def x_end(j):
                dve.wait_ge(xs_pj.sem, xs_pj.at(j))
                dve.tensor_tensor(x2_s[:], X1[:, P:2 * P], x2_all[:, j, :], ALU.add).then_inc(xs_x2.sem, 1)
                dve.wait_ge(xs_x2.sem, xs_x2.at(j))
                dve.bn_stats(f_bn[:], x2_s[:]).then_inc(fs_bn.sem, 1)
                dve.wait_ge(fs_bn.sem, fs_bn.at(j))
                dve.tensor_scalar(x2_all[:, j, :], x2_s[:], 1.0, None, ALU.mult)
                dve.bn_aggr(f_mv[:], f_bn[:]).then_inc(fs_mv.sem, 1)

            def x_src(j):
                dve.wait_ge(fs_r.sem, fs_r.at(j))
                if not (isinstance(j, int) and j == 0):
                    dve.wait_ge(f_tp.sem, f_tp.at(j, 0))
                dve.tensor_scalar(src_s[:], x2_s[:], f_mv[:, 0:1], f_ve[:, 1:2],
                                  ALU.subtract, ALU.mult).then_inc(fs_src.sem, 1)
                dve.tensor_scalar(src_all[:, j, :], x2_s[:], f_mv[:, 0:1], f_ve[:, 1:2],
                                  ALU.subtract, ALU.mult).then_inc(fs_src.sem, 1)

            def wide(t):
                return t.unsqueeze(2).broadcast_to([P, 2 * H, E])

            def f_top2(i, j):
                rank = rank_t.unsqueeze(1).broadcast_to([P, 2 * H, E])

                def step(n, ins):
                    ins.then_inc(f_top.sem, 1)
                    dve.wait_ge(f_top.sem, f_top.at(i, n))

                if j is not None:
                    dve.wait_ge(xs_bn.sem, xs_bn.at(j))
                dve.wait_ge(f_lg.sem, f_lg.at(i))
                dve.tensor_reduce(top[:, 0, :], lg[:], AX_X, ALU.max).then_inc(f_top.sem, 1)
                if j is not None:
                    x_aggregate(j)
                dve.wait_ge(f_top.sem, f_top.at(i, 1))
                step(2, dve.tensor_tensor(eq[:], lg[:], wide(top[:, 0, :]), ALU.is_equal))
                step(3, dve.tensor_tensor(eq[:], eq[:], rank, ALU.mult))
                step(4, dve.tensor_reduce(kk[:], eq[:], AX_X, ALU.max))
                step(5, dve.tensor_tensor(oh1[:], eq[:], wide(kk[:]), ALU.is_equal))
                step(6, dve.scalar_tensor_tensor(out=l2[:], in0=oh1[:], scalar=-BIG, in1=lg[:],
                                                 op0=ALU.mult, op1=ALU.add))
                step(7, dve.tensor_reduce(top[:, 1, :], l2[:], AX_X, ALU.max))
                step(8, dve.tensor_tensor(eq[:], l2[:], wide(top[:, 1, :]), ALU.is_equal))
                step(9, dve.tensor_tensor(eq[:], eq[:], rank, ALU.mult))
                step(10, dve.tensor_reduce(kk[:], eq[:], AX_X, ALU.max))
                step(11, dve.tensor_tensor(oh2[:], eq[:], wide(kk[:]), ALU.is_equal))

            def f_sigmoid(i):
                dve.wait_ge(f_exp.sem, f_exp.at(i))
                dve.tensor_scalar(top_e[:], top_e[:], 1.0, None, ALU.add).then_inc(f_sig.sem, 1)
                dve.wait_ge(f_sig.sem, f_sig.at(i, 1))
                dve.reciprocal(top_s[:], top_e[:]).then_inc(f_sig.sem, 1)

            def f_rope(i):
                dve.wait_ge(f_qkev.sem, f_qkev.at(i))
                dve.tensor_tensor(rot_c[:], qk[:, :, 0:NROT], cos_t.unsqueeze(1).broadcast_to([P, 2 * H, NROT]),
                                  ALU.mult).then_inc(f_rot.sem, 1)
                dve.tensor_tensor(rot_s[:], qk[:, :, 0:NROT], sin_t.unsqueeze(1).broadcast_to([P, 2 * H, NROT]),
                                  ALU.mult).then_inc(f_rot.sem, 1)

            def f_split(i):
                go = gate[:, 1].rearrange("p (q h) e -> p q h e", q=QUADS)
                r = go_r[:].rearrange("p (q h) e -> p q h e", q=QUADS)
                part = [go3[:, :, :, s, :] for s in range(3)]
                dve.wait_ge(f_gate.sem, f_gate.at(i))
                dve.tensor_copy(part[0], go).then_inc(f_go.sem, 1)
                dve.wait_ge(f_go.sem, f_go.at(i, 1))
                dve.tensor_tensor(r, go, part[0], ALU.subtract).then_inc(f_go.sem, 1)
                dve.wait_ge(f_go.sem, f_go.at(i, 2))
                dve.tensor_copy(part[1], r).then_inc(f_go.sem, 1)
                dve.wait_ge(f_go.sem, f_go.at(i, 3))
                dve.tensor_tensor(part[2], r, part[1], ALU.subtract).then_inc(f_go.sem, 1)

            def f_gate_value(i, h):
                if h == 0:
                    dve.wait_ge(f_gate.sem, f_gate.at(i))
                dve.wait_ge(f_y.sem, f_y.at(i, h + 1))
                if h >= 4 and h % 2 == 0:
                    dve.wait_ge(f_es.sem, f_es.at(i, 3 * (h // 2 - 1)))
                dve.tensor_tensor(gy[:, h % 4], Y[h % 2].rearrange("p (e n) -> p e n", e=E),
                                  gate[:, 0, h, :].unsqueeze(2).broadcast_to([P, E, HD]), ALU.mult).then_inc(f_vg.sem, 1)

            def f_soft(i):
                dve.wait_ge(f_s.sem, f_s.at(i))
                s = A.rearrange("p (h s) -> p h s", h=H)
                dve.tensor_reduce(f_mx[:], s, AX_X, ALU.max).then_inc(f_m.sem, 1)
                dve.wait_ge(f_m.sem, f_m.at(i))
                dve.tensor_tensor(p_f[:], s, f_mx[:].unsqueeze(2).broadcast_to([P, H, SEQ]),
                                  ALU.subtract).then_inc(f_sub.sem, 1)

            def f_divide(i):
                dve.wait_ge(f_pv.sem, f_pv.at(i))
                wide_o = ps[:, 2:4, 0:7 * (HD + 1)].rearrange("p a (h d) -> p a h d", h=7)
                last_o = ps[:, 4, 0:2 * (HD + 1)].rearrange("p (h d) -> p h d", h=2)
                dve.reciprocal(f_rc[:, 0:14].rearrange("p (a h) -> p a h", a=2), wide_o[:, :, :, HD]).then_inc(f_rcs.sem, 1)
                dve.reciprocal(f_rc[:, 14:16], last_o[:, :, HD]).then_inc(f_rcs.sem, 1)
                dve.wait_ge(f_rcs.sem, f_rcs.at(i))
                dve.tensor_tensor(o_sb[:, 0:14, :].rearrange("p (a h) d -> p a h d", a=2), wide_o[:, :, :, 0:HD],
                                  f_rc[:, 0:14].rearrange("p (a h q) -> p a h q", a=2, q=1).broadcast_to([P, 2, 7, HD]),
                                  ALU.mult).then_inc(f_on.sem, 1)
                dve.tensor_tensor(o_sb[:, 14:16, :], last_o[:, :, 0:HD],
                                  f_rc[:, 14:16].unsqueeze(2).broadcast_to([P, 2, HD]), ALU.mult).then_inc(f_on.sem, 1)

            def tile(i, j):
                if j is not None:
                    x_stats(j)
                f_top2(i, j)
                if j is not None:
                    x_center(j)
                f_sigmoid(i)
                f_rope(i)
                xs = {1: [x_keys], 5: [x_soft], 12: [x_divide], 15: [x_end]}
                fs = {2: [f_split], 8: [f_soft]}
                for h in range(H):
                    f_gate_value(i, h)
                    if j is not None:
                        for f in xs.get(h, ()):
                            f(j)
                    for f in fs.get(h, ()):
                        f(i)
                if j is not None:
                    x_src(j)
                f_divide(i)

            dve.sem_inc(f_vg.sem, 1)
            dve.wait_ge(loads["mask"].sem, 48)
            dve.tensor_scalar(keep_k[:], mask_k, 0.0, None, ALU.not_equal).then_inc(set_dve.sem, 1)
            dve.tensor_scalar(fill_f[:], mask_f, 0.0, None, ALU.not_equal).then_inc(set_dve.sem, 1)
            dve.wait_ge(set_dve.sem, 2)
            dve.tensor_scalar(fill_f[:], fill_f[:], -1.0, FILL, ALU.add, ALU.mult).then_inc(set_dve.sem, 1)
            dve.wait_ge(loads["x"].sem, 16)
            dve.wait_ge(loads["ctx"].sem, 16)
            dve.wait_ge(loads["vec"].sem, 16 * 14)
            dve.tensor_tensor(x2_all[:], x_all[:], rows[:, 0, :].unsqueeze(1).broadcast_to([P, TILES, DIM]),
                              ALU.add).then_inc(set_dve.sem, 1)
            dve.wait_ge(loads["const"].sem, 16)
            dve.wait_ge(set_dve.sem, 4)
            dve.wait_ge(set_pool.sem, 1)
            x_stats(0)
            dve.wait_ge(xs_bn.sem, 2)
            x_aggregate(0)
            for f in (x_center, x_keys, x_soft, x_divide, x_end, x_src):
                f(0)
            with dve.Fori(0, TILES - 1) as i:
                tile(i, i + 1)
            tile(TILES - 1, None)

            def normalise(hf, src, z, k, bn, mv, r, done):
                for t in range(HT):
                    dve.bn_stats(tail_bn[:, k, t, :], src[:, P * t:P * t + P]).then_inc(bn.sem, 1)
                dve.wait_ge(bn.sem, bn.at(hf))
                dve.tensor_copy(z, src.rearrange("p (t d) -> p t d", t=HT)).then_inc(done.sem, 1)
                for t in range(HT):
                    dve.bn_aggr(tail_mv[:, k, t, :], tail_bn[:, k, t, :]).then_inc(mv.sem, 1)
                dve.wait_ge(done.sem, done.at(hf, 1))
                dve.wait_ge(r.sem, r.at(hf))
                for t in range(HT):
                    dve.tensor_scalar(z[:, t, :], z[:, t, :], tail_mv[:, k, t, 0:1],
                                      tail_ve[:, k, 1, t:t + 1], ALU.subtract, ALU.mult).then_inc(done.sem, 1)

            with dve.Fori(0, HALVES) as hf:
                dve.tensor_copy(z2_t, src_all[:, bass.ds(hf * HT, HT), :]).then_inc(p_res.sem, 1)
                for s in range(STEPS):
                    dve.wait_ge(p_bc.sem, p_bc.at(hf, s + 1))
                    if s >= 4:
                        dve.wait_ge(p_fin.sem, p_fin.at(hf, s - 3))
                    dve.tensor_tensor(g_ring[s % 4], BC[s % 3], oT_all[:, s // E, bass.ds(hf * HTOK, HTOK)],
                                      ALU.mult).then_inc(p_gm.sem, 1)
                dve.wait_ge(t_rt.sem, t_rt.at(hf))
                normalise(hf, TA, z_t, 0, t_bn, t_mv, t_r, t_z)
                dve.wait_ge(t_o.sem, t_o.at(hf))
                dve.scalar_tensor_tensor(out=z2T, in0=TO, scalar=COL["b2"], in1=y1T, op0=ALU.add,
                                         op1=ALU.add).then_inc(t_z2.sem, 1)
                dve.wait_ge(t_z2t.sem, t_z2t.at(hf))
                normalise(hf, TA, z_t, 1, u_bn, u_mv, u_r, u_z)
                dve.wait_ge(u_z.sem, u_z.at(hf))
                dve.tensor_tensor(z_t, z_t, rows[:, 1, :].unsqueeze(1).broadcast_to([P, HT, DIM]),
                                  ALU.mult).then_inc(u_g.sem, 1)
                dve.wait_ge(u_g.sem, u_g.at(hf))
                dve.tensor_tensor(z_t, z_t, rows[:, 2, :].unsqueeze(1).broadcast_to([P, HT, DIM]),
                                  ALU.add).then_inc(u_b.sem, 1)
                dve.wait_ge(u_b.sem, u_b.at(hf))
                dve.tensor_tensor(x_all[:, bass.ds(hf * HT, HT), :], z_t, x2_all[:, bass.ds(hf * HT, HT), :], ALU.add).then_inc(u_out.sem, 1)

        @block.gpsimd
        def _(pool):
            def x_rstd(j):
                def step(n, ins):
                    ins.then_inc(xs_r.sem, 1)
                    if n < 7:
                        pool.wait_ge(xs_r.sem, xs_r.at(j, n))

                pool.wait_ge(xs_mv.sem, xs_mv.at(j))
                step(1, pool.tensor_tensor(x_ve[:, 0:2], x_mv[:, :, 1], eps_t[:, 0:2], ALU.add))
                step(2, pool.tensor_tensor(x_ve[:, 2:4], x_ve[:, 0:2], powers[:, 0:2], ALU.pow))
                step(3, pool.tensor_tensor(x_ve[:, 4:5], x_mv[:, 0, 1:2], x_ve[:, 2:3], ALU.mult))
                step(4, pool.tensor_tensor(x_ve[:, 4:5], x_ve[:, 4:5], x_ve[:, 2:3], ALU.mult))
                step(5, pool.tensor_tensor(x_ve[:, 4:5], x_ve[:, 4:5], eps_t[:, 0:1], ALU.add))
                step(6, pool.tensor_tensor(x_ve[:, 5:6], x_ve[:, 4:5], powers[:, 0:1], ALU.pow))
                step(7, pool.tensor_tensor(x_ve[:, 6:7], x_ve[:, 5:6], x_ve[:, 2:3], ALU.mult))

            def f_rstd(j):
                pool.wait_ge(fs_mv.sem, fs_mv.at(j))
                pool.tensor_tensor(f_ve[:, 0:1], f_mv[:, 1:2], eps_t[:, 0:1], ALU.add).then_inc(fs_r.sem, 1)
                pool.wait_ge(fs_r.sem, fs_r.at(j, 1))
                pool.tensor_tensor(f_ve[:, 1:2], f_ve[:, 0:1], powers[:, 0:1], ALU.pow).then_inc(fs_r.sem, 1)

            def f_gates(i):
                def s12(k):
                    return top_s[:, k, :].unsqueeze(2).broadcast_to([P, 2 * H, E])

                g = gate[:].rearrange("p a h e -> p (a h) e")
                pool.wait_ge(f_sig.sem, f_sig.at(i))
                pool.wait_ge(f_top.sem, f_top.at(i))
                pool.tensor_tensor(oh1[:], oh1[:], s12(0), ALU.mult).then_inc(f_gate.sem, 1)
                pool.tensor_tensor(oh2[:], oh2[:], s12(1), ALU.mult).then_inc(f_gate.sem, 1)
                pool.wait_ge(f_gate.sem, f_gate.at(i, 2))
                pool.tensor_tensor(g, oh1[:], oh2[:], ALU.add).then_inc(f_gate.sem, 1)

            def f_rot_add(i):
                h = HALF_ROT
                pool.wait_ge(f_rot.sem, f_rot.at(i))
                pool.tensor_tensor(qk[:, :, 0:h], rot_c[:, :, 0:h], rot_s[:, :, h:2 * h], ALU.add).then_inc(f_ra.sem, 1)
                pool.tensor_tensor(qk[:, :, h:2 * h], rot_c[:, :, h:2 * h], rot_s[:, :, 0:h],
                                   ALU.add).then_inc(f_ra.sem, 1)

            def f_expert_sum(i, pair):
                g = gy[:, 2 * (pair % 2):2 * (pair % 2) + 2]
                pool.wait_ge(f_vg.sem, f_vg.at(i, 2 * pair + 2))
                pool.tensor_tensor(g[:, :, 0:4, :], g[:, :, 0:4, :], g[:, :, 4:8, :], ALU.add).then_inc(f_es.sem, 1)
                pool.wait_ge(f_es.sem, f_es.at(i, 3 * pair + 1))
                pool.tensor_tensor(g[:, :, 0:2, :], g[:, :, 0:2, :], g[:, :, 2:4, :], ALU.add).then_inc(f_es.sem, 1)
                pool.wait_ge(f_es.sem, f_es.at(i, 3 * pair + 2))
                pool.tensor_tensor(v[:, 2 * pair:2 * pair + 2, 0:HD], g[:, :, 0, :], g[:, :, 1, :],
                                   ALU.add).then_inc(f_es.sem, 1)

            def tile(i, j):
                if j is not None:
                    x_rstd(j)
                f_gates(i)
                f_rot_add(i)
                for pair in range(H // 2):
                    f_expert_sum(i, pair)
                if j is not None:
                    f_rstd(j)

            pool.memset(powers[:], -0.5)
            pool.memset(eps_t[:], EPS)
            pool.memset(x_v[:], 1.0)
            pool.memset(v[:], 1.0)
            pool.memset(x_att[:], 0.0)
            pool.memset(att[:], 0.0)
            pool.memset(q_bd[:], 0.0)
            pool.memset(go3[:], 0.0).then_inc(set_pool.sem, 1)
            pool.wait_ge(set_pool.sem, 1)
            x_rstd(0)
            f_rstd(0)
            with pool.Fori(0, TILES - 1) as i:
                tile(i, i + 1)
            tile(TILES - 1, None)

            with pool.Fori(0, HALVES) as hf:
                for k, mv, r in ((0, t_mv, t_r), (1, u_mv, u_r)):
                    pool.wait_ge(mv.sem, mv.at(hf))
                    pool.tensor_tensor(tail_ve[:, k, 0, :], tail_mv[:, k, :, 1], eps_t[:, 0:HT],
                                       ALU.add).then_inc(r.sem, 1)
                    pool.wait_ge(r.sem, r.at(hf, 1))
                    pool.tensor_tensor(tail_ve[:, k, 1, :], tail_ve[:, k, 0, :], powers[:, 0:HT],
                                       ALU.pow).then_inc(r.sem, 1)


_INS = ["x", "ctx_1024", "mask_BxS2_ik0", "L0_xattn_w_q", "L0_xattn_w_kv", "L0_xattn_w_proj", "L0_xattn_b_proj",
        "L0_xattn_g_x", "L0_xattn_b_x", "L0_xattn_g_kv", "L0_xattn_b_kv", "L0_ffn_Wq", "L0_ffn_Wk", "L0_ffn_Wv",
        "L0_ffn_Wo", "L0_ffn_Wsel_v", "L0_ffn_Wsel_o", "L0_ffn_ln1_g", "L0_ffn_ln1_b", "L0_ffn_ln2_g",
        "L0_ffn_ln2_b", "L0_ffn_W1", "L0_ffn_b1", "L0_ffn_W2", "L0_ffn_b2"]


def kernel(**inputs):
    import concourse.bacc as bacc
    import ml_dtypes
    from concourse.bass_utils import run_bass_kernel_spmd

    nc = bacc.Bacc("TRN2", target_bir_lowering=False, num_devices=1)
    const, const_sel = constants()
    data = {name: np.ascontiguousarray(inputs[name]) for name in _INS}
    data["const"] = const
    data["const_sel"] = const_sel.astype(ml_dtypes.bfloat16)
    data["const_idb"] = np.eye(P).astype(ml_dtypes.bfloat16)
    arrays, args = {}, []
    for name, a in data.items():
        arrays[f"in_{name}"] = a
        args.append(nc.dram_tensor(f"in_{name}", a.shape, mybir.dt.from_np(a.dtype), kind="ExternalInput").ap())
    args.append(nc.dram_tensor("out_0", (BATCH, SEQ, DIM), F32, kind="ExternalOutput").ap())
    build(nc, *args)
    r = run_bass_kernel_spmd(nc, [arrays], core_ids=[0])
    return r.results[0]["out_0"]
```

```python
from contextlib import ExitStack

import numpy as np

import concourse.bass as bass
from concourse import mybir

F32 = mybir.dt.float32
F32R = mybir.dt.float32r
BF16 = mybir.dt.bfloat16
I32 = mybir.dt.int32
ALU = mybir.AluOpType
ACT = mybir.ActivationFunctionType
AX_X = mybir.AxisListType.X

P = 128
BATCH, SEQ, DIM = 16, 64, 128
TILES = BATCH * SEQ // P
XH, XD = 16, 8
H, HD, E = 16, 64, 8
HP = H // 2
NROT, HALF_ROT = 32, 16
FF = 512
HALVES, HTOK = 2, 512
HT = HTOK // P
QUADS = H // 4
SPLITS = 3
EPS = 1e-5
FILL = 1e9
BIG = 1e30

C_ID, C_BLK, C_COS, C_SIN, C_RANK, C_END = 0, 128, 132, 164, 196, 204


def constants():
    c = np.zeros((P, C_END), np.float32)
    c[:, C_ID:C_ID + P] = np.eye(P)
    own = np.arange(P)[:, None] // XD % 4 == np.arange(4)[None]
    c[:, C_BLK:C_BLK + 4] = own * np.float32(XD ** -0.5)
    inv = 10000.0 ** (-np.arange(HALF_ROT, dtype=np.float32) / HALF_ROT)
    angle = (np.arange(P) % SEQ).astype(np.float32)[:, None] * inv[None].astype(np.float32)
    cos, sin = np.cos(angle), np.sin(angle)
    c[:, C_COS:C_COS + NROT] = np.concatenate([cos, cos], 1)
    c[:, C_SIN:C_SIN + NROT] = np.concatenate([sin, -sin], 1)
    c[:, C_RANK:C_RANK + E] = E - np.arange(E)
    row = np.arange(P)
    sel = np.zeros((P, 2, E, P), np.float32)
    for pair in range(2):
        for e in range(E):
            for half in range(2):
                rows = (row // 32 == 2 * pair + half) & (row % 32 < 8 * SPLITS) & (row % 8 == e)
                sel[rows, pair, e, half * HD:(half + 1) * HD] = 1
    fill = np.full(1, -FILL, np.float32)
    parts = []
    for _ in range(SPLITS):
        part = (fill.view(np.uint32) & 0xFFFF0000).view(np.float32)
        parts.append(np.repeat(part, P))
        fill = fill - part
    assert not fill.any()
    return c, sel.reshape(P, 2 * E * P), np.stack(parts)


class Count:

    def __init__(self, sem, per, first=0):
        self.sem, self.per, self.first = sem, per, first

    def at(self, i, k=None):
        return i * self.per + (self.per if k is None else k) + self.first


class Room:

    def __init__(self, hat, nT, kT, v, qd, p, mx, att, rc, o, oT, X, X0, X1):
        self.hat, self.nT, self.kT, self.v, self.qd, self.p, self.mx = hat, nT, kT, v, qd, p, mx
        self.att, self.rc, self.o, self.oT, self.X, self.X0, self.X1 = att, rc, o, oT, X, X0, X1


def build(nc, x, ctx_in, mask, w_q, w_kv, w_proj, b_proj, g_x, b_x, g_kv, b_kv, Wq, Wk, Wv, Wo,
          Wsel_v, Wsel_o, ln1_g, ln1_b, ln2_g, ln2_b, W1, b1, W2, b2, const, const_sel, const_fill, const_idb, out):
    st = ExitStack()
    with st:
        def sb(name, shape, dt=F32):
            return st.enter_context(nc.sbuf_tensor(name, shape, dt))

        def sem(name, per=1, first=0):
            return Count(st.enter_context(nc.semaphore(name)), per, first)

        cst = sb("cst", [P, C_END])
        ident = cst[:, C_ID:C_ID + P]
        head_block = cst[:, C_BLK:C_BLK + 4]
        cos_t, sin_t = cst[:, C_COS:C_COS + NROT], cst[:, C_SIN:C_SIN + NROT]
        rank_t = cst[:, C_RANK:C_RANK + E]
        identb = sb("identb", [P, P], BF16)
        fill_row = sb("fill_row", [SPLITS, P], BF16)
        masked = sb("masked", [SPLITS, TILES, P], BF16)
        wq_sb = sb("wq_sb", [P, DIM])
        wkv_sb = sb("wkv_sb", [P, 2 * DIM])
        wproj_sb = sb("wproj_sb", [P, DIM])
        Wq_sb = sb("Wq_sb", [P, H, HD])
        Wk_sb = sb("Wk_sb", [P, H, HD])
        wsel_sb = sb("wsel_sb", [P, 2 * H * E])
        cols = sb("cols", [P, 16])
        COL = {n: cols[:, k:k + 1] for k, n in enumerate(
            ["g_x", "b_x", "g_kv", "b_kv", "ln1_g", "ln1_b", "b2"])}
        b1_sb = cols[:, 8:12]
        rows = sb("rows", [P, 3, DIM])
        powers = sb("powers", [P, 2 * TILES])
        eps_t = sb("eps_t", [P, 2 * TILES])

        x_all = sb("x_all", [P, TILES, DIM])
        c_all = sb("c_all", [P, TILES, DIM])
        src_all, x2_all = c_all, x_all
        keep_k = sb("keep_k", [P, TILES, P], BF16)
        oT_all = sb("oT_all", [P, HP, TILES * P])
        wv_raw = oT_all[:, :, :].rearrange("p a (b n) -> p (a b) n", b=2)
        goT_all = sb("goT_all", [P, QUADS, TILES * P], BF16)

        x_bn = sb("x_bn", [P, 2, TILES, 6])
        x_mv = sb("x_mv", [P, 2, TILES, 2])
        x_ve = sb("x_ve", [P, 2, TILES])
        x_r = sb("x_r", [P, 2, TILES])
        x_hat = sb("x_hat", [P, 2, DIM])
        x_nT = sb("x_nT", [P, 2, P])
        x_kT = sb("x_kT", [P, P])
        x_v = sb("x_v", [P, XH, XD + 1])
        x_qd = sb("x_qd", [P, 2, 2, 2, SEQ])
        x_p = sb("x_p", [P, XH, SEQ])
        x_mx = sb("x_mx", [P, XH])
        x_att = sb("x_att", [P, XH, P])
        x_rc = sb("x_rc", [P, XH])
        x_o = sb("x_o", [P, XH, XD])
        x_oT = sb("x_oT", [P, P])
        f_bn = sb("f_bn", [P, 6])
        f_mv = sb("f_mv", [P, 2])
        f_ve = sb("f_ve", [P, 2])
        x2_s = sb("x2_s", [P, DIM])
        src_s = sb("src_s", [P, DIM])

        srcT_next = sb("srcT_next", [P, P])
        gate_next = sb("gate_next", [P, 2, H, E])
        srcT = sb("srcT", [P, P])
        srcT_hi = sb("srcT_hi", [P, P], F32R)
        srcT_lo = sb("srcT_lo", [P, P], F32R)
        sg = sb("sg", [P, 2 * H, E])
        lg_e = sb("lg_e", [P, 2 * H, E])
        top = sb("top", [P, 2, 2 * H])
        eq = sb("eq", [P, 2 * H, E])
        oh1 = sb("oh1", [P, 2 * H, E])
        oh2 = sb("oh2", [P, 2 * H, E])
        l2 = lg_e
        kk = sb("kk", [P, 2 * H])
        gate = sb("gate", [P, 2, H, E])
        go3 = sb("go3", [P, QUADS, 4, 4, E], BF16)
        go_r = sb("go_r", [P, H, E])
        qk = sb("qk", [P, 2 * H, HD])
        q_bd = sb("q_bd", [P, HP, 2, 2, SEQ])
        kT = sb("kT", [P, HP, P])
        p_f = sb("p_f", [P, H, SEQ])
        f_mx = sb("f_mx", [P, H])
        att = sb("att", [P, H, P])
        v = sb("v", [P, H, HD + 1])
        gy = sb("gy", [P, 4, E, HD])
        f_rc = sb("f_rc", [P, H])
        rot_c = kT[:].rearrange("p k t -> p (k t)").rearrange("p (h n) -> p h n", n=NROT)
        rot_s = p_f[:].rearrange("p h s -> p (h s)").rearrange("p (h n) -> p h n", n=NROT)
        o_sb = x_p
        gy_flat = gy[:].rearrange("p k e n -> p (k e n)")
        mask_k = gy_flat[:, 0:TILES * P].bitcast(I32).rearrange("p (t s) -> p t s", t=TILES)
        wsel_raw = gy_flat[:, TILES * P:TILES * P + 2 * DIM].rearrange("p (a d) -> p a d", a=2)
        sel = x_att[:, 0:8, :].rearrange("p h s -> p (h s)").bitcast(BF16).rearrange("p (a m) -> p a m", m=P)
        W1_sb = x_att[:, 8:12, :].rearrange("p h s -> p (h s)")
        W2_sb = x_att[:, 12:16, :]
        tail_bn = sb("tail_bn", [P, 2, HT, 6])
        tail_mv = sb("tail_mv", [P, 2, HT, 2])
        tail_ve = sb("tail_ve", [P, 2, 2, HT])
        wv_rooms = ExitStack()
        wv_hi = wv_rooms.enter_context(nc.sbuf_tensor("wv_hi", [P, H, E * HD], F32R))
        wv_lo = wv_rooms.enter_context(nc.sbuf_tensor("wv_lo", [P, H, E * HD], F32R))
        wv_rooms.close()
        big_w = sb("big_w", [P, H, E * HD])

        ps = st.enter_context(nc.psum_tensor("ps", [P, 8, 512], F32))
        Y = [ps[:, 0, :], ps[:, 1, :]]
        A = ps[:, 2:4, :].rearrange("p a b -> p (a b)")
        T = ps[:, 4:6, :].rearrange("p a b -> p (a b)")
        X = ps[:, 6:8, :].rearrange("p a b -> p (a b)")
        X0, X1 = ps[:, 6, :], ps[:, 7, :]

        room = Room(hat=x_hat, nT=x_nT, kT=x_kT, v=x_v, qd=x_qd, p=x_p, mx=x_mx, att=x_att, rc=x_rc,
                    o=x_o, oT=x_oT, X=X, X0=X0, X1=X1)
        spare = qk[:].rearrange("p h n -> p (h n)")
        beside_room = Room(
            hat=spare[:, 0:2 * P].rearrange("p (a d) -> p a d", a=2),
            nT=spare[:, 2 * P:4 * P].rearrange("p (a d) -> p a d", a=2),
            kT=spare[:, 4 * P:5 * P], oT=spare[:, 5 * P:6 * P],
            o=spare[:, 6 * P:7 * P].rearrange("p (h d) -> p h d", d=XD),
            qd=spare[:, 8 * P:12 * P].rearrange("p (b a h s) -> p b a h s", b=2, a=2, h=2),
            v=v[:, :, HD - XD:HD + 1], p=p_f, mx=f_mx, att=att, rc=f_rc,
            X=T, X0=ps[:, 4, :], X1=ps[:, 5, :])

        def at_room(j):
            return beside_room if isinstance(j, int) and j == 1 else room

        loads = {n: sem("ld_" + n) for n in
                 ["const", "sel", "x", "ctx", "mask", "vec", "xw", "qk", "wsel", "ff", "idb"]}
        ld_wv = [sem(f"ld_wv{k}") for k in range(4)]
        ld_wo = [sem(f"ld_wo{k}") for k in range(4)]
        wv_rounded, wv_split, wv_split_dve = sem("wv_rounded"), sem("wv_split"), sem("wv_split_dve")
        ready_w, set_dve, set_pool, set_t = sem("ready_w"), sem("set_dve"), sem("set_pool"), sem("set_t")
        HEAD_TILES = 2
        xs_bn, xs_mv, xs_r, xs_hat = sem("xs_bn"), sem("xs_mv"), sem("xs_r", 7), sem("xs_hat", 2)
        xs_tp, xs_n, xs_proj = sem("xs_tp"), sem("xs_n", 2), sem("xs_proj")
        xs_qk, xs_sa, xs_s = sem("xs_qk", 3), sem("xs_sa", 2), sem("xs_s")
        xs_mx, xs_sub, xs_e, xs_pt = sem("xs_mx"), sem("xs_sub"), sem("xs_e"), sem("xs_pt")
        xs_att, xs_pv, xs_rc, xs_o = sem("xs_att", 2), sem("xs_pv"), sem("xs_rc"), sem("xs_o")
        xs_ot, xs_otc, xs_pj, xs_x2 = sem("xs_ot"), sem("xs_otc"), sem("xs_pj"), sem("xs_x2")
        xs_b = sem("xs_b")
        fs_bn, fs_mv, fs_r, fs_src = sem("fs_bn"), sem("fs_mv"), sem("fs_r", 2), sem("fs_src", 2)
        g_tp, g_srcT, g_g, g_lg, g_top = sem("g_tp"), sem("g_srcT"), sem("g_g"), sem("g_lg"), sem("g_top", 11)
        g_sig, g_gate = sem("g_sig", 2), sem("g_gate", 2)
        f_srcT, f_gate, f_q, f_k, f_qkev = sem("f_srcT", 2), sem("f_gate"), sem("f_q"), sem("f_k"), sem("f_qkev", 2)
        f_low = sem("f_low")
        f_go, f_gt, f_got, f_rot, f_ra = sem("f_go", 4), sem("f_gt"), sem("f_got"), sem("f_rot", 4), sem("f_ra", 4)
        f_qt, f_kt, f_qb, f_kb = sem("f_qt"), sem("f_kt"), sem("f_qb", 2), sem("f_kb")
        f_s, f_m, f_sub, f_e = sem("f_s"), sem("f_m"), sem("f_sub"), sem("f_e")
        f_pt, f_att, f_pv, f_rcs = sem("f_pt"), sem("f_att", 2), sem("f_pv"), sem("f_rcs", 2)
        f_on, f_ot, f_otev = sem("f_on", 2), sem("f_ot"), sem("f_otev")
        f_y, f_vg, f_es = sem("f_y", H), sem("f_vg", H), sem("f_es", 3 * H // 2)
        STEPS = HP * E
        VEC_LOADS, FF_LOADS = 5, 11
        p_res, p_bc, p_gm, p_fin = sem("p_res"), sem("p_bc", STEPS), sem("p_gm", STEPS), sem("p_fin", STEPS)
        t_acc, t_rt, t_bn, t_mv, t_r = sem("t_acc"), sem("t_rt"), sem("t_bn", HT), sem("t_mv", HT), sem("t_r", 2)
        t_z, t_zt, t_y1, t_h, t_relu = sem("t_z", HT + 1), sem("t_zt"), sem("t_y1"), sem("t_h", 4), sem("t_relu", 4)
        t_o, t_z2, t_z2t = sem("t_o"), sem("t_z2"), sem("t_z2t")
        u_bn, u_mv, u_r, u_z = sem("u_bn", HT), sem("u_mv", HT), sem("u_r", 2), sem("u_z", HT + 1)
        u_g, u_b, u_out, u_st = sem("u_g"), sem("u_b"), sem("u_out"), sem("u_st", 16)
        block = st.enter_context(nc.Block())

        def first(i):
            return isinstance(i, int) and i == 0

        x_tok = x.rearrange("(t b) s d -> (b s) t d", b=2)
        ctx_tok = ctx_in.rearrange("(t b) s d -> (b s) t d", b=2)
        out_tok = out.rearrange("(t b) s d -> (b s) t d", b=2)
        wv_cols = Wv.rearrange("h e d p -> d h e p")
        wo_view = big_w[:, :, :].rearrange("p (a b) n -> p a (b n)", b=2).rearrange("p a (e n) -> p a e n", e=E)
        wv_view = wv_raw.rearrange("p h (e n) -> p h e n", e=E)

        g_ring = [gy[:, k, :, :].rearrange("p e n -> p (e n)") for k in range(4)]
        acc = [ps[:, 0, :], ps[:, 5, :]]
        BC = [ps[:, 1, :], ps[:, 6, :], ps[:, 7, :]]
        TA = ps[:, 4, :]
        TH = [ps[:, 2, :], ps[:, 3, :]]
        att_flat, bd_flat = att[:, :, :].rearrange("p h s -> p (h s)"), q_bd[:].rearrange("p a b c s -> p (a b c s)")
        r1T, y1T, z2T = att_flat[:, 0:HTOK], att_flat[:, HTOK:2 * HTOK], att_flat[:, 2 * HTOK:3 * HTOK]
        hT = bd_flat.rearrange("p (k t) -> p k t", k=4)
        z_t = x_p[:, 0:8, :].rearrange("p h s -> p (h s)").rearrange("p (t d) -> p t d", t=HT)
        z2_t = x_qd[:].rearrange("p b a h s -> p (b a h s)").rearrange("p (t d) -> p t d", t=HT)

        @block.sync
        def _(sp):
            sp.dma_start(x_all[:], x_tok).then_inc(loads["x"].sem, 16)
            sp.dma_start(c_all[:], ctx_tok).then_inc(loads["ctx"].sem, 16)
            def column(name, a, load):
                sp.dma_start(COL[name], a.rearrange("(p o) -> p o", o=1)).then_inc(loads[load].sem, 16)

            def row(k, a, load):
                sp.dma_start(rows[:, k, :], a.rearrange("(o d) -> o d", o=1).broadcast_to([P, DIM])).then_inc(
                    loads[load].sem, 16)

            sp.dma_start(cst[:], const).then_inc(loads["const"].sem, 16)
            for name, a in [("g_x", g_x), ("b_x", b_x), ("g_kv", g_kv), ("b_kv", b_kv)]:
                column(name, a, "vec")
            for dst, a in [(wq_sb, w_q), (wkv_sb, w_kv), (wproj_sb, w_proj)]:
                sp.dma_start(dst[:], a).then_inc(loads["xw"].sem, 16)
            m_row = mask.rearrange("(o t b) s -> o t (b s)", o=1, b=2)
            sp.dma_start(mask_k, m_row.broadcast_to([P, TILES, P])).then_inc(loads["mask"].sem, 16)
            sp.dma_start(fill_row[:], const_fill).then_inc(loads["const"].sem, 16)
            row(0, b_proj, "vec")
            sp.dma_start(wsel_raw[:, 0, :], Wsel_v.rearrange("h e d -> (h e) d")).then_inc(loads["wsel"].sem, 16)
            sp.dma_start(wsel_raw[:, 1, :], Wsel_o.rearrange("h e d -> (h e) d")).then_inc(loads["wsel"].sem, 16)
            sp.dma_start(Wq_sb[:], Wq.rearrange("h d p -> d h p")).then_inc(loads["qk"].sem, 16)
            sp.dma_start(Wk_sb[:], Wk.rearrange("h d p -> d h p")).then_inc(loads["qk"].sem, 16)
            for k in range(4):
                for h in range(4 * k, 4 * k + 4):
                    sp.dma_start(wv_view[:, h], wv_cols[:, h]).then_inc(ld_wv[k].sem, 16)
            sp.dma_start(identb[:], const_idb).then_inc(loads["idb"].sem, 16)
            for name, a in [("ln1_g", ln1_g), ("ln1_b", ln1_b), ("b2", b2)]:
                column(name, a, "ff")
            for k in range(4):
                sp.dma_start(b1_sb[:, k:k + 1], b1[P * k:P * k + P].rearrange("(p o) -> p o", o=1)).then_inc(
                    loads["ff"].sem, 16)
            row(1, ln2_g, "ff")
            row(2, ln2_b, "ff")
            sp.wait_ge(xs_pv.sem, xs_pv.at(TILES - 1))
            sp.dma_start(sel, const_sel.rearrange("p (a m) -> p a m", m=P)).then_inc(loads["sel"].sem, 16)
            sp.dma_start(W1_sb, W1).then_inc(loads["ff"].sem, 16)
            sp.dma_start(W2_sb, W2.rearrange("(k p) n -> p k n", p=P)).then_inc(loads["ff"].sem, 16)
            for k in range(4):
                sp.wait_ge(f_y.sem, f_y.at(TILES - 1, 4 * k + 4))
                for hp in (2 * k, 2 * k + 1):
                    for b in range(2):
                        sp.dma_start(wo_view[64 * b:64 * b + 64, hp],
                                     Wo[2 * hp + b].rearrange("e p n -> p e n")).then_inc(ld_wo[k].sem, 16)
            with sp.Fori(0, HALVES) as hf:
                sp.wait_ge(u_out.sem, u_out.at(hf))
                sp.dma_start(out_tok[:, bass.ds(hf * HT, HT), :], x_all[:, bass.ds(hf * HT, HT), :]).then_inc(u_st.sem, 16)
            sp.wait_ge(u_st.sem, u_st.at(HALVES - 1))

        @block.tensor
        def _(pe):
            def x_transpose(j):
                r = at_room(j)
                pe.wait_ge(xs_hat.sem, xs_hat.at(j))
                pe.transpose(r.X0[:, 0:P], r.hat[:, 0, :], ident)
                pe.transpose(r.X0[:, P:2 * P], r.hat[:, 1, :], ident).then_inc(xs_tp.sem, 1)

            def x_project(j):
                r = at_room(j)
                pe.wait_ge(xs_n.sem, xs_n.at(j))
                pe.matmul(r.X0[:, 2 * P:3 * P], wq_sb[:], r.nT[:, 0, :], start=True, stop=True)
                pe.matmul(r.X0[:, 0:P], r.nT[:, 1, :], wkv_sb[:, DIM:], start=True, stop=True)
                pe.matmul(r.X0[:, 3 * P:4 * P], wkv_sb[:, 0:DIM], r.nT[:, 1, :],
                          start=True, stop=True).then_inc(xs_proj.sem, 1)

            def x_scores(j, half):
                r = at_room(j)
                def fill(c):
                    return pe.matmul(r.X[:, 512 * c:512 * c + 512], fill_row[:],
                                     masked[:, j, :].unsqueeze(1).broadcast_to([SPLITS, 4, P]), start=True,
                                     stop=False, skip_group_check=True)

                def four_heads(g):
                    for k in range(4):
                        pair, b = k // 2, k % 2
                        at = SEQ * (2 * (2 * g + pair) + b)
                        mm = pe.matmul(r.X[:, at:at + SEQ],
                                       r.qd[32 * g:32 * g + 32, b, pair].rearrange("p h s -> p (h s)"),
                                       r.kT[32 * g:32 * g + 32, SEQ * b:SEQ * b + SEQ], start=False,
                                       stop=(g % 2 == 1 and k == 3), skip_group_check=True)
                    return mm

                if half == 0:
                    pe.wait_ge(xs_qk.sem, xs_qk.at(j))
                    if not (isinstance(j, int) and j < 2):
                        pe.wait_ge(f_got.sem, f_got.at(j - 2))
                    fill(1).then_inc(xs_sa.sem, 1)
                    fill(0)
                    four_heads(0)
                    pe.wait_ge(xs_sa.sem, xs_sa.at(j, 1))
                    four_heads(2).then_inc(xs_sa.sem, 1)
                else:
                    pe.wait_ge(xs_sa.sem, xs_sa.at(j, 2))
                    four_heads(1)
                    four_heads(3).then_inc(xs_s.sem, 1)

            def x_ptrans(j):
                r = at_room(j)
                pe.wait_ge(xs_e.sem, xs_e.at(j))
                for k in range(8):
                    mm = pe.transpose(r.X[:, P * k:P * k + P], r.p[:, 2 * k:2 * k + 2, :].rearrange(
                        "p h s -> p (h s)"), ident)
                mm.then_inc(xs_pt.sem, 1)

            def x_values(j, half):
                r = at_room(j)
                if half == 0:
                    pe.wait_ge(xs_att.sem, xs_att.at(j))
                for h in range(XH // 2 * half, XH // 2 * (half + 1)):
                    mm = pe.matmul(r.X0[:, (XD + 1) * h:(XD + 1) * (h + 1)], r.att[:, h, :], r.v[:, h, :],
                                   start=True, stop=True)
                if half == 1:
                    mm.then_inc(xs_pv.sem, 1)

            def x_otrans(j):
                r = at_room(j)
                pe.wait_ge(xs_o.sem, xs_o.at(j))
                pe.transpose(r.X1[:, 0:P], r.o[:, :, :].rearrange("p h d -> p (h d)"), ident).then_inc(xs_ot.sem, 1)

            def x_out(j):
                r = at_room(j)
                pe.wait_ge(xs_otc.sem, xs_otc.at(j))
                pe.matmul(r.X1[:, P:2 * P], r.oT[:], wproj_sb[:], start=True, stop=True).then_inc(xs_pj.sem, 1)

            def g_transpose(g):
                pe.wait_ge(fs_src.sem, fs_src.at(g))
                pe.transpose(X1[:, 3 * P:4 * P], src_s[:], ident).then_inc(g_tp.sem, 1)

            def g_logits(g):
                pe.wait_ge(g_srcT.sem, g_srcT.at(g))
                pe.matmul(X1[:, P:3 * P], srcT_next[:], wsel_sb[:], start=True, stop=True).then_inc(g_g.sem, 1)

            def f_project(i):
                pe.wait_ge(f_srcT.sem, f_srcT.at(i, 1))
                if first(i):
                    pe.wait_ge(xs_x2.sem, xs_x2.at(1))
                else:
                    pe.wait_ge(f_att.sem, f_att.at(i, 0))
                    pe.wait_ge(f_sub.sem, f_sub.at(i, 0))
                for w, dst, done in ((Wq_sb, T, f_q), (Wk_sb, A, f_k)):
                    for c in range(2):
                        mm = pe.matmul(dst[:, 512 * c:512 * c + 512], srcT[:],
                                       w[:, 8 * c:8 * c + 8, :].rearrange("p h s -> p (h s)"),
                                       start=True, stop=True)
                    mm.then_inc(done.sem, 1)

            def f_value(i, h):
                if h < 2 and not first(i):
                    pe.wait_ge(f_vg.sem, f_vg.at(i, h - 1))
                if h >= 2:
                    pe.wait_ge(f_vg.sem, f_vg.at(i, h - 1))
                if h == 0:
                    pe.wait_ge(f_low.sem, f_low.at(i))
                pe.matmul(Y[h % 2], srcT_hi[:], wv_hi[:, h, :], start=True, stop=False)
                pe.matmul(Y[h % 2], srcT_hi[:], wv_lo[:, h, :], start=False, stop=False)
                pe.matmul(Y[h % 2], srcT_lo[:], wv_hi[:, h, :], start=False, stop=True).then_inc(f_y.sem, 1)

            def f_turn(i, half, dst, done):
                pe.wait_ge(f_ra.sem, f_ra.at(i, 2 * half + 2))
                for k in range(8):
                    mm = pe.transpose(dst[:, P * k:P * k + P],
                                      qk[:, H * half + 2 * k:H * half + 2 * k + 2, :].rearrange(
                                          "p h s -> p (h s)"), ident)
                mm.then_inc(done.sem, 1)

            def f_qtrans(i):
                if not first(i):
                    pe.wait_ge(f_on.sem, f_on.at(i, 0))
                f_turn(i, 0, A, f_qt)

            def f_ktrans(i):
                if not first(i):
                    pe.wait_ge(f_otev.sem, f_otev.at(i, 0))
                f_turn(i, 1, T, f_kt)

            def f_scores(i, half):
                if half == 0:
                    pe.wait_ge(f_qb.sem, f_qb.at(i))
                    pe.wait_ge(f_kb.sem, f_kb.at(i))
                for k in range(HP // 2 * half, HP // 2 * (half + 1)):
                    for b in range(2):
                        at = SEQ * (2 * k + b)
                        mm = pe.matmul(A[:, at:at + SEQ], q_bd[:, k, b].rearrange("p h s -> p (h s)"),
                                       kT[:, k, SEQ * b:SEQ * b + SEQ], start=True, stop=True)
                if half == 1:
                    mm.then_inc(f_s.sem, 1)

            def f_ptrans(i):
                pe.wait_ge(f_e.sem, f_e.at(i))
                for k in range(8):
                    mm = pe.transpose(T[:, P * k:P * k + P], p_f[:, 2 * k:2 * k + 2, :].rearrange(
                        "p h s -> p (h s)"), ident)
                mm.then_inc(f_pt.sem, 1)

            def f_gtrans(i):
                pe.wait_ge(f_go.sem, f_go.at(i))
                if not (isinstance(i, int) and i == TILES - 1):
                    pe.wait_ge(g_lg.sem, g_lg.at(i + 1))
                x1 = X1.bitcast(BF16)
                for q in range(QUADS):
                    mm = pe.transpose(x1[:, P * (q + 2):P * (q + 3)],
                                      go3[:, q].rearrange("p h s e -> p (h s e)"), identb[:])
                mm.then_inc(f_gt.sem, 1)

            def d_values(i, half):
                if half == 0:
                    pe.wait_ge(f_att.sem, f_att.at(i))
                    pe.wait_ge(f_es.sem, f_es.at(i))
                    if not (isinstance(i, int) and i == TILES - 1):
                        pe.wait_ge(f_qkev.sem, f_qkev.at(i + 1))
                for h in range(H // 2 * half, H // 2 * (half + 1)):
                    mm = pe.matmul(ps[:, 2 + h // 7, (HD + 1) * (h % 7):(HD + 1) * (h % 7 + 1)],
                                   att[:, h, :], v[:, h, :], start=True, stop=True)
                if half == 1:
                    mm.then_inc(f_pv.sem, 1)

            def d_otrans(i):
                pe.wait_ge(f_on.sem, f_on.at(i))
                for k in range(HP):
                    mm = pe.transpose(T[:, P * k:P * k + P],
                                      o_sb[:, 2 * k:2 * k + 2, :].rearrange("p h s -> p (h s)"), ident)
                mm.then_inc(f_ot.sem, 1)

            def tile(i, d, g, x):
                f_project(i)
                beside = {
                    0: [(x_transpose, x)], 1: [(d_values, d, 0)], 2: [(g_transpose, g), (d_values, d, 1)],
                    3: [(g_logits, g), (x_project, x)], 4: [(f_gtrans, i), (d_otrans, d)],
                    5: [(x_scores, x, 0)], 6: [(x_scores, x, 1)], 7: [(f_qtrans, i)], 8: [(f_ktrans, i)],
                    9: [(x_ptrans, x)], 10: [(f_scores, i, 0)], 11: [(f_scores, i, 1)], 12: [(x_values, x, 0)],
                    13: [(x_values, x, 1)], 14: [(f_ptrans, i), (x_otrans, x)], 15: [(x_out, x)],
                }
                for h in range(H):
                    f_value(i, h)
                    for step, t, *half in beside.get(h, ()):
                        if t is not None:
                            step(t, *half)

            pe.wait_ge(loads["const"].sem, 32)
            pe.wait_ge(loads["xw"].sem, 48)

            def x_all_scores(x):
                x_scores(x, 0)
                x_scores(x, 1)

            def x_all_values(x):
                x_values(x, 0)
                x_values(x, 1)

            for f in (x_transpose, x_project, x_all_scores, x_ptrans, x_all_values, x_otrans, x_out):
                f(0)
                f(1)
            pe.wait_ge(loads["wsel"].sem, 32)
            pe.transpose(Y[0][:, 0:P], wsel_raw[:, 0, :], ident)
            pe.transpose(Y[0][:, P:2 * P], wsel_raw[:, 1, :], ident).then_inc(set_t.sem, 1)
            g_transpose(0)
            pe.wait_ge(ready_w.sem, 1)
            g_logits(0)
            pe.wait_ge(loads["qk"].sem, 32)
            pe.wait_ge(wv_split.sem, 4)
            pe.wait_ge(wv_split_dve.sem, 4)
            pe.wait_ge(loads["idb"].sem, 16)
            tile(0, None, 1, 2)
            with pe.Fori(1, TILES - 2) as i:
                tile(i, i - 1, i + 1, i + 2)
            tile(TILES - 2, TILES - 3, TILES - 1, None)
            tile(TILES - 1, TILES - 2, None, None)
            def spread(hf, s):
                if s >= 3:
                    pe.wait_ge(p_gm.sem, p_gm.at(hf, s - 2))
                pe.matmul(BC[s % 3], sel[:, s % 16, :], goT_all[:, s // 16, hf * HTOK:(hf + 1) * HTOK],
                          start=True, stop=True).then_inc(p_bc.sem, 1)

            def experts(hf, beside):
                pe.wait_ge(p_res.sem, p_res.at(hf))
                for t in range(HT):
                    pe.matmul(acc[hf][:, P * t:P * t + P], z2_t[:, t, :], ident, start=(t == 0), stop=False,
                              skip_group_check=True)
                spread(hf, 0)
                spread(hf, 1)
                for s in range(STEPS):
                    if s + 2 < STEPS:
                        spread(hf, s + 2)
                    if s % 16 == 0:
                        pe.wait_ge(ld_wo[s // 16].sem, 64)
                    pe.wait_ge(p_gm.sem, p_gm.at(hf, s + 1))
                    pe.matmul(acc[hf], wo_view[:, s // E, s % E, :], g_ring[s % 4], start=False,
                              stop=(s == STEPS - 1), skip_group_check=True).then_inc(p_fin.sem, 1)
                    if s in beside:
                        beside[s]()

            def turn_back(src, ready, hf, done):
                pe.wait_ge(ready.sem, ready.at(hf))
                for t in range(HT):
                    mm = pe.transpose(TA[:, P * t:P * t + P], src(t), ident)
                mm.then_inc(done.sem, 1)

            def tail_rows(hf):
                turn_back(lambda t: r1T[:, P * t:P * t + P], t_acc, hf, t_rt)

            def tail_columns(hf):
                turn_back(lambda t: z_t[:, t, :], t_z, hf, t_zt)

            def tail_last(hf):
                turn_back(lambda t: z2T[:, P * t:P * t + P], t_z2, hf, t_z2t)

            def tail_hidden(hf, k):
                if k == 0:
                    pe.wait_ge(t_y1.sem, t_y1.at(hf))
                if k >= 2:
                    pe.wait_ge(t_relu.sem, t_relu.at(hf, k - 1))
                pe.matmul(TH[k % 2], W1_sb[:, P * k:P * k + P], y1T, start=True, stop=True).then_inc(t_h.sem, 1)

            def tail_second(hf, k):
                pe.wait_ge(t_relu.sem, t_relu.at(hf, k + 1))
                mm = pe.matmul(TA, W2_sb[:, k, :], hT[:, k, :], start=(k == 0), stop=(k == 3))
                if k == 3:
                    mm.then_inc(t_o.sem, 1)

            def tail(hf):
                return [lambda: tail_rows(hf), lambda: tail_columns(hf), lambda: tail_hidden(hf, 0),
                        lambda: tail_hidden(hf, 1), lambda: tail_hidden(hf, 2), lambda: tail_hidden(hf, 3),
                        lambda: tail_second(hf, 0), lambda: tail_second(hf, 1), lambda: tail_second(hf, 2),
                        lambda: tail_second(hf, 3), lambda: tail_last(hf)]

            last = TILES - 1
            pe.wait_ge(f_got.sem, f_got.at(last))
            pe.wait_ge(loads["sel"].sem, 16)
            experts(0, {0: lambda: d_values(last, 0), 2: lambda: d_values(last, 1), 8: lambda: d_otrans(last)})
            pe.wait_ge(loads["ff"].sem, 16 * FF_LOADS)
            pe.wait_ge(f_otev.sem, f_otev.at(last))
            experts(1, dict(zip((1, 14, 18, 20, 22, 24, 26, 28, 30, 32, 38), tail(0))))
            for step in tail(1):
                step()

        @block.scalar
        def _(act):
            def on_diagonal(src, dst, done):
                for b in range(2):
                    act.activation(dst[64 * b:64 * b + 64, :, 64 * b:64 * b + 64],
                                   src[64 * b:64 * b + 64, :].rearrange("p (h s) -> p h s", s=SEQ),
                                   ACT.Copy).then_inc(done.sem, 1)

            def x_norm(j):
                r = at_room(j)
                act.wait_ge(xs_tp.sem, xs_tp.at(j))
                act.activation(r.nT[:, 0, :], r.X0[:, 0:P], ACT.Identity, bias=COL["b_x"],
                               scale=COL["g_x"]).then_inc(xs_n.sem, 1)
                act.activation(r.nT[:, 1, :], r.X0[:, P:2 * P], ACT.Identity, bias=COL["b_kv"],
                               scale=COL["g_kv"]).then_inc(xs_n.sem, 1)

            def x_exp(j):
                r = at_room(j)
                act.wait_ge(xs_sub.sem, xs_sub.at(j))
                act.activation(r.p[:], r.p[:], ACT.Exp).then_inc(xs_e.sem, 1)

            def x_att_copy(j):
                r = at_room(j)
                act.wait_ge(xs_pt.sem, xs_pt.at(j))
                on_diagonal(r.X, r.att, xs_att)

            def x_ot_copy(j):
                r = at_room(j)
                act.wait_ge(xs_ot.sem, xs_ot.at(j))
                act.activation(r.oT[:], r.X1[:, 0:P], ACT.Copy).then_inc(xs_otc.sem, 1)

            def g_src(g):
                if not first(g):
                    act.wait_ge(f_low.sem, f_low.at(g, 0))
                act.wait_ge(g_tp.sem, g_tp.at(g))
                act.activation(srcT_next[:], X1[:, 3 * P:4 * P], ACT.Copy).then_inc(g_srcT.sem, 1)

            def g_logit(g):
                act.wait_ge(g_g.sem, g_g.at(g))
                act.activation(lg_e[:].rearrange("p h e -> p (h e)"), X1[:, P:3 * P], ACT.Exp,
                               scale=-1.0).then_inc(g_lg.sem, 1)

            def f_take(i):
                if not first(i):
                    act.wait_ge(f_y.sem, f_y.at(i, 0))
                act.activation(srcT[:], srcT_next[:], ACT.Copy).then_inc(f_srcT.sem, 1)
                act.activation(srcT_hi[:], srcT_next[:], ACT.Copy).then_inc(f_srcT.sem, 1)
                act.wait_ge(g_gate.sem, g_gate.at(i))
                if not first(i):
                    act.wait_ge(f_vg.sem, f_vg.at(i, 0))
                    act.wait_ge(f_go.sem, f_go.at(i, 0))
                act.activation(gate[:], gate_next[:], ACT.Copy).then_inc(f_gate.sem, 1)

            def f_q_out(i):
                act.wait_ge(f_q.sem, f_q.at(i))
                act.activation(qk[:, 0:H, :].rearrange("p h s -> p (h s)"), T, ACT.Copy).then_inc(f_qkev.sem, 1)

            def f_k_out(i):
                act.wait_ge(f_k.sem, f_k.at(i))
                act.activation(qk[:, H:2 * H, :].rearrange("p h s -> p (h s)"), A, ACT.Copy).then_inc(f_qkev.sem, 1)

            def f_q_copy(i):
                act.wait_ge(f_qt.sem, f_qt.at(i))
                for a in range(2):
                    act.activation(q_bd[64 * a:64 * a + 64, :, :, a, :],
                                   A[64 * a:64 * a + 64, :].rearrange("p (k b s) -> p k b s", k=HP, b=2),
                                   ACT.Copy).then_inc(f_qb.sem, 1)

            def f_k_copy(i):
                act.wait_ge(f_kt.sem, f_kt.at(i))
                act.activation(kT[:].rearrange("p k s -> p (k s)"), T, ACT.Copy).then_inc(f_kb.sem, 1)

            def f_exps(i):
                act.wait_ge(f_sub.sem, f_sub.at(i))
                act.activation(p_f[:], p_f[:], ACT.Exp, scale=float(HD) ** -0.5).then_inc(f_e.sem, 1)

            def f_att_copy(i):
                act.wait_ge(f_pt.sem, f_pt.at(i))
                on_diagonal(T, att, f_att)

            def f_gt_copy(i):
                act.wait_ge(f_gt.sem, f_gt.at(i))
                act.activation(goT_all[:, :, bass.ds(i * P, P)],
                               X1.bitcast(BF16)[:, 2 * P:(QUADS + 2) * P].rearrange("p (q t) -> p q t", q=QUADS),
                               ACT.Copy).then_inc(f_got.sem, 1)

            def d_ot_copy(i):
                act.wait_ge(f_ot.sem, f_ot.at(i))
                act.activation(oT_all[:, :, bass.ds(i * P, P)], T.rearrange("p (h t) -> p h t", h=HP),
                               ACT.Copy).then_inc(f_otev.sem, 1)

            def tile(i, d, g, x):
                f_take(i)
                for step, t in ((f_q_out, i), (f_k_out, i), (x_norm, x), (g_src, g), (g_logit, g), (f_gt_copy, i),
                                (d_ot_copy, d), (f_q_copy, i), (x_exp, x), (f_k_copy, i), (x_att_copy, x),
                                (f_exps, i), (f_att_copy, i), (x_ot_copy, x)):
                    if t is not None:
                        step(t)

            act.wait_ge(loads["vec"].sem, 16 * VEC_LOADS)
            act.wait_ge(set_pool.sem, 1)
            def round_wv(lo, hi):
                for k in range(lo, hi):
                    act.wait_ge(ld_wv[k // 2].sem, 64)
                    act.activation(wv_hi[:, 2 * k:2 * k + 2, :], wv_raw[:, 2 * k:2 * k + 2, :],
                                   ACT.Copy).then_inc(wv_rounded.sem, 1)

            x_norm(0)
            x_norm(1)
            x_exp(0)
            round_wv(0, 2)
            x_exp(1)
            x_att_copy(0)
            x_att_copy(1)
            round_wv(2, 8)
            x_ot_copy(0)
            x_ot_copy(1)
            act.wait_ge(set_t.sem, 1)
            act.activation(wsel_sb[:], Y[0][:, 0:2 * P], ACT.Copy).then_inc(ready_w.sem, 1)
            g_src(0)
            g_logit(0)
            tile(0, None, 1, 2)
            with act.Fori(1, TILES - 2) as i:
                tile(i, i - 1, i + 1, i + 2)
            tile(TILES - 2, TILES - 3, TILES - 1, None)
            tile(TILES - 1, TILES - 2, None, None)
            d_ot_copy(TILES - 1)
            act.wait_ge(loads["ff"].sem, 16 * FF_LOADS)
            for hf in range(HALVES):
                act.wait_ge(p_fin.sem, p_fin.at(hf))
                act.activation(r1T, acc[hf], ACT.Copy).then_inc(t_acc.sem, 1)
                act.wait_ge(t_zt.sem, t_zt.at(hf))
                act.activation(y1T, TA, ACT.Identity, bias=COL["ln1_b"], scale=COL["ln1_g"]).then_inc(t_y1.sem, 1)
                for k in range(4):
                    act.wait_ge(t_h.sem, t_h.at(hf, k + 1))
                    act.activation(hT[:, k, :], TH[k % 2], ACT.Relu, bias=b1_sb[:, k:k + 1]).then_inc(t_relu.sem, 1)

        @block.vector
        def _(dve):
            def x_stats(lo, hi):
                for j in range(lo, hi):
                    dve.bn_stats(x_bn[:, 0, j, :], x_all[:, j, :]).then_inc(xs_bn.sem, 1)
                    dve.bn_stats(x_bn[:, 1, j, :], c_all[:, j, :]).then_inc(xs_bn.sem, 1)
                dve.wait_ge(xs_bn.sem, 2 * hi)
                for j in range(lo, hi):
                    for k in range(2):
                        dve.bn_aggr(x_mv[:, k, j, :], x_bn[:, k, j, :]).then_inc(xs_mv.sem, 1)

            def x_center(j):
                r = at_room(j)
                dve.tensor_scalar(r.hat[:, 0, :], x_all[:, j, :], x_mv[:, 0, j, 0:1], x_r[:, 0, bass.ds(j, 1)],
                                  ALU.subtract, ALU.mult).then_inc(xs_hat.sem, 1)
                dve.tensor_scalar(r.hat[:, 1, :], c_all[:, j, :], x_mv[:, 1, j, 0:1], x_r[:, 1, bass.ds(j, 1)],
                                  ALU.subtract, ALU.mult).then_inc(xs_hat.sem, 1)

            def x_bias(j):
                if not first(j):
                    dve.wait_ge(fs_src.sem, fs_src.at(j, 0))
                dve.tensor_tensor(x2_s[:], x_all[:, j, :], rows[:, 0, :], ALU.add).then_inc(xs_b.sem, 1)

            def x_blocks(j):
                r = at_room(j)
                dve.wait_ge(xs_proj.sem, xs_proj.at(j))
                q = r.X0[:, 2 * P:3 * P].rearrange("p (b o s) -> p b o s", b=2, o=1)
                dve.tensor_tensor(r.qd[:].rearrange("p b a h s -> p b (a h) s"), q.broadcast_to([P, 2, 4, SEQ]),
                                  head_block.rearrange("p (o h q) -> p o h q", o=1, q=1).broadcast_to([P, 2, 4, SEQ]),
                                  ALU.mult).then_inc(xs_qk.sem, 1)
                dve.tensor_tensor(r.kT[:], r.X0[:, 3 * P:4 * P], keep_k[:, j, :], ALU.mult).then_inc(xs_qk.sem, 1)
                dve.tensor_scalar(r.v[:, :, 0:XD], r.X0[:, 0:P].rearrange("p (h d) -> p h d", d=XD), 1.0, None,
                                  ALU.mult).then_inc(xs_qk.sem, 1)

            def x_soft(j):
                r = at_room(j)
                dve.wait_ge(xs_s.sem, xs_s.at(j))
                s = r.X.rearrange("p (h s) -> p h s", h=XH)
                dve.tensor_reduce(r.mx[:], s, AX_X, ALU.max).then_inc(xs_mx.sem, 1)
                dve.wait_ge(xs_mx.sem, xs_mx.at(j))
                dve.tensor_tensor(r.p[:], s, r.mx[:].unsqueeze(2).broadcast_to([P, XH, SEQ]),
                                  ALU.subtract).then_inc(xs_sub.sem, 1)

            def x_divide(j):
                r = at_room(j)
                dve.wait_ge(xs_pv.sem, xs_pv.at(j))
                o = r.X0[:, 0:XH * (XD + 1)].rearrange("p (h d) -> p h d", h=XH)
                dve.reciprocal(r.rc[:], o[:, :, XD]).then_inc(xs_rc.sem, 1)
                dve.wait_ge(xs_rc.sem, xs_rc.at(j))
                dve.tensor_tensor(r.o[:], o[:, :, 0:XD], r.rc[:].unsqueeze(2).broadcast_to([P, XH, XD]),
                                  ALU.mult).then_inc(xs_o.sem, 1)

            def x_end(j):
                r = at_room(j)
                dve.wait_ge(xs_b.sem, xs_b.at(j))
                dve.wait_ge(xs_pj.sem, xs_pj.at(j))
                dve.tensor_tensor(x2_s[:], r.X1[:, P:2 * P], x2_s[:], ALU.add).then_inc(xs_x2.sem, 1)
                dve.wait_ge(xs_x2.sem, xs_x2.at(j))
                dve.bn_stats(f_bn[:], x2_s[:]).then_inc(fs_bn.sem, 1)
                dve.wait_ge(fs_bn.sem, fs_bn.at(j))
                dve.tensor_scalar(x2_all[:, j, :], x2_s[:], 1.0, None, ALU.mult)
                dve.bn_aggr(f_mv[:], f_bn[:]).then_inc(fs_mv.sem, 1)

            def x_src(j):
                dve.wait_ge(fs_r.sem, fs_r.at(j))
                if not (isinstance(j, int) and j == 0):
                    dve.wait_ge(g_tp.sem, g_tp.at(j, 0))
                dve.tensor_scalar(src_s[:], x2_s[:], f_mv[:, 0:1], f_ve[:, 1:2],
                                  ALU.subtract, ALU.mult).then_inc(fs_src.sem, 1)
                dve.tensor_scalar(src_all[:, j, :], x2_s[:], f_mv[:, 0:1], f_ve[:, 1:2],
                                  ALU.subtract, ALU.mult).then_inc(fs_src.sem, 1)

            def f_low_part(i):
                dve.wait_ge(f_srcT.sem, f_srcT.at(i))
                dve.tensor_tensor(srcT_lo[:], srcT_next[:], srcT_hi[:].bitcast(F32), ALU.subtract).then_inc(f_low.sem, 1)

            def wide(t):
                return t.unsqueeze(2).broadcast_to([P, 2 * H, E])

            def g_top2(g, x):
                rank = rank_t.unsqueeze(1).broadcast_to([P, 2 * H, E])

                def larger_one():
                    dve.wait_ge(g_lg.sem, g_lg.at(g))
                    dve.tensor_scalar(lg_e[:], lg_e[:], 1.0, None, ALU.add).then_inc(g_sig.sem, 1)

                def inverse():
                    dve.wait_ge(g_sig.sem, g_sig.at(g, 1))
                    dve.reciprocal(sg[:], lg_e[:]).then_inc(g_sig.sem, 1)

                def waits(n):
                    dve.wait_ge(g_top.sem, g_top.at(g, n))

                def largest():
                    dve.wait_ge(g_sig.sem, g_sig.at(g))
                    dve.tensor_reduce(top[:, 0, :], sg[:], AX_X, ALU.max).then_inc(g_top.sem, 1)

                def equal(n, l, m):
                    waits(n - 1)
                    dve.tensor_tensor(eq[:], l[:], wide(m), ALU.is_equal).then_inc(g_top.sem, 1)

                def ranked(n):
                    waits(n - 1)
                    dve.tensor_tensor(eq[:], eq[:], rank, ALU.mult).then_inc(g_top.sem, 1)

                def best(n):
                    waits(n - 1)
                    dve.tensor_reduce(kk[:], eq[:], AX_X, ALU.max).then_inc(g_top.sem, 1)

                def chosen(n, oh):
                    waits(n - 1)
                    dve.tensor_tensor(oh[:], eq[:], wide(kk[:]), ALU.is_equal).then_inc(g_top.sem, 1)

                def without_first():
                    waits(5)
                    dve.scalar_tensor_tensor(out=l2[:], in0=oh1[:], scalar=-BIG, in1=sg[:], op0=ALU.mult,
                                             op1=ALU.add).then_inc(g_top.sem, 1)

                def second():
                    waits(6)
                    dve.tensor_reduce(top[:, 1, :], l2[:], AX_X, ALU.max).then_inc(g_top.sem, 1)

                return [larger_one, inverse, largest, lambda: equal(2, sg, top[:, 0, :]), lambda: ranked(3), lambda: best(4),
                        lambda: chosen(5, oh1), without_first, second, lambda: equal(8, l2, top[:, 1, :]),
                        lambda: ranked(9), lambda: best(10), lambda: chosen(11, oh2)]

            def f_rope(i, half):
                part = qk[:, H * half:H * half + H, 0:NROT]
                dve.wait_ge(f_qkev.sem, f_qkev.at(i, half + 1))
                for dst, table in ((rot_c, cos_t), (rot_s, sin_t)):
                    dve.tensor_tensor(dst[:, H * half:H * half + H, :], part,
                                      table.unsqueeze(1).broadcast_to([P, H, NROT]), ALU.mult).then_inc(f_rot.sem, 1)

            def f_split(i):
                go = gate[:, 1].rearrange("p (q h) e -> p q h e", q=QUADS)
                r = go_r[:].rearrange("p (q h) e -> p q h e", q=QUADS)
                part = [go3[:, :, :, s, :] for s in range(3)]
                dve.wait_ge(f_gate.sem, f_gate.at(i))
                dve.tensor_copy(part[0], go).then_inc(f_go.sem, 1)
                dve.wait_ge(f_go.sem, f_go.at(i, 1))
                dve.tensor_tensor(r, go, part[0], ALU.subtract).then_inc(f_go.sem, 1)
                dve.wait_ge(f_go.sem, f_go.at(i, 2))
                dve.tensor_copy(part[1], r).then_inc(f_go.sem, 1)
                dve.wait_ge(f_go.sem, f_go.at(i, 3))
                dve.tensor_tensor(part[2], r, part[1], ALU.subtract).then_inc(f_go.sem, 1)

            def f_gate_value(i, h):
                if h == 0:
                    dve.wait_ge(f_gate.sem, f_gate.at(i))
                dve.wait_ge(f_y.sem, f_y.at(i, h + 1))
                if h % 2 == 0 and (h >= 4 or not first(i)):
                    dve.wait_ge(f_es.sem, f_es.at(i, 3 * (h // 2 - 1)))
                dve.tensor_tensor(gy[:, h % 4], Y[h % 2].rearrange("p (e n) -> p e n", e=E),
                                  gate[:, 0, h, :].unsqueeze(2).broadcast_to([P, E, HD]), ALU.mult).then_inc(f_vg.sem, 1)

            def f_soft(i):
                dve.wait_ge(f_s.sem, f_s.at(i))
                s = A.rearrange("p (h s) -> p h s", h=H)
                dve.tensor_reduce(f_mx[:], s, AX_X, ALU.max).then_inc(f_m.sem, 1)
                dve.wait_ge(f_m.sem, f_m.at(i))
                dve.tensor_tensor(p_f[:], s, f_mx[:].unsqueeze(2).broadcast_to([P, H, SEQ]),
                                  ALU.subtract).then_inc(f_sub.sem, 1)

            def d_divide(i):
                dve.wait_ge(f_pv.sem, f_pv.at(i))
                wide_o = ps[:, 2:4, 0:7 * (HD + 1)].rearrange("p a (h d) -> p a h d", h=7)
                last_o = ps[:, 4, 0:2 * (HD + 1)].rearrange("p (h d) -> p h d", h=2)
                dve.reciprocal(f_rc[:, 0:14].rearrange("p (a h) -> p a h", a=2), wide_o[:, :, :, HD]).then_inc(f_rcs.sem, 1)
                dve.reciprocal(f_rc[:, 14:16], last_o[:, :, HD]).then_inc(f_rcs.sem, 1)
                dve.wait_ge(f_rcs.sem, f_rcs.at(i))
                dve.tensor_tensor(o_sb[:, 0:14, :].rearrange("p (a h) d -> p a h d", a=2), wide_o[:, :, :, 0:HD],
                                  f_rc[:, 0:14].rearrange("p (a h q) -> p a h q", a=2, q=1).broadcast_to([P, 2, 7, HD]),
                                  ALU.mult).then_inc(f_on.sem, 1)
                dve.tensor_tensor(o_sb[:, 14:16, :], last_o[:, :, 0:HD],
                                  f_rc[:, 14:16].unsqueeze(2).broadcast_to([P, 2, HD]), ALU.mult).then_inc(f_on.sem, 1)

            def tile(i, d, g, x):
                top2 = g_top2(g, x) if g is not None else []
                beside = {
                    0: [(lambda i: f_rope(i, 0), i)], 1: [(lambda i: f_rope(i, 1), i)], 2: [(f_split, i)],
                    3: [(d_divide, d)], 4: [(x_blocks, x)], 5: [(x_bias, x)], 6: [(x_soft, x)], 11: [(f_soft, i)], 13: [(x_divide, x)],
                }
                steps = {4: 1, 7: 1, 8: 3, 9: 3, 10: 3, 12: 2}
                f_low_part(i)
                if g is not None and not first(i):
                    x_end(g)
                if x is not None:
                    x_center(x)
                if g is not None:
                    x_src(g)
                for h in range(H):
                    f_gate_value(i, h)
                    for step, t in beside.get(h, ()):
                        if t is not None:
                            step(t)
                    for _ in range(steps.get(h, 0)):
                        if top2:
                            top2.pop(0)()
                assert not top2

            dve.wait_ge(loads["x"].sem, 16)
            dve.wait_ge(loads["ctx"].sem, 16)
            x_stats(0, HEAD_TILES)
            dve.wait_ge(loads["mask"].sem, 16)
            dve.tensor_scalar(keep_k[:], mask_k, 0.0, None, ALU.not_equal).then_inc(set_dve.sem, 1)
            dve.tensor_scalar(masked[:], mask_k[0:SPLITS], 0.0, None, ALU.is_equal).then_inc(set_dve.sem, 1)
            dve.wait_ge(xs_r.sem, xs_r.at(0))
            x_center(0)
            x_center(1)
            dve.wait_ge(loads["const"].sem, 32)
            dve.wait_ge(set_dve.sem, 2)
            dve.wait_ge(set_pool.sem, 1)
            x_blocks(0)
            x_blocks(1)
            x_stats(HEAD_TILES, TILES)
            dve.wait_ge(loads["vec"].sem, 16 * VEC_LOADS)
            x_bias(0)
            x_soft(0)
            x_soft(1)
            for k in range(4):
                dve.wait_ge(wv_rounded.sem, k + 1)
                dve.tensor_tensor(wv_lo[:, 2 * k:2 * k + 2, :], wv_raw[:, 2 * k:2 * k + 2, :],
                                  wv_hi[:, 2 * k:2 * k + 2, :].bitcast(F32), ALU.subtract).then_inc(wv_split_dve.sem, 1)
            x_divide(0)
            x_divide(1)
            x_end(0)
            x_src(0)
            x_bias(1)
            x_end(1)
            for step in g_top2(0, None):
                step()
            dve.wait_ge(xs_r.sem, xs_r.at(1))
            tile(0, None, 1, 2)
            with dve.Fori(1, TILES - 2) as i:
                tile(i, i - 1, i + 1, i + 2)
            tile(TILES - 2, TILES - 3, TILES - 1, None)
            tile(TILES - 1, TILES - 2, None, None)
            def tail_stats(hf, k, ready, bn, mv, done):
                dve.wait_ge(ready.sem, ready.at(hf))
                for t in range(HT):
                    dve.bn_stats(tail_bn[:, k, t, :], TA[:, P * t:P * t + P]).then_inc(bn.sem, 1)
                dve.wait_ge(bn.sem, bn.at(hf))
                dve.tensor_copy(z_t, TA.rearrange("p (t d) -> p t d", t=HT)).then_inc(done.sem, 1)
                for t in range(HT):
                    dve.bn_aggr(tail_mv[:, k, t, :], tail_bn[:, k, t, :]).then_inc(mv.sem, 1)

            def tail_center(hf, k, r, done):
                dve.wait_ge(done.sem, done.at(hf, 1))
                dve.wait_ge(r.sem, r.at(hf))
                for t in range(HT):
                    dve.tensor_scalar(z_t[:, t, :], z_t[:, t, :], tail_mv[:, k, t, 0:1],
                                      tail_ve[:, k, 1, t:t + 1], ALU.subtract, ALU.mult).then_inc(done.sem, 1)

            def tail_second(hf):
                dve.wait_ge(t_o.sem, t_o.at(hf))
                dve.scalar_tensor_tensor(out=z2T, in0=TA, scalar=COL["b2"], in1=y1T, op0=ALU.add,
                                         op1=ALU.add).then_inc(t_z2.sem, 1)

            def tail_gain(hf):
                dve.wait_ge(u_z.sem, u_z.at(hf))
                dve.tensor_tensor(z_t, z_t, rows[:, 1, :].unsqueeze(1).broadcast_to([P, HT, DIM]),
                                  ALU.mult).then_inc(u_g.sem, 1)

            def tail_bias(hf):
                dve.wait_ge(u_g.sem, u_g.at(hf))
                dve.tensor_tensor(z_t, z_t, rows[:, 2, :].unsqueeze(1).broadcast_to([P, HT, DIM]),
                                  ALU.add).then_inc(u_b.sem, 1)

            def tail_residual(hf):
                dve.wait_ge(u_b.sem, u_b.at(hf))
                dve.tensor_tensor(x_all[:, hf * HT:(hf + 1) * HT, :], z_t, x2_all[:, hf * HT:(hf + 1) * HT, :],
                                  ALU.add).then_inc(u_out.sem, 1)

            def tail(hf):
                return [lambda: tail_stats(hf, 0, t_rt, t_bn, t_mv, t_z), lambda: tail_center(hf, 0, t_r, t_z),
                        lambda: tail_second(hf), lambda: tail_stats(hf, 1, t_z2t, u_bn, u_mv, u_z),
                        lambda: tail_center(hf, 1, u_r, u_z), lambda: tail_gain(hf), lambda: tail_bias(hf),
                        lambda: tail_residual(hf)]

            def experts(hf, beside):
                for s in range(STEPS):
                    dve.wait_ge(p_bc.sem, p_bc.at(hf, s + 1))
                    if s >= 4:
                        dve.wait_ge(p_fin.sem, p_fin.at(hf, s - 3))
                    dve.tensor_tensor(g_ring[s % 4], BC[s % 3], oT_all[:, s // E, hf * HTOK:(hf + 1) * HTOK],
                                      ALU.mult).then_inc(p_gm.sem, 1)
                    if s in beside:
                        beside[s]()

            dve.tensor_copy(z2_t, src_all[:, 0:HT, :]).then_inc(p_res.sem, 1)
            dve.wait_ge(f_es.sem, f_es.at(TILES - 1))
            experts(0, {6: lambda: d_divide(TILES - 1)})
            dve.tensor_copy(z2_t, src_all[:, HT:2 * HT, :]).then_inc(p_res.sem, 1)
            experts(1, dict(zip((4, 10, 36, 44, 48, 51, 53, 55), tail(0))))
            for step in tail(1):
                step()

        @block.gpsimd
        def _(pool):
            def x_rstd(n, lo, hi):
                t = slice(lo, hi)
                var, ve, r = x_mv[:, :, t, 1], x_ve[:, :, t], x_r[:, :, t]
                width = hi - lo
                eps = eps_t[:, 0:2 * width].rearrange("p (a t) -> p a t", a=2)
                power = powers[:, 0:2 * width].rearrange("p (a t) -> p a t", a=2)
                pool.wait_ge(xs_mv.sem, 2 * hi)
                pool.tensor_tensor(ve, var, eps, ALU.add).then_inc(xs_r.sem, 1)
                for k, (dst, a, b, op) in enumerate((
                        (r, ve, power, ALU.pow), (ve[:, 0], var[:, 0], r[:, 0], ALU.mult),
                        (ve[:, 0], ve[:, 0], r[:, 0], ALU.mult), (ve[:, 0], ve[:, 0], eps[:, 0], ALU.add),
                        (ve[:, 0], ve[:, 0], power[:, 0], ALU.pow), (r[:, 0], ve[:, 0], r[:, 0], ALU.mult))):
                    pool.wait_ge(xs_r.sem, xs_r.at(n, k + 1))
                    pool.tensor_tensor(dst, a, b, op).then_inc(xs_r.sem, 1)

            def f_rstd(j):
                pool.wait_ge(fs_mv.sem, fs_mv.at(j))
                pool.tensor_tensor(f_ve[:, 0:1], f_mv[:, 1:2], eps_t[:, 0:1], ALU.add).then_inc(fs_r.sem, 1)
                pool.wait_ge(fs_r.sem, fs_r.at(j, 1))
                pool.tensor_tensor(f_ve[:, 1:2], f_ve[:, 0:1], powers[:, 0:1], ALU.pow).then_inc(fs_r.sem, 1)

            def g_gates(g):
                pool.wait_ge(g_top.sem, g_top.at(g))
                pool.tensor_tensor(oh1[:], oh1[:], oh2[:], ALU.add).then_inc(g_gate.sem, 1)
                pool.wait_ge(g_gate.sem, g_gate.at(g, 1))
                if not first(g):
                    pool.wait_ge(f_gate.sem, f_gate.at(g, 0))
                pool.tensor_tensor(gate_next[:].rearrange("p a h e -> p (a h) e"), oh1[:], sg[:],
                                   ALU.mult).then_inc(g_gate.sem, 1)

            def f_rot_add(i, half):
                h, a = HALF_ROT, slice(H * half, H * half + H)
                pool.wait_ge(f_rot.sem, f_rot.at(i, 2 * half + 2))
                pool.tensor_tensor(qk[:, a, 0:h], rot_c[:, a, 0:h], rot_s[:, a, h:2 * h], ALU.add).then_inc(f_ra.sem, 1)
                pool.tensor_tensor(qk[:, a, h:2 * h], rot_c[:, a, h:2 * h], rot_s[:, a, 0:h],
                                   ALU.add).then_inc(f_ra.sem, 1)

            def f_expert_sum(i, pair):
                g = gy[:, 2 * (pair % 2):2 * (pair % 2) + 2]
                pool.wait_ge(f_vg.sem, f_vg.at(i, 2 * pair + 2))
                pool.tensor_tensor(g[:, :, 0:4, :], g[:, :, 0:4, :], g[:, :, 4:8, :], ALU.add).then_inc(f_es.sem, 1)
                pool.wait_ge(f_es.sem, f_es.at(i, 3 * pair + 1))
                pool.tensor_tensor(g[:, :, 0:2, :], g[:, :, 0:2, :], g[:, :, 2:4, :], ALU.add).then_inc(f_es.sem, 1)
                pool.wait_ge(f_es.sem, f_es.at(i, 3 * pair + 2))
                if pair == 0 and not first(i):
                    pool.wait_ge(f_pv.sem, f_pv.at(i, 0))
                pool.tensor_tensor(v[:, 2 * pair:2 * pair + 2, 0:HD], g[:, :, 0, :], g[:, :, 1, :],
                                   ALU.add).then_inc(f_es.sem, 1)

            def tile(i, d, g, x):
                if g is not None:
                    f_rstd(g)
                f_rot_add(i, 0)
                f_rot_add(i, 1)
                for pair in range(H // 2):
                    if pair == 6 and g is not None:
                        g_gates(g)
                    f_expert_sum(i, pair)

            pool.memset(powers[:], -0.5)
            pool.memset(eps_t[:], EPS)
            pool.memset(x_v[:], 1.0)
            pool.memset(v[:], 1.0)
            pool.memset(x_att[:], 0.0)
            pool.memset(att[:], 0.0)
            pool.memset(q_bd[:], 0.0)
            pool.memset(go3[:], 0.0).then_inc(set_pool.sem, 1)
            pool.wait_ge(set_pool.sem, 1)
            x_rstd(0, 0, HEAD_TILES)
            x_rstd(1, HEAD_TILES, TILES)
            for k in range(4, 8):
                pool.wait_ge(wv_rounded.sem, k + 1)
                pool.tensor_tensor(wv_lo[:, 2 * k:2 * k + 2, :], wv_raw[:, 2 * k:2 * k + 2, :],
                                   wv_hi[:, 2 * k:2 * k + 2, :].bitcast(F32), ALU.subtract).then_inc(wv_split.sem, 1)
            f_rstd(0)
            g_gates(0)
            tile(0, None, 1, 2)
            with pool.Fori(1, TILES - 2) as i:
                tile(i, i - 1, i + 1, i + 2)
            tile(TILES - 2, TILES - 3, TILES - 1, None)
            tile(TILES - 1, TILES - 2, None, None)

            with pool.Fori(0, HALVES) as hf:
                for k, mv, r in ((0, t_mv, t_r), (1, u_mv, u_r)):
                    pool.wait_ge(mv.sem, mv.at(hf))
                    pool.tensor_tensor(tail_ve[:, k, 0, :], tail_mv[:, k, :, 1], eps_t[:, 0:HT],
                                       ALU.add).then_inc(r.sem, 1)
                    pool.wait_ge(r.sem, r.at(hf, 1))
                    pool.tensor_tensor(tail_ve[:, k, 1, :], tail_ve[:, k, 0, :], powers[:, 0:HT],
                                       ALU.pow).then_inc(r.sem, 1)


_INS = ["x", "ctx_1024", "mask_BxS2_ik0", "L0_xattn_w_q", "L0_xattn_w_kv", "L0_xattn_w_proj", "L0_xattn_b_proj",
        "L0_xattn_g_x", "L0_xattn_b_x", "L0_xattn_g_kv", "L0_xattn_b_kv", "L0_ffn_Wq", "L0_ffn_Wk", "L0_ffn_Wv",
        "L0_ffn_Wo", "L0_ffn_Wsel_v", "L0_ffn_Wsel_o", "L0_ffn_ln1_g", "L0_ffn_ln1_b", "L0_ffn_ln2_g",
        "L0_ffn_ln2_b", "L0_ffn_W1", "L0_ffn_b1", "L0_ffn_W2", "L0_ffn_b2"]


def kernel(**inputs):
    import concourse.bacc as bacc
    import ml_dtypes
    from concourse.bass_utils import run_bass_kernel_spmd

    nc = bacc.Bacc("TRN2", target_bir_lowering=False, num_devices=1)
    const, const_sel, const_fill = constants()
    data = {name: np.ascontiguousarray(inputs[name]) for name in _INS}
    data["const"] = const
    data["const_sel"] = const_sel.astype(ml_dtypes.bfloat16)
    data["const_fill"] = const_fill.astype(ml_dtypes.bfloat16)
    data["const_idb"] = np.eye(P).astype(ml_dtypes.bfloat16)
    arrays, args = {}, []
    for name, a in data.items():
        arrays[f"in_{name}"] = a
        args.append(nc.dram_tensor(f"in_{name}", a.shape, mybir.dt.from_np(a.dtype), kind="ExternalInput").ap())
    args.append(nc.dram_tensor("out_0", (BATCH, SEQ, DIM), F32, kind="ExternalOutput").ap())
    build(nc, *args)
    r = run_bass_kernel_spmd(nc, [arrays], core_ids=[0])
    return r.results[0]["out_0"]
```

```python
from contextlib import ExitStack

import numpy as np

import concourse.bass as bass
from concourse import mybir

F32 = mybir.dt.float32
F32R = mybir.dt.float32r
BF16 = mybir.dt.bfloat16
I32 = mybir.dt.int32
ALU = mybir.AluOpType
ACT = mybir.ActivationFunctionType
AX_X = mybir.AxisListType.X

P = 128
BATCH, SEQ, DIM = 16, 64, 128
TILES = BATCH * SEQ // P
XH, XD = 16, 8
H, HD, E = 16, 64, 8
HP = H // 2
NROT, HALF_ROT = 32, 16
FF = 512
HALVES, HTOK = 2, 512
HT = HTOK // P
QUARTERS, QTOK = 4, 256
QT = QTOK // P
QUADS = H // 4
SPLITS = 3
EPS = 1e-5
FILL = 1e9
BIG = 1e30

C_ID, C_BLK, C_COS, C_SIN, C_RANK, C_END = 0, 128, 132, 164, 196, 204


def constants():
    c = np.zeros((P, C_END), np.float32)
    c[:, C_ID:C_ID + P] = np.eye(P)
    own = np.arange(P)[:, None] // XD % 4 == np.arange(4)[None]
    c[:, C_BLK:C_BLK + 4] = own * np.float32(XD ** -0.5)
    inv = 10000.0 ** (-np.arange(HALF_ROT, dtype=np.float32) / HALF_ROT)
    angle = (np.arange(P) % SEQ).astype(np.float32)[:, None] * inv[None].astype(np.float32)
    cos, sin = np.cos(angle), np.sin(angle)
    c[:, C_COS:C_COS + NROT] = np.concatenate([cos, cos], 1)
    c[:, C_SIN:C_SIN + NROT] = np.concatenate([sin, -sin], 1)
    c[:, C_RANK:C_RANK + E] = E - np.arange(E)
    row = np.arange(P)
    sel = np.zeros((P, 2, E, P), np.float32)
    for pair in range(2):
        for e in range(E):
            for half in range(2):
                rows = (row // 32 == 2 * pair + half) & (row % 32 < 8 * SPLITS) & (row % 8 == e)
                sel[rows, pair, e, half * HD:(half + 1) * HD] = 1
    fill = np.full(1, -FILL, np.float32)
    parts = []
    for _ in range(SPLITS):
        part = (fill.view(np.uint32) & 0xFFFF0000).view(np.float32)
        parts.append(np.repeat(part, P))
        fill = fill - part
    assert not fill.any()
    return c, sel.reshape(P, 2 * E * P), np.stack(parts)


class Count:

    def __init__(self, sem, per, first=0):
        self.sem, self.per, self.first = sem, per, first

    def at(self, i, k=None):
        return i * self.per + (self.per if k is None else k) + self.first


class QuarterCount:

    def __init__(self, shared, last, per):
        self.shared, self.last, self.per = shared, last, per

    def of(self, n):
        return self.last if n == QUARTERS - 1 else self.shared

    def at(self, n, k=None):
        before = 0 if n == QUARTERS - 1 else n * self.per
        return self.of(n), before + (self.per if k is None else k)


class Room:

    def __init__(self, hat, nT, kT, v, qd, p, mx, att, rc, o, oT, X, X0, X1):
        self.hat, self.nT, self.kT, self.v, self.qd, self.p, self.mx = hat, nT, kT, v, qd, p, mx
        self.att, self.rc, self.o, self.oT, self.X, self.X0, self.X1 = att, rc, o, oT, X, X0, X1


def build(nc, x, ctx_in, mask, w_q, w_kv, w_proj, b_proj, g_x, b_x, g_kv, b_kv, Wq, Wk, Wv, Wo,
          Wsel_v, Wsel_o, ln1_g, ln1_b, ln2_g, ln2_b, W1, b1, W2, b2, const, const_sel, const_fill, const_idb, out):
    st = ExitStack()
    with st:
        def sb(name, shape, dt=F32):
            return st.enter_context(nc.sbuf_tensor(name, shape, dt))

        def sem(name, per=1, first=0):
            return Count(st.enter_context(nc.semaphore(name)), per, first)

        def quarter_sem(name, per=1):
            shared, last = (st.enter_context(nc.semaphore(name + end)) for end in ("", "_last"))
            return QuarterCount(shared, last, per)

        cst = sb("cst", [P, C_END])
        ident = cst[:, C_ID:C_ID + P]
        head_block = cst[:, C_BLK:C_BLK + 4]
        cos_t, sin_t = cst[:, C_COS:C_COS + NROT], cst[:, C_SIN:C_SIN + NROT]
        rank_t = cst[:, C_RANK:C_RANK + E]
        identb = sb("identb", [P, P], BF16)
        fill_row = sb("fill_row", [SPLITS, P], BF16)
        masked = sb("masked", [SPLITS, TILES, P], BF16)
        wq_sb = sb("wq_sb", [P, DIM])
        wkv_sb = sb("wkv_sb", [P, 2 * DIM])
        wproj_sb = sb("wproj_sb", [P, DIM])
        Wq_sb = sb("Wq_sb", [P, H, HD])
        Wk_sb = sb("Wk_sb", [P, H, HD])
        wsel_sb = sb("wsel_sb", [P, 2 * H * E])
        cols = sb("cols", [P, 16])
        COL = {n: cols[:, k:k + 1] for k, n in enumerate(
            ["g_x", "b_x", "g_kv", "b_kv", "ln1_g", "ln1_b", "b2"])}
        b1_sb = cols[:, 8:12]
        rows = sb("rows", [P, 3, DIM])
        powers = sb("powers", [P, 2 * TILES])
        warm_up = sb("warm_up", [P, 1])
        eps_t = sb("eps_t", [P, 2 * TILES])

        x_all = sb("x_all", [P, TILES, DIM])
        c_all = sb("c_all", [P, TILES, DIM])
        src_all, x2_all = c_all, x_all
        keep_k = sb("keep_k", [P, TILES, P], BF16)
        oT_all = sb("oT_all", [P, HP, TILES * P])
        wv_raw = oT_all[:, :, :].rearrange("p a (b n) -> p (a b) n", b=2)
        goT_all = sb("goT_all", [P, QUADS, TILES * P], BF16)

        x_bn = sb("x_bn", [P, 2, TILES, 6])
        x_mv = sb("x_mv", [P, 2, TILES, 2])
        x_ve = sb("x_ve", [P, 2, TILES])
        x_r = sb("x_r", [P, 2, TILES])
        x_hat = sb("x_hat", [P, 2, DIM])
        x_nT = sb("x_nT", [P, 2, P])
        x_kT = sb("x_kT", [P, P])
        x_v = sb("x_v", [P, XH, XD + 1])
        x_qd = sb("x_qd", [P, 2, 2, 2, SEQ])
        x_p = sb("x_p", [P, XH, SEQ])
        x_mx = sb("x_mx", [P, XH])
        x_att = sb("x_att", [P, XH, P])
        x_rc = sb("x_rc", [P, XH])
        x_o = sb("x_o", [P, XH, XD])
        x_oT = sb("x_oT", [P, P])
        f_bn = sb("f_bn", [P, 6])
        f_mv = sb("f_mv", [P, 2])
        f_ve = sb("f_ve", [P, 2])
        x2_s = sb("x2_s", [P, DIM])
        src_s = sb("src_s", [P, DIM])

        srcT_next = sb("srcT_next", [P, P])
        gate_next = sb("gate_next", [P, 2, H, E])
        srcT = sb("srcT", [P, P])
        srcT_hi = sb("srcT_hi", [P, P], F32R)
        srcT_lo = sb("srcT_lo", [P, P], F32R)
        sg = sb("sg", [P, 2 * H, E])
        lg_e = sb("lg_e", [P, 2 * H, E])
        top = sb("top", [P, 2, 2 * H])
        eq = sb("eq", [P, 2 * H, E])
        oh1 = sb("oh1", [P, 2 * H, E])
        oh2 = sb("oh2", [P, 2 * H, E])
        l2 = lg_e
        kk = sb("kk", [P, 2 * H])
        gate = sb("gate", [P, 2, H, E])
        go3 = sb("go3", [P, QUADS, 4, 4, E], BF16)
        go_r = sb("go_r", [P, H, E])
        q_bd = sb("q_bd", [P, HP, 2, 2, SEQ])
        f_mx = sb("f_mx", [P, H])
        att = sb("att", [P, H, P])
        v = sb("v", [P, H, HD + 1])
        gy = sb("gy", [P, 4, E, HD])
        f_rc = sb("f_rc", [P, H])
        tail_bn = sb("tail_bn", [P, 2, QUARTERS, QT, 6])
        tail_mv = sb("tail_mv", [P, 2, QUARTERS, QT, 2])
        tail_ve = sb("tail_ve", [P, 2, QUARTERS, 2, QT])

        with ExitStack() as phase_1:
            def sb_1(name, shape, dt=F32):
                return phase_1.enter_context(nc.sbuf_tensor(name, shape, dt))

            wv_hi = sb_1("wv_hi", [P, H, E * HD], F32R)
            wv_lo = sb_1("wv_lo", [P, H, E * HD], F32R)
            qk = sb_1("qk", [P, 2 * H, HD])
            kT = sb_1("kT", [P, HP, P])
            p_f = sb_1("p_f", [P, H, SEQ])
        with ExitStack() as arrival:
            big_w = arrival.enter_context(nc.sbuf_tensor("big_w", [P, H, E * HD], F32))
        wo_lo = sb("wo_lo", [P, H, E * HD], F32R)
        wo_hi = sb("wo_hi", [P, H, E * HD], F32R)
        g_hi = sb("g_hi", [P, 4, HTOK], F32R)
        g_lo = sb("g_lo", [P, 4, HTOK], F32R)

        rot_c = kT[:].rearrange("p k t -> p (k t)").rearrange("p (h n) -> p h n", n=NROT)
        rot_s = p_f[:].rearrange("p h s -> p (h s)").rearrange("p (h n) -> p h n", n=NROT)
        o_sb = x_p
        gy_flat = gy[:].rearrange("p k e n -> p (k e n)")
        mask_k = gy_flat[:, 0:TILES * P].bitcast(I32).rearrange("p (t s) -> p t s", t=TILES)
        wsel_raw = gy_flat[:, TILES * P:TILES * P + 2 * DIM].rearrange("p (a d) -> p a d", a=2)
        sel = x_att[:, 0:8, :].rearrange("p h s -> p (h s)").bitcast(BF16).rearrange("p (a m) -> p a m", m=P)
        W1_sb = x_att[:, 8:12, :].rearrange("p h s -> p (h s)")
        W2_sb = x_att[:, 12:16, :]

        ps = st.enter_context(nc.psum_tensor("ps", [P, 8, 512], F32))
        Y = [ps[:, 0, :], ps[:, 1, :]]
        A = ps[:, 2:4, :].rearrange("p a b -> p (a b)")
        T = ps[:, 4:6, :].rearrange("p a b -> p (a b)")
        X = ps[:, 6:8, :].rearrange("p a b -> p (a b)")
        X0, X1 = ps[:, 6, :], ps[:, 7, :]

        room = Room(hat=x_hat, nT=x_nT, kT=x_kT, v=x_v, qd=x_qd, p=x_p, mx=x_mx, att=x_att, rc=x_rc,
                    o=x_o, oT=x_oT, X=X, X0=X0, X1=X1)
        spare = qk[:].rearrange("p h n -> p (h n)")
        beside_room = Room(
            hat=spare[:, 0:2 * P].rearrange("p (a d) -> p a d", a=2),
            nT=spare[:, 2 * P:4 * P].rearrange("p (a d) -> p a d", a=2),
            kT=spare[:, 4 * P:5 * P], oT=kT[:, 0, :], o=kT[:, 1, :].rearrange("p (h d) -> p h d", d=XD),
            qd=spare[:, 8 * P:12 * P].rearrange("p (b a h s) -> p b a h s", b=2, a=2, h=2),
            v=v[:, :, HD - XD:HD + 1], p=p_f, mx=f_mx, att=att, rc=f_rc,
            X=ps[:, 0:2, :].rearrange("p a b -> p (a b)"), X0=ps[:, 0, :], X1=ps[:, 1, :])

        def at_room(j):
            return beside_room if isinstance(j, int) and j == 1 else room

        loads = {n: sem("ld_" + n) for n in
                 ["const", "sel", "x", "ctx", "mask", "vec", "xw", "qk", "wsel", "ff", "idb"]}
        ld_wv = [sem(f"ld_wv{k}") for k in range(4)]
        ld_wo = [sem(f"ld_wo{k}") for k in range(4)]
        wv_rounded, wv_split, wv_split_dve = sem("wv_rounded"), sem("wv_split"), sem("wv_split_dve")
        ready_w, set_dve, set_pool, set_t = sem("ready_w"), sem("set_dve"), sem("set_pool"), sem("set_t")
        HEAD_TILES = 2
        xs_bn, xs_mv, xs_r, xs_hat = sem("xs_bn"), sem("xs_mv"), sem("xs_r", 7), sem("xs_hat", 2)
        xs_tp, xs_n, xs_proj = sem("xs_tp"), sem("xs_n", 2), sem("xs_proj")
        xs_qk, xs_sa, xs_s = sem("xs_qk", 3), sem("xs_sa", 2), sem("xs_s")
        xs_mx, xs_sub, xs_e, xs_pt = sem("xs_mx"), sem("xs_sub"), sem("xs_e"), sem("xs_pt")
        xs_att, xs_pv, xs_rc, xs_o = sem("xs_att", 2), sem("xs_pv"), sem("xs_rc"), sem("xs_o")
        xs_ot, xs_otc, xs_pj, xs_x2 = sem("xs_ot"), sem("xs_otc"), sem("xs_pj"), sem("xs_x2")
        xs_b = sem("xs_b")
        fs_bn, fs_mv, fs_r, fs_src = sem("fs_bn"), sem("fs_mv"), sem("fs_r", 2), sem("fs_src", 2)
        g_tp, g_srcT, g_g, g_lg, g_top = sem("g_tp"), sem("g_srcT"), sem("g_g"), sem("g_lg"), sem("g_top", 11)
        g_sig, g_gate = sem("g_sig", 2), sem("g_gate", 2)
        f_srcT, f_gate, f_q, f_k, f_qkev = sem("f_srcT", 2), sem("f_gate"), sem("f_q"), sem("f_k"), sem("f_qkev", 2)
        f_low = sem("f_low")
        f_go, f_gt, f_got, f_rot, f_ra = sem("f_go", 4), sem("f_gt"), sem("f_got"), sem("f_rot", 4), sem("f_ra", 4)
        f_qt, f_kt, f_qb, f_kb = sem("f_qt"), sem("f_kt"), sem("f_qb", 2), sem("f_kb")
        f_s, f_m, f_sub, f_e = sem("f_s"), sem("f_m"), sem("f_sub"), sem("f_e")
        f_pt, f_att, f_pv, f_rcs = sem("f_pt"), sem("f_att", 2), sem("f_pv"), sem("f_rcs", 2)
        f_on, f_ot, f_otev = sem("f_on", 2), sem("f_ot"), sem("f_otev")
        f_y, f_vg, f_es = sem("f_y", H), sem("f_vg", H), sem("f_es", 3 * H // 2)
        STEPS = HP * E
        VEC_LOADS, FF_LOADS = 5, 11
        p_res, p_bc, p_gm, p_fin = sem("p_res"), sem("p_bc", STEPS), sem("p_gm", STEPS), sem("p_fin", STEPS)
        wo_rounded, wo_split, p_hi = sem("wo_rounded"), sem("wo_split"), sem("p_hi", STEPS)
        WO_PIECES = H // 2
        TAIL_SHIFT = 31
        AHEAD = 4

        def early_tails(s, at, tail):
            for n in range(2):
                if s - TAIL_SHIFT * n in at:
                    tail(n, at.index(s - TAIL_SHIFT * n))

        def late_tails(steps, tail):
            for k in range(steps):
                tail(QUARTERS - 2, k)
                tail(QUARTERS - 1, k)

        def on_dve(s):
            return s % 10 in (0, 3, 6)

        def lows(s, dve):
            return sum(on_dve(t) == dve for t in range(s + 1))

        p_lo = {dve: sem("p_lo_dve" if dve else "p_lo_pool", lows(STEPS - 1, dve)) for dve in (True, False)}

        def wait_low(engine, hf, s):
            done = p_lo[on_dve(s)]
            engine.wait_ge(done.sem, done.at(hf, lows(s, on_dve(s))))

        t_acc, t_rt, t_bn, t_mv = [quarter_sem(*a) for a in (("t_acc",), ("t_rt",), ("t_bn", QT), ("t_mv", QT))]
        t_r, t_z, t_zt, t_y1 = [quarter_sem(*a) for a in (("t_r", 2), ("t_z", QT), ("t_zt",), ("t_y1",))]
        t_h, t_relu, t_o = [quarter_sem(*a) for a in (("t_h", 4), ("t_relu", 4), ("t_o",))]
        t_z2, t_z2t, u_bn = [quarter_sem(*a) for a in (("t_z2",), ("t_z2t",), ("u_bn", QT))]
        u_mv, u_r, u_g = [quarter_sem(*a) for a in (("u_mv", QT), ("u_r", 2), ("u_g", QT))]
        u_out, u_st, u_x2 = quarter_sem("u_out", QT), quarter_sem("u_st", 16), sem("u_x2")
        block = st.enter_context(nc.Block())

        def first(i):
            return isinstance(i, int) and i == 0

        x_tok = x.rearrange("(t b) s d -> (b s) t d", b=2)
        ctx_tok = ctx_in.rearrange("(t b) s d -> (b s) t d", b=2)
        out_tok = out.rearrange("(t b) s d -> (b s) t d", b=2)
        wv_cols = Wv.rearrange("h e d p -> d h e p")
        wo_part = [w[:, :, :].rearrange("p (a b) n -> p a (b n)", b=2).rearrange("p a (e n) -> p a e n", e=E)
                   for w in (wo_hi, wo_lo)]
        wo_view = big_w[:, :, :].rearrange("p (a b) n -> p a (b n)", b=2).rearrange("p a (e n) -> p a e n", e=E)
        wv_view = wv_raw.rearrange("p h (e n) -> p h e n", e=E)

        g_ring = [gy[:, k, :, :].rearrange("p e n -> p (e n)") for k in range(4)]
        acc = [ps[:, 0, :], ps[:, 5, :]]
        BC = [ps[:, 1, :], ps[:, 6, :], ps[:, 7, :]]

        def tail_banks(n):
            a, h0, h1 = (1, 6, 7) if n == QUARTERS - 1 else (4, 2, 3)
            return ps[:, a, 0:QTOK], [ps[:, h0, 0:QTOK], ps[:, h1, 0:QTOK]]

        def columns(n):
            return slice(n % 2 * QTOK, (n % 2 + 1) * QTOK)

        att_flat, bd_flat = att[:, :, :].rearrange("p h s -> p (h s)"), q_bd[:].rearrange("p a b c s -> p (a b c s)")
        r1T, y1T, z2T = att_flat[:, 0:HTOK], att_flat[:, HTOK:2 * HTOK], att_flat[:, 2 * HTOK:3 * HTOK]
        hT = bd_flat.rearrange("p (k t) -> p k t", k=4)
        z_t = x_p[:, 0:8, :].rearrange("p h s -> p (h s)")
        z2_t = x_qd[:].rearrange("p b a h s -> p (b a h s)").rearrange("p (t d) -> p t d", t=HT)

        @block.sync
        def _(sp):
            sp.dma_start(x_all[:], x_tok).then_inc(loads["x"].sem, 16)
            sp.dma_start(c_all[:], ctx_tok).then_inc(loads["ctx"].sem, 16)
            def column(name, a, load):
                sp.dma_start(COL[name], a.rearrange("(p o) -> p o", o=1)).then_inc(loads[load].sem, 16)

            def row(k, a, load):
                sp.dma_start(rows[:, k, :], a.rearrange("(o d) -> o d", o=1).broadcast_to([P, DIM])).then_inc(
                    loads[load].sem, 16)

            sp.dma_start(cst[:], const).then_inc(loads["const"].sem, 16)
            for name, a in [("g_x", g_x), ("b_x", b_x), ("g_kv", g_kv), ("b_kv", b_kv)]:
                column(name, a, "vec")
            for dst, a in [(wq_sb, w_q), (wkv_sb, w_kv), (wproj_sb, w_proj)]:
                sp.dma_start(dst[:], a).then_inc(loads["xw"].sem, 16)
            m_row = mask.rearrange("(o t b) s -> o t (b s)", o=1, b=2)
            sp.dma_start(mask_k, m_row.broadcast_to([P, TILES, P])).then_inc(loads["mask"].sem, 16)
            sp.dma_start(fill_row[:], const_fill).then_inc(loads["const"].sem, 16)
            row(0, b_proj, "vec")
            sp.dma_start(wsel_raw[:, 0, :], Wsel_v.rearrange("h e d -> (h e) d")).then_inc(loads["wsel"].sem, 16)
            sp.dma_start(wsel_raw[:, 1, :], Wsel_o.rearrange("h e d -> (h e) d")).then_inc(loads["wsel"].sem, 16)
            sp.dma_start(Wq_sb[:], Wq.rearrange("h d p -> d h p")).then_inc(loads["qk"].sem, 16)
            sp.dma_start(Wk_sb[:], Wk.rearrange("h d p -> d h p")).then_inc(loads["qk"].sem, 16)
            for k in range(4):
                for h in range(4 * k, 4 * k + 4):
                    sp.dma_start(wv_view[:, h], wv_cols[:, h]).then_inc(ld_wv[k].sem, 16)
            sp.dma_start(identb[:], const_idb).then_inc(loads["idb"].sem, 16)
            for name, a in [("ln1_g", ln1_g), ("ln1_b", ln1_b), ("b2", b2)]:
                column(name, a, "ff")
            for k in range(4):
                sp.dma_start(b1_sb[:, k:k + 1], b1[P * k:P * k + P].rearrange("(p o) -> p o", o=1)).then_inc(
                    loads["ff"].sem, 16)
            row(1, ln2_g, "ff")
            row(2, ln2_b, "ff")
            sp.wait_ge(xs_pv.sem, xs_pv.at(TILES - 1))
            sp.dma_start(sel, const_sel.rearrange("p (a m) -> p a m", m=P)).then_inc(loads["sel"].sem, 16)
            sp.dma_start(W1_sb, W1).then_inc(loads["ff"].sem, 16)
            sp.dma_start(W2_sb, W2.rearrange("(k p) n -> p k n", p=P)).then_inc(loads["ff"].sem, 16)
            for k in range(4):
                sp.wait_ge(f_y.sem, f_y.at(TILES - 1, 4 * k + 4))
                for hp in (2 * k, 2 * k + 1):
                    for b in range(2):
                        sp.dma_start(wo_view[64 * b:64 * b + 64, hp],
                                     Wo[2 * hp + b].rearrange("e p n -> p e n")).then_inc(ld_wo[k].sem, 16)
            for n in range(QUARTERS):
                sp.wait_ge(*u_out.at(n))
                tiles = slice(n * QT, (n + 1) * QT)
                sp.dma_start(out_tok[:, tiles, :], x_all[:, tiles, :]).then_inc(u_st.of(n), 16)
            sp.wait_ge(*u_st.at(QUARTERS - 2))
            sp.wait_ge(*u_st.at(QUARTERS - 1))

        @block.tensor
        def _(pe):
            def x_transpose(j):
                r = at_room(j)
                pe.wait_ge(xs_hat.sem, xs_hat.at(j))
                pe.transpose(r.X0[:, 0:P], r.hat[:, 0, :], ident)
                pe.transpose(r.X0[:, P:2 * P], r.hat[:, 1, :], ident).then_inc(xs_tp.sem, 1)

            def x_project(j):
                r = at_room(j)
                pe.wait_ge(xs_n.sem, xs_n.at(j))
                pe.matmul(r.X0[:, 2 * P:3 * P], wq_sb[:], r.nT[:, 0, :], start=True, stop=True)
                pe.matmul(r.X0[:, 0:P], r.nT[:, 1, :], wkv_sb[:, DIM:], start=True, stop=True)
                pe.matmul(r.X0[:, 3 * P:4 * P], wkv_sb[:, 0:DIM], r.nT[:, 1, :],
                          start=True, stop=True).then_inc(xs_proj.sem, 1)

            def x_scores(j, half):
                r = at_room(j)
                def fill(c):
                    return pe.matmul(r.X[:, 512 * c:512 * c + 512], fill_row[:],
                                     masked[:, j, :].unsqueeze(1).broadcast_to([SPLITS, 4, P]), start=True,
                                     stop=False, skip_group_check=True)

                def four_heads(g):
                    for k in range(4):
                        pair, b = k // 2, k % 2
                        at = SEQ * (2 * (2 * g + pair) + b)
                        mm = pe.matmul(r.X[:, at:at + SEQ],
                                       r.qd[32 * g:32 * g + 32, b, pair].rearrange("p h s -> p (h s)"),
                                       r.kT[32 * g:32 * g + 32, SEQ * b:SEQ * b + SEQ], start=False,
                                       stop=(g % 2 == 1 and k == 3), skip_group_check=True)
                    return mm

                if half == 0:
                    pe.wait_ge(xs_qk.sem, xs_qk.at(j))
                    if not (isinstance(j, int) and j < 2):
                        pe.wait_ge(f_got.sem, f_got.at(j - 2))
                    fill(1).then_inc(xs_sa.sem, 1)
                    fill(0)
                    four_heads(0)
                    pe.wait_ge(xs_sa.sem, xs_sa.at(j, 1))
                    four_heads(2).then_inc(xs_sa.sem, 1)
                else:
                    pe.wait_ge(xs_sa.sem, xs_sa.at(j, 2))
                    four_heads(1)
                    four_heads(3).then_inc(xs_s.sem, 1)

            def x_ptrans(j):
                r = at_room(j)
                pe.wait_ge(xs_e.sem, xs_e.at(j))
                for k in range(8):
                    mm = pe.transpose(r.X[:, P * k:P * k + P], r.p[:, 2 * k:2 * k + 2, :].rearrange(
                        "p h s -> p (h s)"), ident)
                mm.then_inc(xs_pt.sem, 1)

            def x_values(j, half):
                r = at_room(j)
                if half == 0:
                    pe.wait_ge(xs_att.sem, xs_att.at(j))
                for h in range(XH // 2 * half, XH // 2 * (half + 1)):
                    mm = pe.matmul(r.X0[:, (XD + 1) * h:(XD + 1) * (h + 1)], r.att[:, h, :], r.v[:, h, :],
                                   start=True, stop=True)
                if half == 1:
                    mm.then_inc(xs_pv.sem, 1)

            def x_otrans(j):
                r = at_room(j)
                pe.wait_ge(xs_o.sem, xs_o.at(j))
                pe.transpose(r.X1[:, 0:P], r.o[:, :, :].rearrange("p h d -> p (h d)"), ident).then_inc(xs_ot.sem, 1)

            def x_out(j):
                r = at_room(j)
                pe.wait_ge(xs_otc.sem, xs_otc.at(j))
                pe.matmul(r.X1[:, P:2 * P], r.oT[:], wproj_sb[:], start=True, stop=True).then_inc(xs_pj.sem, 1)

            def g_transpose(g):
                pe.wait_ge(fs_src.sem, fs_src.at(g))
                pe.transpose(X1[:, 3 * P:4 * P], src_s[:], ident).then_inc(g_tp.sem, 1)

            def g_logits(g):
                pe.wait_ge(g_srcT.sem, g_srcT.at(g))
                pe.matmul(X1[:, P:3 * P], srcT_next[:], wsel_sb[:], start=True, stop=True).then_inc(g_g.sem, 1)

            def f_project(i):
                pe.wait_ge(f_srcT.sem, f_srcT.at(i, 1))
                if not first(i):
                    pe.wait_ge(f_att.sem, f_att.at(i, 0))
                    pe.wait_ge(f_sub.sem, f_sub.at(i, 0))
                for w, dst, done in ((Wq_sb, T, f_q), (Wk_sb, A, f_k)):
                    for c in range(2):
                        mm = pe.matmul(dst[:, 512 * c:512 * c + 512], srcT[:],
                                       w[:, 8 * c:8 * c + 8, :].rearrange("p h s -> p (h s)"),
                                       start=True, stop=True)
                    mm.then_inc(done.sem, 1)

            def f_value(i, h):
                if h < 2 and not first(i):
                    pe.wait_ge(f_vg.sem, f_vg.at(i, h - 1))
                if h >= 2:
                    pe.wait_ge(f_vg.sem, f_vg.at(i, h - 1))
                if h == 0:
                    pe.wait_ge(f_low.sem, f_low.at(i))
                    if first(i):
                        pe.wait_ge(xs_x2.sem, xs_x2.at(1))
                        pe.wait_ge(wv_split.sem, 3)
                        pe.wait_ge(wv_split_dve.sem, 5)
                pe.matmul(Y[h % 2], srcT_hi[:], wv_hi[:, h, :], start=True, stop=False)
                pe.matmul(Y[h % 2], srcT_hi[:], wv_lo[:, h, :], start=False, stop=False)
                pe.matmul(Y[h % 2], srcT_lo[:], wv_hi[:, h, :], start=False, stop=True).then_inc(f_y.sem, 1)

            def f_turn(i, half, dst, done):
                pe.wait_ge(f_ra.sem, f_ra.at(i, 2 * half + 2))
                for k in range(8):
                    mm = pe.transpose(dst[:, P * k:P * k + P],
                                      qk[:, H * half + 2 * k:H * half + 2 * k + 2, :].rearrange(
                                          "p h s -> p (h s)"), ident)
                mm.then_inc(done.sem, 1)

            def f_qtrans(i):
                if not first(i):
                    pe.wait_ge(f_on.sem, f_on.at(i, 0))
                f_turn(i, 0, A, f_qt)

            def f_ktrans(i):
                if not first(i):
                    pe.wait_ge(f_otev.sem, f_otev.at(i, 0))
                f_turn(i, 1, T, f_kt)

            def f_scores(i, half):
                if half == 0:
                    pe.wait_ge(f_qb.sem, f_qb.at(i))
                    pe.wait_ge(f_kb.sem, f_kb.at(i))
                for k in range(HP // 2 * half, HP // 2 * (half + 1)):
                    for b in range(2):
                        at = SEQ * (2 * k + b)
                        mm = pe.matmul(A[:, at:at + SEQ], q_bd[:, k, b].rearrange("p h s -> p (h s)"),
                                       kT[:, k, SEQ * b:SEQ * b + SEQ], start=True, stop=True)
                if half == 1:
                    mm.then_inc(f_s.sem, 1)

            def f_ptrans(i):
                pe.wait_ge(f_e.sem, f_e.at(i))
                for k in range(8):
                    mm = pe.transpose(T[:, P * k:P * k + P], p_f[:, 2 * k:2 * k + 2, :].rearrange(
                        "p h s -> p (h s)"), ident)
                mm.then_inc(f_pt.sem, 1)

            def f_gtrans(i):
                pe.wait_ge(f_go.sem, f_go.at(i))
                if not (isinstance(i, int) and i == TILES - 1):
                    pe.wait_ge(g_lg.sem, g_lg.at(i + 1))
                x1 = X1.bitcast(BF16)
                for q in range(QUADS):
                    mm = pe.transpose(x1[:, P * (q + 2):P * (q + 3)],
                                      go3[:, q].rearrange("p h s e -> p (h s e)"), identb[:])
                mm.then_inc(f_gt.sem, 1)

            def d_values(i, half):
                if half == 0:
                    pe.wait_ge(f_att.sem, f_att.at(i))
                    pe.wait_ge(f_es.sem, f_es.at(i))
                    if not (isinstance(i, int) and i == TILES - 1):
                        pe.wait_ge(f_qkev.sem, f_qkev.at(i + 1))
                for h in range(H // 2 * half, H // 2 * (half + 1)):
                    mm = pe.matmul(ps[:, 2 + h // 7, (HD + 1) * (h % 7):(HD + 1) * (h % 7 + 1)],
                                   att[:, h, :], v[:, h, :], start=True, stop=True)
                if half == 1:
                    mm.then_inc(f_pv.sem, 1)

            def d_otrans(i):
                pe.wait_ge(f_on.sem, f_on.at(i))
                for k in range(HP):
                    mm = pe.transpose(T[:, P * k:P * k + P],
                                      o_sb[:, 2 * k:2 * k + 2, :].rearrange("p h s -> p (h s)"), ident)
                mm.then_inc(f_ot.sem, 1)

            def tile(i, d, g, x):
                if not first(i):
                    f_project(i)
                f_value(i, 0)
                if x is not None:
                    x_transpose(x)
                f_value(i, 1)
                if d is not None:
                    d_values(d, 0)
                f_value(i, 2)
                if d is not None:
                    d_values(d, 1)
                if g is not None:
                    g_transpose(g)
                f_value(i, 3)
                if g is not None:
                    g_logits(g)
                f_value(i, 4)
                if x is not None:
                    x_project(x)
                f_gtrans(i)
                f_value(i, 5)
                if d is not None:
                    d_otrans(d)
                if x is not None:
                    x_scores(x, 0)
                f_value(i, 6)
                f_value(i, 7)
                if x is not None:
                    x_scores(x, 1)
                f_qtrans(i)
                f_ktrans(i)
                f_value(i, 8)
                f_value(i, 9)
                f_value(i, 10)
                if x is not None:
                    x_ptrans(x)
                f_scores(i, 0)
                f_scores(i, 1)
                f_value(i, 11)
                if x is not None:
                    x_values(x, 0)
                f_value(i, 12)
                f_value(i, 13)
                if x is not None:
                    x_values(x, 1)
                f_ptrans(i)
                f_value(i, 14)
                f_value(i, 15)
                if x is not None:
                    x_otrans(x)
                    x_out(x)

            pe.wait_ge(loads["const"].sem, 32)
            pe.wait_ge(loads["xw"].sem, 48)

            x_transpose(0)
            x_transpose(1)
            x_project(0)
            x_project(1)
            x_scores(0, 0)
            x_scores(0, 1)
            x_scores(1, 0)
            x_ptrans(0)
            x_scores(1, 1)
            x_values(0, 0)
            x_values(0, 1)
            x_otrans(0)
            x_ptrans(1)
            x_out(0)
            pe.wait_ge(loads["wsel"].sem, 32)
            pe.transpose(T[:, 0:P], wsel_raw[:, 0, :], ident)
            pe.transpose(T[:, P:2 * P], wsel_raw[:, 1, :], ident).then_inc(set_t.sem, 1)
            g_transpose(0)
            pe.wait_ge(ready_w.sem, 1)
            g_logits(0)
            pe.wait_ge(loads["qk"].sem, 32)
            f_project(0)
            x_values(1, 0)
            x_values(1, 1)
            x_otrans(1)
            x_out(1)
            pe.wait_ge(loads["idb"].sem, 16)
            tile(0, None, 1, 2)
            with pe.Fori(1, TILES - 2) as i:
                tile(i, i - 1, i + 1, i + 2)
            tile(TILES - 2, TILES - 3, TILES - 1, None)
            tile(TILES - 1, TILES - 2, None, None)
            def spread(hf, s):
                if s >= 3:
                    pe.wait_ge(p_gm.sem, p_gm.at(hf, s - 2))
                pe.matmul(BC[s % 3], sel[:, s % 16, :], goT_all[:, s // 16, hf * HTOK:(hf + 1) * HTOK],
                          start=True, stop=True).then_inc(p_bc.sem, 1)

            def experts(hf, beside):
                pe.wait_ge(p_res.sem, p_res.at(hf))
                for t in range(HT):
                    pe.matmul(acc[hf][:, P * t:P * t + P], z2_t[:, t, :], ident, start=(t == 0), stop=False,
                              skip_group_check=True)
                for s in range(AHEAD):
                    spread(hf, s)
                for s in range(STEPS):
                    if s + AHEAD < STEPS:
                        spread(hf, s + AHEAD)
                    if hf == 0 and s % (STEPS // WO_PIECES) == 0:
                        pe.wait_ge(wo_split.sem, s // (STEPS // WO_PIECES) + 1)
                    hi, lo = [w[:, s // E, s % E, :] for w in wo_part]
                    pe.wait_ge(p_hi.sem, p_hi.at(hf, s + 1))
                    pe.matmul(acc[hf], lo, g_hi[:, s % 4, :], start=False, stop=False, skip_group_check=True)
                    pe.matmul(acc[hf], hi, g_hi[:, s % 4, :], start=False, stop=False, skip_group_check=True)
                    wait_low(pe, hf, s)
                    pe.matmul(acc[hf], hi, g_lo[:, s % 4, :], start=False, stop=(s == STEPS - 1),
                              skip_group_check=True).then_inc(p_fin.sem, 1)
                    beside(s)

            def turn_back(src, ready, n, done):
                pe.wait_ge(*ready.at(n))
                for t in range(QT):
                    mm = pe.transpose(tail_banks(n)[0][:, P * t:P * t + P], src[:, P * t:P * t + P], ident)
                mm.then_inc(done.of(n), 1)

            def tail_rows(n):
                if n > 0:
                    pe.wait_ge(*u_g.at(n - 1 if n < QUARTERS - 1 else n - 2))
                turn_back(r1T[:, columns(n)], t_acc, n, t_rt)

            def tail_columns(n):
                turn_back(z_t[:, columns(n)], t_z, n, t_zt)

            def tail_last(n):
                turn_back(z2T[:, columns(n)], t_z2, n, t_z2t)

            def tail_hidden(n, k):
                if k == 0:
                    pe.wait_ge(*t_y1.at(n))
                if k >= 2:
                    pe.wait_ge(*t_relu.at(n, k - 1))
                pe.matmul(tail_banks(n)[1][k % 2], W1_sb[:, P * k:P * k + P], y1T[:, columns(n)], start=True,
                          stop=True).then_inc(t_h.of(n), 1)

            def tail_second(n, k):
                pe.wait_ge(*t_relu.at(n, k + 1))
                mm = pe.matmul(tail_banks(n)[0], W2_sb[:, k, :], hT[:, k, columns(n)], start=(k == 0), stop=(k == 3))
                if k == 3:
                    mm.then_inc(t_o.of(n), 1)

            def tail(n, k):
                if k == 0:
                    tail_rows(n)
                elif k == 1:
                    tail_columns(n)
                elif k < 6:
                    tail_hidden(n, k - 2)
                elif k < 10:
                    tail_second(n, k - 6)
                else:
                    tail_last(n)

            def first_half(s):
                if s == 0:
                    d_values(last, 0)
                if s == 1:
                    d_values(last, 1)
                if s == 7:
                    d_otrans(last)

            last = TILES - 1
            pe.wait_ge(f_got.sem, f_got.at(last))
            pe.wait_ge(loads["sel"].sem, 16)
            experts(0, first_half)
            pe.wait_ge(loads["ff"].sem, 16 * FF_LOADS)
            pe.wait_ge(f_otev.sem, f_otev.at(last))
            experts(1, lambda s: early_tails(s, (1, 7, 14, 15, 16, 17, 18, 19, 20, 21, 24), tail))
            late_tails(11, tail)

        @block.scalar
        def _(act):
            def on_diagonal(src, dst, done):
                for b in range(2):
                    act.activation(dst[64 * b:64 * b + 64, :, 64 * b:64 * b + 64],
                                   src[64 * b:64 * b + 64, :].rearrange("p (h s) -> p h s", s=SEQ),
                                   ACT.Copy).then_inc(done.sem, 1)

            def x_norm(j):
                r = at_room(j)
                act.wait_ge(xs_tp.sem, xs_tp.at(j))
                act.activation(r.nT[:, 0, :], r.X0[:, 0:P], ACT.Identity, bias=COL["b_x"],
                               scale=COL["g_x"]).then_inc(xs_n.sem, 1)
                act.activation(r.nT[:, 1, :], r.X0[:, P:2 * P], ACT.Identity, bias=COL["b_kv"],
                               scale=COL["g_kv"]).then_inc(xs_n.sem, 1)

            def x_exp(j):
                r = at_room(j)
                act.wait_ge(xs_sub.sem, xs_sub.at(j))
                act.activation(r.p[:], r.p[:], ACT.Exp).then_inc(xs_e.sem, 1)

            def x_att_copy(j):
                r = at_room(j)
                act.wait_ge(xs_pt.sem, xs_pt.at(j))
                on_diagonal(r.X, r.att, xs_att)

            def x_ot_copy(j):
                r = at_room(j)
                act.wait_ge(xs_ot.sem, xs_ot.at(j))
                act.activation(r.oT[:], r.X1[:, 0:P], ACT.Copy).then_inc(xs_otc.sem, 1)

            def g_src(g):
                if not first(g):
                    act.wait_ge(f_low.sem, f_low.at(g, 0))
                act.wait_ge(g_tp.sem, g_tp.at(g))
                act.activation(srcT_next[:], X1[:, 3 * P:4 * P], ACT.Copy).then_inc(g_srcT.sem, 1)

            def g_logit(g):
                act.wait_ge(g_g.sem, g_g.at(g))
                act.activation(lg_e[:].rearrange("p h e -> p (h e)"), X1[:, P:3 * P], ACT.Exp,
                               scale=-1.0).then_inc(g_lg.sem, 1)

            def f_take_src(i):
                act.wait_ge(g_srcT.sem, g_srcT.at(i))
                if not first(i):
                    act.wait_ge(f_y.sem, f_y.at(i, 0))
                act.activation(srcT[:], srcT_next[:], ACT.Copy).then_inc(f_srcT.sem, 1)
                act.activation(srcT_hi[:], srcT_next[:], ACT.Copy).then_inc(f_srcT.sem, 1)

            def f_take_gates(i):
                act.wait_ge(g_gate.sem, g_gate.at(i))
                if not first(i):
                    act.wait_ge(f_vg.sem, f_vg.at(i, 0))
                    act.wait_ge(f_go.sem, f_go.at(i, 0))
                act.activation(gate[:], gate_next[:], ACT.Copy).then_inc(f_gate.sem, 1)

            def f_q_out(i):
                act.wait_ge(f_q.sem, f_q.at(i))
                act.activation(qk[:, 0:H, :].rearrange("p h s -> p (h s)"), T, ACT.Copy).then_inc(f_qkev.sem, 1)

            def f_k_out(i):
                act.wait_ge(f_k.sem, f_k.at(i))
                act.activation(qk[:, H:2 * H, :].rearrange("p h s -> p (h s)"), A, ACT.Copy).then_inc(f_qkev.sem, 1)

            def f_q_copy(i):
                act.wait_ge(f_qt.sem, f_qt.at(i))
                for a in range(2):
                    act.activation(q_bd[64 * a:64 * a + 64, :, :, a, :],
                                   A[64 * a:64 * a + 64, :].rearrange("p (k b s) -> p k b s", k=HP, b=2),
                                   ACT.Copy).then_inc(f_qb.sem, 1)

            def f_k_copy(i):
                act.wait_ge(f_kt.sem, f_kt.at(i))
                act.activation(kT[:].rearrange("p k s -> p (k s)"), T, ACT.Copy).then_inc(f_kb.sem, 1)

            def f_exps(i):
                act.wait_ge(f_sub.sem, f_sub.at(i))
                act.activation(p_f[:], p_f[:], ACT.Exp, scale=float(HD) ** -0.5).then_inc(f_e.sem, 1)

            def f_att_copy(i):
                act.wait_ge(f_pt.sem, f_pt.at(i))
                on_diagonal(T, att, f_att)

            def f_gt_copy(i):
                act.wait_ge(f_gt.sem, f_gt.at(i))
                act.activation(goT_all[:, :, bass.ds(i * P, P)],
                               X1.bitcast(BF16)[:, 2 * P:(QUADS + 2) * P].rearrange("p (q t) -> p q t", q=QUADS),
                               ACT.Copy).then_inc(f_got.sem, 1)

            def d_ot_copy(i):
                act.wait_ge(f_ot.sem, f_ot.at(i))
                act.activation(oT_all[:, :, bass.ds(i * P, P)], T.rearrange("p (h t) -> p h t", h=HP),
                               ACT.Copy).then_inc(f_otev.sem, 1)

            def round_wo(k):
                act.wait_ge(ld_wo[k // 2].sem, 64)
                act.activation(wo_hi[:, 2 * k:2 * k + 2, :], big_w[:, 2 * k:2 * k + 2, :], ACT.Copy).then_inc(
                    wo_rounded.sem, 1)

            def tile(i, d, g, x):
                if not first(i):
                    f_take_src(i)
                    f_take_gates(i)
                    f_q_out(i)
                    f_k_out(i)
                if x is not None:
                    x_norm(x)
                if g is not None:
                    g_src(g)
                    g_logit(g)
                f_gt_copy(i)
                if d is not None:
                    d_ot_copy(d)
                f_q_copy(i)
                if x is not None:
                    x_exp(x)
                f_k_copy(i)
                if x is not None:
                    x_att_copy(x)
                f_exps(i)
                if isinstance(i, int) and i == TILES - 1:
                    round_wo(0)
                    round_wo(1)
                f_att_copy(i)
                if x is not None:
                    x_ot_copy(x)

            act.wait_ge(set_pool.sem, 1)
            act.activation(warm_up[:], powers[:, 0:1], ACT.Exp)
            act.wait_ge(loads["vec"].sem, 16 * VEC_LOADS)

            def round_wv(lo, hi):
                for k in range(lo, hi):
                    act.wait_ge(ld_wv[k // 2].sem, 64)
                    act.activation(wv_hi[:, 2 * k:2 * k + 2, :], wv_raw[:, 2 * k:2 * k + 2, :],
                                   ACT.Copy).then_inc(wv_rounded.sem, 1)

            x_norm(0)
            x_norm(1)
            x_exp(0)
            x_att_copy(0)
            round_wv(0, 2)
            x_exp(1)
            round_wv(2, 5)
            x_ot_copy(0)
            x_att_copy(1)
            act.wait_ge(set_t.sem, 1)
            act.activation(wsel_sb[:], T[:, 0:2 * P], ACT.Copy).then_inc(ready_w.sem, 1)
            round_wv(5, 6)
            g_src(0)
            f_take_src(0)
            g_logit(0)
            round_wv(6, 8)
            f_q_out(0)
            f_k_out(0)
            x_ot_copy(1)
            f_take_gates(0)
            tile(0, None, 1, 2)
            with act.Fori(1, TILES - 2) as i:
                tile(i, i - 1, i + 1, i + 2)
            tile(TILES - 2, TILES - 3, TILES - 1, None)
            tile(TILES - 1, TILES - 2, None, None)
            round_wo(2)
            round_wo(3)

            def experts(hf, beside):
                for s in range(STEPS):
                    act.wait_ge(p_gm.sem, p_gm.at(hf, s + 1))
                    if s >= 4:
                        act.wait_ge(p_fin.sem, p_fin.at(hf, s - 3))
                    act.activation(g_hi[:, s % 4, :], g_ring[s % 4], ACT.Copy).then_inc(p_hi.sem, 1)
                    beside(s)

            def tail_take(n):
                act.wait_ge(p_fin.sem, p_fin.at(n // 2))
                act.activation(r1T[:, columns(n)], acc[n // 2][:, columns(n)], ACT.Copy).then_inc(t_acc.of(n), 1)

            def tail_gain(n):
                act.wait_ge(*t_zt.at(n))
                act.activation(y1T[:, columns(n)], tail_banks(n)[0], ACT.Identity, bias=COL["ln1_b"],
                               scale=COL["ln1_g"]).then_inc(t_y1.of(n), 1)

            def tail_relu(n, k):
                act.wait_ge(*t_h.at(n, k + 1))
                act.activation(hT[:, k, columns(n)], tail_banks(n)[1][k % 2], ACT.Relu,
                               bias=b1_sb[:, k:k + 1]).then_inc(t_relu.of(n), 1)

            def tail(n, k):
                if k == 0:
                    tail_gain(n)
                else:
                    tail_relu(n, k - 1)

            def first_half(s):
                if s == 11:
                    d_ot_copy(TILES - 1)
                if s in (8, 16, 21, 28):
                    round_wo(4 + (8, 16, 21, 28).index(s))

            experts(0, first_half)
            act.wait_ge(loads["ff"].sem, 16 * FF_LOADS)
            tail_take(0)
            tail_take(1)
            experts(1, lambda s: early_tails(s, (13, 16, 17, 18, 19), tail))
            tail_take(2)
            tail_take(3)
            late_tails(5, tail)

        @block.vector
        def _(dve):
            def x_stats(lo, hi):
                for j in range(lo, hi):
                    dve.bn_stats(x_bn[:, 0, j, :], x_all[:, j, :]).then_inc(xs_bn.sem, 1)
                    dve.bn_stats(x_bn[:, 1, j, :], c_all[:, j, :]).then_inc(xs_bn.sem, 1)
                dve.wait_ge(xs_bn.sem, 2 * hi)
                for j in range(lo, hi):
                    for k in range(2):
                        dve.bn_aggr(x_mv[:, k, j, :], x_bn[:, k, j, :]).then_inc(xs_mv.sem, 1)

            def x_center(j):
                r = at_room(j)
                dve.tensor_scalar(r.hat[:, 0, :], x_all[:, j, :], x_mv[:, 0, j, 0:1], x_r[:, 0, bass.ds(j, 1)],
                                  ALU.subtract, ALU.mult).then_inc(xs_hat.sem, 1)
                dve.tensor_scalar(r.hat[:, 1, :], c_all[:, j, :], x_mv[:, 1, j, 0:1], x_r[:, 1, bass.ds(j, 1)],
                                  ALU.subtract, ALU.mult).then_inc(xs_hat.sem, 1)

            def x_bias(j):
                if not first(j):
                    dve.wait_ge(fs_src.sem, fs_src.at(j, 0))
                dve.tensor_tensor(x2_s[:], x_all[:, j, :], rows[:, 0, :], ALU.add).then_inc(xs_b.sem, 1)

            def x_blocks(j):
                r = at_room(j)
                dve.wait_ge(xs_proj.sem, xs_proj.at(j))
                q = r.X0[:, 2 * P:3 * P].rearrange("p (b o s) -> p b o s", b=2, o=1)
                dve.tensor_tensor(r.qd[:].rearrange("p b a h s -> p b (a h) s"), q.broadcast_to([P, 2, 4, SEQ]),
                                  head_block.rearrange("p (o h q) -> p o h q", o=1, q=1).broadcast_to([P, 2, 4, SEQ]),
                                  ALU.mult).then_inc(xs_qk.sem, 1)
                dve.tensor_tensor(r.kT[:], r.X0[:, 3 * P:4 * P], keep_k[:, j, :], ALU.mult).then_inc(xs_qk.sem, 1)
                dve.tensor_scalar(r.v[:, :, 0:XD], r.X0[:, 0:P].rearrange("p (h d) -> p h d", d=XD), 1.0, None,
                                  ALU.mult).then_inc(xs_qk.sem, 1)

            def x_soft(j):
                r = at_room(j)
                dve.wait_ge(xs_s.sem, xs_s.at(j))
                s = r.X.rearrange("p (h s) -> p h s", h=XH)
                dve.tensor_reduce(r.mx[:], s, AX_X, ALU.max).then_inc(xs_mx.sem, 1)
                dve.wait_ge(xs_mx.sem, xs_mx.at(j))
                dve.tensor_tensor(r.p[:], s, r.mx[:].unsqueeze(2).broadcast_to([P, XH, SEQ]),
                                  ALU.subtract).then_inc(xs_sub.sem, 1)

            def x_divide(j):
                r = at_room(j)
                dve.wait_ge(xs_pv.sem, xs_pv.at(j))
                o = r.X0[:, 0:XH * (XD + 1)].rearrange("p (h d) -> p h d", h=XH)
                dve.reciprocal(r.rc[:], o[:, :, XD]).then_inc(xs_rc.sem, 1)
                dve.wait_ge(xs_rc.sem, xs_rc.at(j))
                dve.tensor_tensor(r.o[:], o[:, :, 0:XD], r.rc[:].unsqueeze(2).broadcast_to([P, XH, XD]),
                                  ALU.mult).then_inc(xs_o.sem, 1)

            def x_end(j):
                r = at_room(j)
                dve.wait_ge(xs_b.sem, xs_b.at(j))
                dve.wait_ge(xs_pj.sem, xs_pj.at(j))
                dve.tensor_tensor(x2_s[:], r.X1[:, P:2 * P], x2_s[:], ALU.add).then_inc(xs_x2.sem, 1)
                dve.wait_ge(xs_x2.sem, xs_x2.at(j))
                dve.bn_stats(f_bn[:], x2_s[:]).then_inc(fs_bn.sem, 1)
                dve.wait_ge(fs_bn.sem, fs_bn.at(j))
                dve.tensor_scalar(x2_all[:, j, :], x2_s[:], 1.0, None, ALU.mult)
                dve.bn_aggr(f_mv[:], f_bn[:]).then_inc(fs_mv.sem, 1)

            def x_src(j):
                dve.wait_ge(fs_r.sem, fs_r.at(j))
                if not (isinstance(j, int) and j == 0):
                    dve.wait_ge(g_tp.sem, g_tp.at(j, 0))
                dve.tensor_scalar(src_s[:], x2_s[:], f_mv[:, 0:1], f_ve[:, 1:2],
                                  ALU.subtract, ALU.mult).then_inc(fs_src.sem, 1)
                dve.tensor_scalar(src_all[:, j, :], x2_s[:], f_mv[:, 0:1], f_ve[:, 1:2],
                                  ALU.subtract, ALU.mult).then_inc(fs_src.sem, 1)

            def f_low_part(i):
                dve.wait_ge(f_srcT.sem, f_srcT.at(i))
                dve.tensor_tensor(srcT_lo[:], srcT_next[:], srcT_hi[:].bitcast(F32),
                                  ALU.subtract).then_inc(f_low.sem, 1)

            def wide(t):
                return t.unsqueeze(2).broadcast_to([P, 2 * H, E])

            def g_top2(g, start, end):
                rank = rank_t.unsqueeze(1).broadcast_to([P, 2 * H, E])

                def at(step):
                    turn = start <= step < end
                    if turn and step >= 3:
                        dve.wait_ge(g_top.sem, g_top.at(g, step - 2))
                    return turn

                if at(0):
                    dve.wait_ge(g_lg.sem, g_lg.at(g))
                    dve.tensor_scalar(lg_e[:], lg_e[:], 1.0, None, ALU.add).then_inc(g_sig.sem, 1)
                if at(1):
                    dve.wait_ge(g_sig.sem, g_sig.at(g, 1))
                    dve.reciprocal(sg[:], lg_e[:]).then_inc(g_sig.sem, 1)
                if at(2):
                    dve.wait_ge(g_sig.sem, g_sig.at(g))
                    dve.tensor_reduce(top[:, 0, :], sg[:], AX_X, ALU.max).then_inc(g_top.sem, 1)
                for k, values, one_hot in ((0, sg, oh1), (1, l2, oh2)):
                    if at(6 * k + 3):
                        dve.tensor_tensor(eq[:], values[:], wide(top[:, k, :]), ALU.is_equal).then_inc(g_top.sem, 1)
                    if at(6 * k + 4):
                        dve.tensor_tensor(eq[:], eq[:], rank, ALU.mult).then_inc(g_top.sem, 1)
                    if at(6 * k + 5):
                        dve.tensor_reduce(kk[:], eq[:], AX_X, ALU.max).then_inc(g_top.sem, 1)
                    if at(6 * k + 6):
                        dve.tensor_tensor(one_hot[:], eq[:], wide(kk[:]), ALU.is_equal).then_inc(g_top.sem, 1)
                    if k == 0 and at(7):
                        dve.scalar_tensor_tensor(out=l2[:], in0=oh1[:], scalar=-BIG, in1=sg[:], op0=ALU.mult,
                                                 op1=ALU.add).then_inc(g_top.sem, 1)
                    if k == 0 and at(8):
                        dve.tensor_reduce(top[:, 1, :], l2[:], AX_X, ALU.max).then_inc(g_top.sem, 1)

            def f_rope(i, half):
                part = qk[:, H * half:H * half + H, 0:NROT]
                dve.wait_ge(f_qkev.sem, f_qkev.at(i, half + 1))
                for dst, table in ((rot_c, cos_t), (rot_s, sin_t)):
                    dve.tensor_tensor(dst[:, H * half:H * half + H, :], part,
                                      table.unsqueeze(1).broadcast_to([P, H, NROT]), ALU.mult).then_inc(f_rot.sem, 1)

            def f_split(i):
                go = gate[:, 1].rearrange("p (q h) e -> p q h e", q=QUADS)
                r = go_r[:].rearrange("p (q h) e -> p q h e", q=QUADS)
                part = [go3[:, :, :, s, :] for s in range(3)]
                dve.wait_ge(f_gate.sem, f_gate.at(i))
                dve.tensor_copy(part[0], go).then_inc(f_go.sem, 1)
                dve.wait_ge(f_go.sem, f_go.at(i, 1))
                dve.tensor_tensor(r, go, part[0], ALU.subtract).then_inc(f_go.sem, 1)
                dve.wait_ge(f_go.sem, f_go.at(i, 2))
                dve.tensor_copy(part[1], r).then_inc(f_go.sem, 1)
                dve.wait_ge(f_go.sem, f_go.at(i, 3))
                dve.tensor_tensor(part[2], r, part[1], ALU.subtract).then_inc(f_go.sem, 1)

            def f_gate_value(i, h):
                if h == 0:
                    dve.wait_ge(f_gate.sem, f_gate.at(i))
                dve.wait_ge(f_y.sem, f_y.at(i, h + 1))
                if h % 2 == 0 and (h >= 4 or not first(i)):
                    dve.wait_ge(f_es.sem, f_es.at(i, 3 * (h // 2 - 1)))
                dve.tensor_tensor(gy[:, h % 4], Y[h % 2].rearrange("p (e n) -> p e n", e=E),
                                  gate[:, 0, h, :].unsqueeze(2).broadcast_to([P, E, HD]),
                                  ALU.mult).then_inc(f_vg.sem, 1)

            def f_soft(i):
                dve.wait_ge(f_s.sem, f_s.at(i))
                s = A.rearrange("p (h s) -> p h s", h=H)
                dve.tensor_reduce(f_mx[:], s, AX_X, ALU.max).then_inc(f_m.sem, 1)
                dve.wait_ge(f_m.sem, f_m.at(i))
                dve.tensor_tensor(p_f[:], s, f_mx[:].unsqueeze(2).broadcast_to([P, H, SEQ]),
                                  ALU.subtract).then_inc(f_sub.sem, 1)

            def d_divide(i):
                dve.wait_ge(f_pv.sem, f_pv.at(i))
                wide_o = ps[:, 2:4, 0:7 * (HD + 1)].rearrange("p a (h d) -> p a h d", h=7)
                last_o = ps[:, 4, 0:2 * (HD + 1)].rearrange("p (h d) -> p h d", h=2)
                dve.reciprocal(f_rc[:, 0:14].rearrange("p (a h) -> p a h", a=2),
                               wide_o[:, :, :, HD]).then_inc(f_rcs.sem, 1)
                dve.reciprocal(f_rc[:, 14:16], last_o[:, :, HD]).then_inc(f_rcs.sem, 1)
                dve.wait_ge(f_rcs.sem, f_rcs.at(i))
                dve.tensor_tensor(o_sb[:, 0:14, :].rearrange("p (a h) d -> p a h d", a=2), wide_o[:, :, :, 0:HD],
                                  f_rc[:, 0:14].rearrange("p (a h q) -> p a h q", a=2, q=1).broadcast_to([P, 2, 7, HD]),
                                  ALU.mult).then_inc(f_on.sem, 1)
                dve.tensor_tensor(o_sb[:, 14:16, :], last_o[:, :, 0:HD],
                                  f_rc[:, 14:16].unsqueeze(2).broadcast_to([P, 2, HD]), ALU.mult).then_inc(f_on.sem, 1)

            def tile(i, d, g, x):
                if not first(i):
                    f_low_part(i)
                if g is not None and not first(i):
                    x_end(g)
                if x is not None:
                    x_center(x)
                if g is not None:
                    x_src(g)
                f_gate_value(i, 0)
                f_rope(i, 0)
                f_gate_value(i, 1)
                f_rope(i, 1)
                f_gate_value(i, 2)
                f_split(i)
                f_gate_value(i, 3)
                if d is not None:
                    d_divide(d)
                if x is not None:
                    x_blocks(x)
                f_gate_value(i, 4)
                f_gate_value(i, 5)
                if x is not None:
                    x_bias(x)
                if g is not None:
                    g_top2(g, 0, 2)
                f_gate_value(i, 6)
                f_gate_value(i, 7)
                if x is not None:
                    x_soft(x)
                f_gate_value(i, 8)
                if g is not None:
                    g_top2(g, 2, 6)
                f_gate_value(i, 9)
                if g is not None:
                    g_top2(g, 6, 8)
                f_gate_value(i, 10)
                if g is not None:
                    g_top2(g, 8, 10)
                f_gate_value(i, 11)
                f_soft(i)
                if g is not None:
                    g_top2(g, 10, 12)
                f_gate_value(i, 12)
                if g is not None:
                    g_top2(g, 12, 13)
                f_gate_value(i, 13)
                f_gate_value(i, 14)
                if x is not None:
                    x_divide(x)
                f_gate_value(i, 15)

            def wv_low(k):
                dve.wait_ge(wv_rounded.sem, k + 1)
                dve.tensor_tensor(wv_lo[:, 2 * k:2 * k + 2, :], wv_raw[:, 2 * k:2 * k + 2, :],
                                  wv_hi[:, 2 * k:2 * k + 2, :].bitcast(F32), ALU.subtract).then_inc(wv_split_dve.sem, 1)

            dve.wait_ge(loads["x"].sem, 16)
            dve.wait_ge(loads["ctx"].sem, 16)
            x_stats(0, HEAD_TILES)
            dve.wait_ge(loads["mask"].sem, 16)
            dve.tensor_scalar(keep_k[:], mask_k, 0.0, None, ALU.not_equal).then_inc(set_dve.sem, 1)
            dve.tensor_scalar(masked[:], mask_k[0:SPLITS], 0.0, None, ALU.is_equal).then_inc(set_dve.sem, 1)
            dve.wait_ge(xs_r.sem, xs_r.at(0))
            x_center(0)
            x_center(1)
            dve.wait_ge(loads["const"].sem, 32)
            dve.wait_ge(set_dve.sem, 2)
            dve.wait_ge(set_pool.sem, 1)
            x_blocks(0)
            x_blocks(1)
            x_stats(HEAD_TILES, TILES)
            dve.wait_ge(loads["vec"].sem, 16 * VEC_LOADS)
            x_bias(0)
            x_soft(0)
            x_soft(1)
            for k in range(3):
                wv_low(k)
            x_divide(0)
            x_end(0)
            x_src(0)
            x_bias(1)
            wv_low(3)
            f_low_part(0)
            g_top2(0, 0, 13)
            wv_low(7)
            x_divide(1)
            x_end(1)
            dve.wait_ge(xs_r.sem, xs_r.at(1))
            tile(0, None, 1, 2)
            with dve.Fori(1, TILES - 2) as i:
                tile(i, i - 1, i + 1, i + 2)
            tile(TILES - 2, TILES - 3, TILES - 1, None)
            tile(TILES - 1, TILES - 2, None, None)
            def wo_low(k):
                dve.wait_ge(wo_rounded.sem, k + 1)
                dve.tensor_tensor(wo_lo[:, 2 * k:2 * k + 2, :], big_w[:, 2 * k:2 * k + 2, :],
                                  wo_hi[:, 2 * k:2 * k + 2, :].bitcast(F32), ALU.subtract).then_inc(wo_split.sem, 1)

            def tail_stats(n, k, ready, bn, mv):
                dve.wait_ge(*ready.at(n))
                for t in range(QT):
                    dve.bn_stats(tail_bn[:, k, n, t, :], tail_banks(n)[0][:, P * t:P * t + P]).then_inc(bn.of(n), 1)
                dve.wait_ge(*bn.at(n))
                for t in range(QT):
                    dve.bn_aggr(tail_mv[:, k, n, t, :], tail_bn[:, k, n, t, :]).then_inc(mv.of(n), 1)

            def tail_center(n):
                dve.wait_ge(*t_mv.at(n))
                dve.wait_ge(*t_r.at(n))
                for t in range(QT):
                    dve.tensor_scalar(z_t[:, columns(n)][:, P * t:P * t + P], tail_banks(n)[0][:, P * t:P * t + P],
                                      tail_mv[:, 0, n, t, 0:1], tail_ve[:, 0, n, 1, t:t + 1],
                                      ALU.subtract, ALU.mult).then_inc(t_z.of(n), 1)

            def tail_second(n):
                dve.wait_ge(*t_o.at(n))
                dve.scalar_tensor_tensor(out=z2T[:, columns(n)], in0=tail_banks(n)[0], scalar=COL["b2"],
                                         in1=y1T[:, columns(n)], op0=ALU.add, op1=ALU.add).then_inc(t_z2.of(n), 1)

            def tail_gain(n):
                dve.wait_ge(*u_mv.at(n))
                for t in range(QT):
                    dve.scalar_tensor_tensor(out=z_t[:, columns(n)][:, P * t:P * t + P],
                                             in0=tail_banks(n)[0][:, P * t:P * t + P],
                                             scalar=tail_mv[:, 1, n, t, 0:1], in1=rows[:, 1, :], op0=ALU.subtract,
                                             op1=ALU.mult).then_inc(u_g.of(n), 1)

            def tail_end(n):
                dve.wait_ge(*u_g.at(n))
                dve.wait_ge(*u_r.at(n))
                for t in range(QT):
                    dve.scalar_tensor_tensor(out=x_all[:, n * QT + t, :], in0=z_t[:, columns(n)][:, P * t:P * t + P],
                                             scalar=tail_ve[:, 1, n, 1, t:t + 1], in1=x2_all[:, n * QT + t, :],
                                             op0=ALU.mult, op1=ALU.add).then_inc(u_out.of(n), 1)

            def tail_bias():
                dve.wait_ge(loads["ff"].sem, 16 * FF_LOADS)
                dve.tensor_tensor(x2_all[:], x2_all[:], rows[:, 2, :].unsqueeze(1).broadcast_to([P, TILES, DIM]),
                                  ALU.add).then_inc(u_x2.sem, 1)
                dve.wait_ge(u_x2.sem, 1)

            def tail(n, k):
                if k == 0:
                    tail_stats(n, 0, t_rt, t_bn, t_mv)
                elif k == 1:
                    tail_center(n)
                elif k == 2:
                    tail_second(n)
                elif k == 3:
                    tail_stats(n, 1, t_z2t, u_bn, u_mv)
                elif k == 4:
                    tail_gain(n)
                else:
                    tail_end(n)

            def first_half(s):
                if s == 6:
                    d_divide(TILES - 1)
                if s in (2, 11, 17, 22, 29, 37):
                    wo_low(2 + (2, 11, 17, 22, 29, 37).index(s))

            def low(hf, s):
                dve.wait_ge(p_hi.sem, p_hi.at(hf, s + 1))
                dve.tensor_tensor(g_lo[:, s % 4, :], g_ring[s % 4], g_hi[:, s % 4, :].bitcast(F32),
                                  ALU.subtract).then_inc(p_lo[True].sem, 1)

            def experts(hf, beside):
                for s in range(STEPS + 2):
                    if s < STEPS:
                        dve.wait_ge(p_bc.sem, p_bc.at(hf, s + 1))
                        if s >= 4:
                            wait_low(dve, hf, s - 4)
                        dve.tensor_tensor(g_ring[s % 4], BC[s % 3], oT_all[:, s // E, hf * HTOK:(hf + 1) * HTOK],
                                          ALU.mult).then_inc(p_gm.sem, 1)
                    if s >= 2 and on_dve(s - 2):
                        low(hf, s - 2)
                    beside(s)

            for k in range(2):
                wo_low(k)
            dve.tensor_copy(z2_t, src_all[:, 0:HT, :]).then_inc(p_res.sem, 1)
            dve.wait_ge(f_es.sem, f_es.at(TILES - 1))
            experts(0, first_half)
            dve.tensor_copy(z2_t, src_all[:, HT:2 * HT, :]).then_inc(p_res.sem, 1)
            tail_bias()
            experts(1, lambda s: early_tails(s, (5, 9, 25, 29, 30, 31), tail))
            late_tails(6, tail)

        @block.gpsimd
        def _(pool):
            def x_rstd(n, lo, hi):
                t = slice(lo, hi)
                var, ve, r = x_mv[:, :, t, 1], x_ve[:, :, t], x_r[:, :, t]
                width = hi - lo
                eps = eps_t[:, 0:2 * width].rearrange("p (a t) -> p a t", a=2)
                power = powers[:, 0:2 * width].rearrange("p (a t) -> p a t", a=2)
                pool.wait_ge(xs_mv.sem, 2 * hi)
                pool.tensor_tensor(ve, var, eps, ALU.add).then_inc(xs_r.sem, 1)
                for k, (dst, a, b, op) in enumerate((
                        (r, ve, power, ALU.pow), (ve[:, 0], var[:, 0], r[:, 0], ALU.mult),
                        (ve[:, 0], ve[:, 0], r[:, 0], ALU.mult), (ve[:, 0], ve[:, 0], eps[:, 0], ALU.add),
                        (ve[:, 0], ve[:, 0], power[:, 0], ALU.pow), (r[:, 0], ve[:, 0], r[:, 0], ALU.mult))):
                    pool.wait_ge(xs_r.sem, xs_r.at(n, k + 1))
                    pool.tensor_tensor(dst, a, b, op).then_inc(xs_r.sem, 1)

            def f_rstd(j):
                pool.wait_ge(fs_mv.sem, fs_mv.at(j))
                pool.tensor_tensor(f_ve[:, 0:1], f_mv[:, 1:2], eps_t[:, 0:1], ALU.add).then_inc(fs_r.sem, 1)
                pool.wait_ge(fs_r.sem, fs_r.at(j, 1))
                pool.tensor_tensor(f_ve[:, 1:2], f_ve[:, 0:1], powers[:, 0:1], ALU.pow).then_inc(fs_r.sem, 1)

            def g_gates(g):
                pool.wait_ge(g_top.sem, g_top.at(g))
                pool.tensor_tensor(oh1[:], oh1[:], oh2[:], ALU.add).then_inc(g_gate.sem, 1)
                pool.wait_ge(g_gate.sem, g_gate.at(g, 1))
                if not first(g):
                    pool.wait_ge(f_gate.sem, f_gate.at(g, 0))
                pool.tensor_tensor(gate_next[:].rearrange("p a h e -> p (a h) e"), oh1[:], sg[:],
                                   ALU.mult).then_inc(g_gate.sem, 1)

            def f_rot_add(i, half):
                h, a = HALF_ROT, slice(H * half, H * half + H)
                pool.wait_ge(f_rot.sem, f_rot.at(i, 2 * half + 2))
                pool.tensor_tensor(qk[:, a, 0:h], rot_c[:, a, 0:h], rot_s[:, a, h:2 * h], ALU.add).then_inc(f_ra.sem, 1)
                pool.tensor_tensor(qk[:, a, h:2 * h], rot_c[:, a, h:2 * h], rot_s[:, a, 0:h],
                                   ALU.add).then_inc(f_ra.sem, 1)

            def f_expert_sum(i, pair):
                g = gy[:, 2 * (pair % 2):2 * (pair % 2) + 2]
                pool.wait_ge(f_vg.sem, f_vg.at(i, 2 * pair + 2))
                pool.tensor_tensor(g[:, :, 0:4, :], g[:, :, 0:4, :], g[:, :, 4:8, :], ALU.add).then_inc(f_es.sem, 1)
                pool.wait_ge(f_es.sem, f_es.at(i, 3 * pair + 1))
                pool.tensor_tensor(g[:, :, 0:2, :], g[:, :, 0:2, :], g[:, :, 2:4, :], ALU.add).then_inc(f_es.sem, 1)
                pool.wait_ge(f_es.sem, f_es.at(i, 3 * pair + 2))
                if pair == 0 and not first(i):
                    pool.wait_ge(f_pv.sem, f_pv.at(i, 0))
                pool.tensor_tensor(v[:, 2 * pair:2 * pair + 2, 0:HD], g[:, :, 0, :], g[:, :, 1, :],
                                   ALU.add).then_inc(f_es.sem, 1)

            def tile(i, d, g, x):
                if g is not None:
                    f_rstd(g)
                f_rot_add(i, 0)
                f_rot_add(i, 1)
                for pair in range(H // 2):
                    if pair == 6 and g is not None:
                        g_gates(g)
                    f_expert_sum(i, pair)

            pool.memset(powers[:], -0.5)
            pool.memset(eps_t[:], EPS)
            pool.memset(x_v[:], 1.0)
            pool.memset(v[:], 1.0)
            pool.memset(x_att[:], 0.0)
            pool.memset(att[:], 0.0)
            pool.memset(q_bd[:], 0.0)
            pool.memset(go3[:], 0.0).then_inc(set_pool.sem, 1)
            pool.wait_ge(set_pool.sem, 1)
            x_rstd(0, 0, HEAD_TILES)
            x_rstd(1, HEAD_TILES, TILES)

            def wv_low(k):
                pool.wait_ge(wv_rounded.sem, k + 1)
                pool.tensor_tensor(wv_lo[:, 2 * k:2 * k + 2, :], wv_raw[:, 2 * k:2 * k + 2, :],
                                   wv_hi[:, 2 * k:2 * k + 2, :].bitcast(F32), ALU.subtract).then_inc(wv_split.sem, 1)

            wv_low(4)
            f_rstd(0)
            wv_low(5)
            wv_low(6)
            g_gates(0)
            tile(0, None, 1, 2)
            with pool.Fori(1, TILES - 2) as i:
                tile(i, i - 1, i + 1, i + 2)
            tile(TILES - 2, TILES - 3, TILES - 1, None)
            tile(TILES - 1, TILES - 2, None, None)

            def tail_rstd(n, k, mv, r):
                pool.wait_ge(*mv.at(n))
                pool.tensor_tensor(tail_ve[:, k, n, 0, :], tail_mv[:, k, n, :, 1], eps_t[:, 0:QT],
                                   ALU.add).then_inc(r.of(n), 1)
                pool.wait_ge(*r.at(n, 1))
                pool.tensor_tensor(tail_ve[:, k, n, 1, :], tail_ve[:, k, n, 0, :], powers[:, 0:QT],
                                   ALU.pow).then_inc(r.of(n), 1)

            def experts(hf, beside):
                for s in range(STEPS):
                    if not on_dve(s):
                        pool.wait_ge(p_hi.sem, p_hi.at(hf, s + 1))
                        pool.tensor_tensor(g_lo[:, s % 4, :], g_ring[s % 4], g_hi[:, s % 4, :].bitcast(F32),
                                           ALU.subtract).then_inc(p_lo[False].sem, 1)
                    beside(s)

            def tail(n, k):
                if k == 0:
                    tail_rstd(n, 0, t_mv, t_r)
                else:
                    tail_rstd(n, 1, u_mv, u_r)

            experts(0, lambda s: None)
            experts(1, lambda s: early_tails(s, (4, 27), tail))
            late_tails(2, tail)


_INS = ["x", "ctx_1024", "mask_BxS2_ik0", "L0_xattn_w_q", "L0_xattn_w_kv", "L0_xattn_w_proj", "L0_xattn_b_proj",
        "L0_xattn_g_x", "L0_xattn_b_x", "L0_xattn_g_kv", "L0_xattn_b_kv", "L0_ffn_Wq", "L0_ffn_Wk", "L0_ffn_Wv",
        "L0_ffn_Wo", "L0_ffn_Wsel_v", "L0_ffn_Wsel_o", "L0_ffn_ln1_g", "L0_ffn_ln1_b", "L0_ffn_ln2_g",
        "L0_ffn_ln2_b", "L0_ffn_W1", "L0_ffn_b1", "L0_ffn_W2", "L0_ffn_b2"]


def kernel(**inputs):
    import concourse.bacc as bacc
    import ml_dtypes
    from concourse.bass_utils import run_bass_kernel_spmd

    nc = bacc.Bacc("TRN2", target_bir_lowering=False, num_devices=1)
    const, const_sel, const_fill = constants()
    data = {name: np.ascontiguousarray(inputs[name]) for name in _INS}
    data["const"] = const
    data["const_sel"] = const_sel.astype(ml_dtypes.bfloat16)
    data["const_fill"] = const_fill.astype(ml_dtypes.bfloat16)
    data["const_idb"] = np.eye(P).astype(ml_dtypes.bfloat16)
    arrays, args = {}, []
    for name, a in data.items():
        arrays[f"in_{name}"] = a
        args.append(nc.dram_tensor(f"in_{name}", a.shape, mybir.dt.from_np(a.dtype), kind="ExternalInput").ap())
    args.append(nc.dram_tensor("out_0", (BATCH, SEQ, DIM), F32, kind="ExternalOutput").ap())
    build(nc, *args)
    r = run_bass_kernel_spmd(nc, [arrays], core_ids=[0])
    return r.results[0]["out_0"]
```
